# Optimizing a Trainium2 kernel written in Bass

```python
import numpy as np
import jax
import jax.numpy as jnp

def _softmax(x, axis=-1):
    return jax.nn.softmax(x, axis=axis)

def _gelu(x):
    return jax.nn.gelu(x, approximate=True)

def _silu(x):
    return jax.nn.silu(x)

def _sigmoid(x):
    return jax.nn.sigmoid(x)

def _layernorm(x, axis=-1, eps=1e-05):
    m = jnp.mean(x, axis=axis, keepdims=True)
    v = jnp.var(x, axis=axis, keepdims=True)
    return (x - m) / jnp.sqrt(v + eps)

def _scatter_add(tgt, idx, src, axis=0):
    return tgt.at[idx].add(src)

def _segment_sum(src, seg, n):
    return jax.ops.segment_sum(src, seg, n)
kernel_name = 'mk_vit_tower_d1_tok_img2048_r4_6f97e8'

def setup_inputs(seed: int=0):
    np.random.seed(seed)
    _w = jnp.asarray

    def _rec_inputs():
        import jax
        import jax.numpy as jnp
        _rk = jax.random.key(seed)
        x = -0.00340659 + 1.00146 * jax.random.normal(jax.random.fold_in(_rk, 1), (16, 256, 64, 2), jnp.float32)
        return x
    x = _rec_inputs()

    def _L0_tok_setup():
        import jax, jax.numpy as jnp
        import numpy as np
        CH, H, N, N_SSM, SEQ_L = (1, 256, 64, 256, 512)

        def _kernel(C_ri, log_dt, B_ri, inv_A_real, A_imag, L):
            C = C_ri[..., 0] + 1j * C_ri[..., 1]
            B = B_ri[..., 0] + 1j * B_ri[..., 1]
            A = -jnp.exp(inv_A_real) + 1j * A_imag
            rep = log_dt.shape[0] // inv_A_real.shape[0]
            B = jnp.tile(B, (rep, 1))
            A = jnp.tile(A, (rep, 1))
            dt = jnp.exp(log_dt)
            dtA = A * dt[:, None]
            Ct = B[None] * C / (1.0 - dtA / 2) * dt[:, None]
            dA = (1.0 + dtA / 2) / (1.0 - dtA / 2)
            dA_log = jnp.log(dA)
            l = jnp.arange(L, dtype=jnp.float32)
            V = jnp.exp(dA_log[:, :, None] * l)
            K = 2.0 * jnp.einsum('chn,hnl->chl', Ct, V).real
            return K
        key = jax.random.key(seed)
        ks = jax.random.split(key, 5)
        return {'C_ri': jax.random.normal(ks[0], (CH, H, N, 2), dtype=jnp.float32), 'log_dt': jax.random.normal(ks[1], (H,), dtype=jnp.float32), 'B_ri': jax.random.normal(ks[2], (N_SSM, N, 2), dtype=jnp.float32), 'inv_A_real': jax.random.normal(ks[3], (N_SSM, N), dtype=jnp.float32), 'A_imag': jax.random.normal(ks[4], (N_SSM, N), dtype=jnp.float32), 'L': SEQ_L}
    _L0_tok_all = _L0_tok_setup()
    _L0_tok_in = {k: v for k, v in _L0_tok_all.items() if k in ('log_dt', 'B_ri', 'inv_A_real', 'A_imag')}
    del _L0_tok_all

    def _L0_attn_setup():
        import jax, jax.numpy as jnp
        import numpy as np
        THETA = 10000.0

        def _rope_tables(seq_len, d_head):
            inv = 1.0 / THETA ** (jnp.arange(0, d_head, 2, dtype=jnp.float32) / d_head)
            t = jnp.arange(seq_len, dtype=jnp.float32)
            ang = jnp.outer(t, inv)
            return (jnp.cos(ang), jnp.sin(ang))

        def _apply_rope(x, cos, sin):
            xr = x[..., 0::2]
            xi = x[..., 1::2]
            c = cos[None, :, None, :]
            s = sin[None, :, None, :]
            out_r = xr * c - xi * s
            out_i = xr * s + xi * c
            return jnp.stack([out_r, out_i], axis=-1).reshape(x.shape)
        key = jax.random.key(seed)
        ks = jax.random.split(key, 5)
        B, S, D = (2, 512, 512)
        sc = 0.02
        return {'x': jax.random.normal(ks[0], (B, S, D), dtype=jnp.float32), 'wq': jax.random.normal(ks[1], (D, D), dtype=jnp.float32) * sc, 'wk': jax.random.normal(ks[2], (D, D), dtype=jnp.float32) * sc, 'wv': jax.random.normal(ks[3], (D, D), dtype=jnp.float32) * sc, 'wo': jax.random.normal(ks[4], (D, D), dtype=jnp.float32) * sc}
    _L0_attn_all = _L0_attn_setup()
    _L0_attn_in = {k: v for k, v in _L0_attn_all.items() if k in ('wq', 'wk', 'wv', 'wo')}
    del _L0_attn_all

    def _L0_ffn_setup():
        import math
        import jax, jax.numpy as jnp
        import numpy as np
        from jax import lax
        D = 512
        I = 256
        E = 32
        K = 4
        NG = 8
        TKG = 3
        NSH = 2
        SCALE = 2.5
        CF = 1.25
        B, S = (2, 512)

        def _router(x, router_w, e_bias):
            scores = jax.nn.sigmoid(x @ router_w.T)
            sc = scores + e_bias[None, :]
            T = x.shape[0]
            gs = sc.reshape(T, NG, E // NG)
            group_scores = lax.top_k(gs, 2)[0].sum(-1)
            _, gidx = lax.top_k(group_scores, TKG)
            gmask = jnp.zeros((T, NG), sc.dtype).at[jnp.arange(T)[:, None], gidx].set(1.0)
            smask = jnp.repeat(gmask, E // NG, axis=1)
            masked = jnp.where(smask > 0, sc, 0.0)
            _, topk_idx = lax.top_k(masked, K)
            topk_w = jnp.take_along_axis(scores, topk_idx, axis=1)
            topk_w = topk_w / (topk_w.sum(-1, keepdims=True) + 1e-20)
            topk_w = topk_w * SCALE
            return (topk_idx.astype(jnp.int32), topk_w)

        def _moe_forward(hidden_states, router_w, e_bias, W_gate, W_up, W_down, shared_gate, shared_up, shared_down):
            b, s, d = hidden_states.shape
            T = b * s
            C = int(math.ceil(CF * T / E))
            EC = E * C
            x = hidden_states.reshape(T, d)
            topk_idx, topk_w = _router(x, router_w, e_bias)
            expert_flat = topk_idx.reshape(-1)
            w_flat = topk_w.reshape(-1)
            tok_flat = jnp.repeat(jnp.arange(T, dtype=jnp.int32), K)
            sort_ix = jnp.argsort(expert_flat)
            e_sorted = expert_flat[sort_ix]
            tok_s = tok_flat[sort_ix]
            w_s = w_flat[sort_ix]
            counts = jnp.zeros(E, jnp.int32).at[e_sorted].add(1)
            group_start = jnp.concatenate([jnp.zeros(1, jnp.int32), jnp.cumsum(counts)[:-1].astype(jnp.int32)])
            pos = jnp.arange(T * K, dtype=jnp.int32) - group_start[e_sorted]
            valid = pos < C
            dest = e_sorted * C + jnp.where(valid, pos, 0)
            slots_token = jnp.zeros(EC, jnp.int32).at[dest].add(jnp.where(valid, tok_s, 0))
            slots_w = jnp.zeros(EC, w_s.dtype).at[dest].add(jnp.where(valid, w_s, 0.0))
            Xp = x[slots_token].reshape(E, C, d)
            G = jnp.einsum('ecd,edi->eci', Xp, W_gate)
            U = jnp.einsum('ecd,edi->eci', Xp, W_up)
            Y = jnp.einsum('eci,eid->ecd', jax.nn.silu(G) * U, W_down)
            Yf = Y.reshape(EC, d) * slots_w[:, None]
            out = jnp.zeros((T, d), x.dtype).at[slots_token].add(Yf)
            shared = jax.nn.silu(x @ shared_gate.T) * (x @ shared_up.T) @ shared_down.T
            return (out + shared).reshape(b, s, d)
        key = jax.random.key(seed)
        ks = jax.random.split(key, 8)

        def rn(k, shape, scale=0.02):
            return jax.random.normal(k, shape, jnp.float32) * scale
        return {'hidden_states': jax.random.normal(ks[0], (B, S, D), jnp.float32), 'router_w': rn(ks[1], (E, D)), 'e_bias': jnp.zeros((E,), jnp.float32), 'W_gate': rn(ks[2], (E, D, I)), 'W_up': rn(ks[3], (E, D, I)), 'W_down': rn(ks[4], (E, I, D)), 'shared_gate': rn(ks[5], (I * NSH, D)), 'shared_up': rn(ks[6], (I * NSH, D)), 'shared_down': rn(ks[7], (D, I * NSH))}
    _L0_ffn_all = _L0_ffn_setup()
    _L0_ffn_in = {k: v for k, v in _L0_ffn_all.items() if k in ('router_w', 'e_bias', 'W_gate', 'W_up', 'W_down', 'shared_gate', 'shared_up', 'shared_down')}
    del _L0_ffn_all
    return {'x': x, 'L0_tok_log_dt': _L0_tok_in['log_dt'], 'L0_tok_B_ri': _L0_tok_in['B_ri'], 'L0_tok_inv_A_real': _L0_tok_in['inv_A_real'], 'L0_tok_A_imag': _L0_tok_in['A_imag'], 'L0_attn_wq': _L0_attn_in['wq'], 'L0_attn_wk': _L0_attn_in['wk'], 'L0_attn_wv': _L0_attn_in['wv'], 'L0_attn_wo': _L0_attn_in['wo'], 'L0_ffn_router_w': _L0_ffn_in['router_w'], 'L0_ffn_e_bias': _L0_ffn_in['e_bias'], 'L0_ffn_W_gate': _L0_ffn_in['W_gate'], 'L0_ffn_W_up': _L0_ffn_in['W_up'], 'L0_ffn_W_down': _L0_ffn_in['W_down'], 'L0_ffn_shared_gate': _L0_ffn_in['shared_gate'], 'L0_ffn_shared_up': _L0_ffn_in['shared_up'], 'L0_ffn_shared_down': _L0_ffn_in['shared_down']}

def reference(x, L0_tok_log_dt, L0_tok_B_ri, L0_tok_inv_A_real, L0_tok_A_imag, L0_attn_wq, L0_attn_wk, L0_attn_wv, L0_attn_wo, L0_ffn_router_w, L0_ffn_e_bias, L0_ffn_W_gate, L0_ffn_W_up, L0_ffn_W_down, L0_ffn_shared_gate, L0_ffn_shared_up, L0_ffn_shared_down):
    import jax
    import jax.numpy as jnp

    def _L0_tok_ref(C_ri, log_dt, B_ri, inv_A_real, A_imag, L):
        import jax, jax.numpy as jnp
        import numpy as np
        CH, H, N, N_SSM, SEQ_L = (1, 256, 64, 256, 512)

        def _kernel(C_ri, log_dt, B_ri, inv_A_real, A_imag, L):
            C = C_ri[..., 0] + 1j * C_ri[..., 1]
            B = B_ri[..., 0] + 1j * B_ri[..., 1]
            A = -jnp.exp(inv_A_real) + 1j * A_imag
            rep = log_dt.shape[0] // inv_A_real.shape[0]
            B = jnp.tile(B, (rep, 1))
            A = jnp.tile(A, (rep, 1))
            dt = jnp.exp(log_dt)
            dtA = A * dt[:, None]
            Ct = B[None] * C / (1.0 - dtA / 2) * dt[:, None]
            dA = (1.0 + dtA / 2) / (1.0 - dtA / 2)
            dA_log = jnp.log(dA)
            l = jnp.arange(L, dtype=jnp.float32)
            V = jnp.exp(dA_log[:, :, None] * l)
            K = 2.0 * jnp.einsum('chn,hnl->chl', Ct, V).real
            return K
        return _kernel(C_ri, log_dt, B_ri, inv_A_real, A_imag, L)

    def _L0_attn_ref(x, wq, wk, wv, wo):
        import jax, jax.numpy as jnp
        import numpy as np
        THETA = 10000.0

        def _rope_tables(seq_len, d_head):
            inv = 1.0 / THETA ** (jnp.arange(0, d_head, 2, dtype=jnp.float32) / d_head)
            t = jnp.arange(seq_len, dtype=jnp.float32)
            ang = jnp.outer(t, inv)
            return (jnp.cos(ang), jnp.sin(ang))

        def _apply_rope(x, cos, sin):
            xr = x[..., 0::2]
            xi = x[..., 1::2]
            c = cos[None, :, None, :]
            s = sin[None, :, None, :]
            out_r = xr * c - xi * s
            out_i = xr * s + xi * c
            return jnp.stack([out_r, out_i], axis=-1).reshape(x.shape)
        B, S, D = x.shape
        H = 16
        Dh = D // H
        scale = 1.0 / jnp.sqrt(jnp.float32(Dh))
        cos, sin = _rope_tables(S, Dh)
        q = (x @ wq.T).reshape(B, S, H, Dh)
        k = (x @ wk.T).reshape(B, S, H, Dh)
        v = (x @ wv.T).reshape(B, S, H, Dh)
        q = _apply_rope(q, cos, sin)
        k = _apply_rope(k, cos, sin)
        attn = jnp.einsum('bqhd,bkhd->bhqk', q, k) * scale
        causal = jnp.tril(jnp.ones((S, S), dtype=bool))
        attn = jnp.where(causal[None, None], attn, -jnp.inf)
        probs = jax.nn.softmax(attn, axis=-1)
        head_out = jnp.einsum('bhqk,bkhd->bqhd', probs, v).reshape(B, S, D)
        return head_out @ wo.T

    def _L0_ffn_ref(hidden_states, router_w, e_bias, W_gate, W_up, W_down, shared_gate, shared_up, shared_down):
        import math
        import jax, jax.numpy as jnp
        import numpy as np
        from jax import lax
        D = 512
        I = 256
        E = 32
        K = 4
        NG = 8
        TKG = 3
        NSH = 2
        SCALE = 2.5
        CF = 1.25
        B, S = (2, 512)

        def _router(x, router_w, e_bias):
            scores = jax.nn.sigmoid(x @ router_w.T)
            sc = scores + e_bias[None, :]
            T = x.shape[0]
            gs = sc.reshape(T, NG, E // NG)
            group_scores = lax.top_k(gs, 2)[0].sum(-1)
            _, gidx = lax.top_k(group_scores, TKG)
            gmask = jnp.zeros((T, NG), sc.dtype).at[jnp.arange(T)[:, None], gidx].set(1.0)
            smask = jnp.repeat(gmask, E // NG, axis=1)
            masked = jnp.where(smask > 0, sc, 0.0)
            _, topk_idx = lax.top_k(masked, K)
            topk_w = jnp.take_along_axis(scores, topk_idx, axis=1)
            topk_w = topk_w / (topk_w.sum(-1, keepdims=True) + 1e-20)
            topk_w = topk_w * SCALE
            return (topk_idx.astype(jnp.int32), topk_w)

        def _moe_forward(hidden_states, router_w, e_bias, W_gate, W_up, W_down, shared_gate, shared_up, shared_down):
            b, s, d = hidden_states.shape
            T = b * s
            C = int(math.ceil(CF * T / E))
            EC = E * C
            x = hidden_states.reshape(T, d)
            topk_idx, topk_w = _router(x, router_w, e_bias)
            expert_flat = topk_idx.reshape(-1)
            w_flat = topk_w.reshape(-1)
            tok_flat = jnp.repeat(jnp.arange(T, dtype=jnp.int32), K)
            sort_ix = jnp.argsort(expert_flat)
            e_sorted = expert_flat[sort_ix]
            tok_s = tok_flat[sort_ix]
            w_s = w_flat[sort_ix]
            counts = jnp.zeros(E, jnp.int32).at[e_sorted].add(1)
            group_start = jnp.concatenate([jnp.zeros(1, jnp.int32), jnp.cumsum(counts)[:-1].astype(jnp.int32)])
            pos = jnp.arange(T * K, dtype=jnp.int32) - group_start[e_sorted]
            valid = pos < C
            dest = e_sorted * C + jnp.where(valid, pos, 0)
            slots_token = jnp.zeros(EC, jnp.int32).at[dest].add(jnp.where(valid, tok_s, 0))
            slots_w = jnp.zeros(EC, w_s.dtype).at[dest].add(jnp.where(valid, w_s, 0.0))
            Xp = x[slots_token].reshape(E, C, d)
            G = jnp.einsum('ecd,edi->eci', Xp, W_gate)
            U = jnp.einsum('ecd,edi->eci', Xp, W_up)
            Y = jnp.einsum('eci,eid->ecd', jax.nn.silu(G) * U, W_down)
            Yf = Y.reshape(EC, d) * slots_w[:, None]
            out = jnp.zeros((T, d), x.dtype).at[slots_token].add(Yf)
            shared = jax.nn.silu(x @ shared_gate.T) * (x @ shared_up.T) @ shared_down.T
            return (out + shared).reshape(b, s, d)
        return _moe_forward(hidden_states, router_w, e_bias, W_gate, W_up, W_down, shared_gate, shared_up, shared_down)
    h = _L0_tok_ref(x, L0_tok_log_dt, L0_tok_B_ri, L0_tok_inv_A_real, L0_tok_A_imag, 512)
    h = h + _L0_attn_ref(_layernorm(h, axis=-1), L0_attn_wq, L0_attn_wk, L0_attn_wv, L0_attn_wo)
    h = h + _L0_ffn_ref(_layernorm(h, axis=-1), L0_ffn_router_w, L0_ffn_e_bias, L0_ffn_W_gate, L0_ffn_W_up, L0_ffn_W_down, L0_ffn_shared_gate, L0_ffn_shared_up, L0_ffn_shared_down)
    return h

_drawn_inputs = setup_inputs


def setup_inputs(seed=0):
    import zlib

    import numpy as np

    out = dict(_drawn_inputs(seed))
    spreads = {'L0_ffn_e_bias': (0.0, 0.39)}
    factors = {'L0_attn_wq': 4.798,
     'L0_attn_wk': 4.678,
     'L0_ffn_router_w': 3.626,
     'L0_ffn_W_gate': 3.447,
     'L0_ffn_W_up': 3.383,
     'L0_ffn_W_down': 3.397}
    for name, (base, spread) in spreads.items():
        noise = np.random.default_rng([zlib.crc32(name.encode()), seed]).standard_normal(out[name].shape)
        drawn = base * np.exp(spread * noise) if base else spread * noise
        out[name] = jnp.asarray(drawn.astype(out[name].dtype))
    for name, factor in factors.items():
        out[name] = (out[name] * factor).astype(out[name].dtype)
    return out
```

```python
import numpy as np
import concourse.bass as bass
from concourse import mybir
from contextlib import ExitStack

F32 = mybir.dt.float32
BF16 = mybir.dt.bfloat16
I32 = mybir.dt.int32
U32 = mybir.dt.uint32
ALU = mybir.AluOpType
ACT = mybir.ActivationFunctionType
AX = mybir.AxisListType

P = 128
NB, S, D = 16, 256, 512
T = NB * S
NT = T // P
NSTATE = 64
NPAIR = S // 2
JG = 16
NCHUNK = NPAIR // JG
LO, NHI = 128, 4


START = 1


def semaphores(nc, ctx):
    made = []

    def sem(name):
        made.append(ctx.enter_context(nc.semaphore(name)))
        return made[-1]

    return sem, made


def start(eng, made):
    for s in made:
        eng.sem_inc(s, START)


class Chain:

    def __init__(self, eng, sem):
        self.eng, self.sem, self.base, self.n = eng, sem, 0, 0

    def did(self, ins):
        ins.then_inc(self.sem, 1)
        self.n += 1

    def wait(self):
        self.eng.wait_ge(self.sem, self.base + self.n + START)

    def step(self, ins):
        self.did(ins)
        self.wait()

    def enter(self, i, per):
        self.outer, self.per = self.base + self.n, per
        self.base, self.n = self.outer + i * per, 0

    def leave(self, trips):
        assert self.n == self.per, (self.n, self.per)
        self.base, self.n = self.outer + self.per * trips, 0


def state_space(nc, c_in, params, h_dram):
    with ExitStack() as ctx:
        sb = lambda name, shape, dt=F32: ctx.enter_context(nc.sbuf_tensor(name, shape, dt))
        sem, made = semaphores(nc, ctx)
        prm = sb("prm", [P, 5, NPAIR])
        dt_ = sb("dt_", [P, NPAIR])
        ear = sb("ear", [P, NPAIR])
        tmp = sb("tmp", [P, 8, NPAIR])
        scale = sb("scale", [P, 2, NPAIR])
        pw = sb("pw", [P, 8, 2, NPAIR])
        hop = sb("hop", [P, 2, 2, NPAIR])
        cin = sb("cin", [P, 2, JG, 2, NB])
        q = sb("q", [P, 2, 2, JG, LO])
        w = sb("w", [P, 2, 2, JG, NHI, NB])
        ta = sb("ta", [P, 2, JG, LO // 2])
        tb = sb("tb", [P, 2, JG, LO // 2])
        kout = sb("kout", [P, 2, JG, LO])
        ps = [ctx.enter_context(nc.psum_tensor(f"psk{i}", [P, 4, LO], F32)) for i in range(8)]
        prm_in, exps, dchain = sem("prm_in"), sem("exps"), sem("ssm_dve")
        c_loaded = [sem(f"c_loaded{u}") for u in range(2)]
        c_free = [sem(f"c_free{u}") for u in range(2)]
        qw_ready = [sem(f"qw_ready{u}") for u in range(2)]
        k_ready = [sem(f"k_ready{u}") for u in range(2)]
        kout_ready = [sem(f"kout_ready{u}") for u in range(2)]
        h_written = [sem(f"h_written{u}") for u in range(2)]
        pe_turns = sem("pe_turns")
        block = ctx.enter_context(nc.Block())

        @block.sync
        def _(sp):
            start(sp, made)
            sp.dma_start(prm[:, :, :], params[:, :, :]).then_inc(prm_in, 16)
            with sp.Fori(0, NCHUNK // 2) as i:
                for u in range(2):
                    sp.wait_ge(c_free[u], i + START)
                    sp.dma_start(cin[:, u], c_in[:, bass.ds(i * (2 * JG) + u * JG, JG), :, :]).then_inc(c_loaded[u], 16)

        @block.scalar
        def _(act):
            act.wait_ge(prm_in, 16 + START)
            nc.scalar.activation(dt_[:, :], prm[:, 0, :], ACT.Exp).then_inc(exps, 1)
            nc.scalar.activation(ear[:, :], prm[:, 1, :], ACT.Exp).then_inc(exps, 1)
            with act.Fori(0, NCHUNK // 2) as i:
                for u in range(2):
                    act.wait_ge(h_written[u], i * 128 + START)
                    for b in range(4):
                        act.wait_ge(k_ready[u], i * 4 + (b + 1) + START)
                        nc.scalar.activation(kout[:, u, 4 * b:4 * b + 4, :], ps[4 * u + b][:, :, :],
                                             ACT.Copy).then_inc(kout_ready[u], 1)
                    act.wait_ge(kout_ready[u], i * 4 + 4 + START)
                    for h2 in range(2):
                        for a in range(NHI):
                            p0 = h2 * 64 + a * NB
                            j0 = i * (2 * JG) + u * JG
                            dst = h_dram.rearrange("(c j e) d -> e c j d", c=NB, e=2)[
                                h2, :, bass.ds(j0, JG), a * LO:(a + 1) * LO]
                            act.dma_start(dst, kout[p0:p0 + NB, u, :, :]).then_inc(h_written[u], 16)
            for u in range(2):
                act.wait_ge(h_written[u], NCHUNK // 2 * 128 + START)

        @block.vector
        def _(dve):
            v = nc.vector
            ch = Chain(dve, dchain)
            TT = lambda o, a, b, op: ch.did(v.tensor_tensor(o, a, b, op))
            t = [tmp[:, k, :] for k in range(8)]
            dve.wait_ge(prm_in, 16 + START)
            dve.wait_ge(exps, 2 + START)
            ch.did(v.scalar_tensor_tensor(t[0], ear[:, :], -0.5, dt_[:, :], ALU.mult, ALU.mult))
            ch.did(v.scalar_tensor_tensor(t[1], prm[:, 2, :], 0.5, dt_[:, :], ALU.mult, ALU.mult))
            ch.wait()
            ch.did(v.tensor_scalar(t[2], t[0], -1.0, 1.0, ALU.mult, ALU.add))
            ch.did(v.tensor_scalar(t[3], t[0], 1.0, None, ALU.add))
            TT(t[4], t[1], t[1], ALU.mult)
            ch.wait()
            TT(t[5], t[2], t[2], ALU.mult)
            TT(t[3], t[3], t[2], ALU.mult)
            ch.wait()
            TT(t[5], t[5], t[4], ALU.add)
            TT(t[3], t[3], t[4], ALU.subtract)
            ch.wait()
            ch.step(v.reciprocal(t[5], t[5]))
            TT(pw[:, 0, 0, :], t[3], t[5], ALU.mult)
            ch.did(v.scalar_tensor_tensor(pw[:, 0, 1, :], t[1], -2.0, t[5], ALU.mult, ALU.mult))
            ch.did(v.scalar_tensor_tensor(t[5], t[5], 2.0, dt_[:, :], ALU.mult, ALU.mult))
            TT(t[6], prm[:, 3, :], t[2], ALU.mult)
            TT(t[7], prm[:, 4, :], t[1], ALU.mult)
            TT(t[0], prm[:, 3, :], t[1], ALU.mult)
            TT(t[2], prm[:, 4, :], t[2], ALU.mult)
            ch.wait()
            TT(t[6], t[6], t[7], ALU.subtract)
            TT(t[0], t[0], t[2], ALU.add)
            ch.wait()
            TT(scale[:, 0, :], t[6], t[5], ALU.mult)
            TT(scale[:, 1, :], t[0], t[5], ALU.mult)

            def square(dst, src):
                ch.wait()
                TT(t[0], src[:, 0, :], src[:, 0, :], ALU.mult)
                TT(t[1], src[:, 1, :], src[:, 1, :], ALU.mult)
                ch.did(v.scalar_tensor_tensor(dst[:, 1, :], src[:, 0, :], 2.0, src[:, 1, :], ALU.mult, ALU.mult))
                ch.wait()
                TT(dst[:, 0, :], t[0], t[1], ALU.subtract)

            for k in range(7):
                square(pw[:, k + 1], pw[:, k])
            square(hop[:, 0], pw[:, 6])
            ch.wait()
            ch.did(v.tensor_scalar(hop[:, 0, 1, :], hop[:, 0, 1, :], -1.0, None, ALU.mult))
            square(hop[:, 1], hop[:, 0])
            ch.wait()

            def times(dst, x, y, n):
                yr = y[:, 0:1, :].unsqueeze(3).to_broadcast([P, 2, JG, n])
                yi = y[:, 1:2, :].unsqueeze(3).to_broadcast([P, 2, JG, n])
                TT(ta[:, :, :, 0:n], x, yr, ALU.mult)
                TT(tb[:, :, :, 0:n], x, yi, ALU.mult)
                ch.wait()
                TT(dst[:, 0], ta[:, 0, :, 0:n], tb[:, 1, :, 0:n], ALU.subtract)
                TT(dst[:, 1], ta[:, 1, :, 0:n], tb[:, 0, :, 0:n], ALU.add)
                ch.wait()

            with dve.Fori(0, NCHUNK // 2) as i:
                ch.enter(i, 2 * 39)
                for u in range(2):
                    js = bass.ds(i * (2 * JG) + u * JG, JG)
                    dve.wait_ge(c_loaded[u], i * 16 + 16 + START)
                    dve.wait_ge(k_ready[u], i * 4 + START)
                    qu, wu = q[:, u], w[:, u].rearrange("p r j a c -> p r j (a c)")
                    ch.did(v.memset(qu[:, 0, :, 0:1], 1.0))
                    ch.did(v.memset(qu[:, 1, :, 0:1], 0.0))
                    ch.did(v.tensor_copy(qu[:, :, :, 1:2], pw[:, 0, :, js].unsqueeze(3)))
                    times(wu[:, :, :, 0:NB], cin[:, u].rearrange("p j r c -> p r j c"), scale[:, :, js], NB)
                    dve.sem_inc(c_free[u], 1)
                    times(wu[:, :, :, NB:2 * NB], wu[:, :, :, 0:NB], hop[:, 0, :, js], NB)
                    times(wu[:, :, :, 2 * NB:4 * NB], wu[:, :, :, 0:2 * NB], hop[:, 1, :, js], 2 * NB)
                    n = 2
                    for k in range(1, 7):
                        times(qu[:, :, :, n:2 * n], qu[:, :, :, 0:n], pw[:, k, :, js], n)
                        n *= 2
                    dve.sem_inc(qw_ready[u], 1)
                ch.leave(NCHUNK // 2)

        @block.tensor
        def _(pe):
            with pe.Fori(0, NCHUNK // 2) as i:
                for u in range(2):
                    pe.wait_ge(qw_ready[u], i + 1 + START)
                    pe.wait_ge(kout_ready[u], i * 4 + START)
                    pe.sem_inc(pe_turns, 1)
                    for b in range(4):
                        for j in range(4):
                            for h2 in range(2):
                                rows = slice(64 * h2, 64 * h2 + 64)
                                for r in range(2):
                                    last = nc.tensor.matmul(ps[4 * u + b][rows, j, :],
                                                            w[rows, u, r, 4 * b + j].rearrange("p a c -> p (a c)"),
                                                            q[rows, u, r, 4 * b + j], start=(r == 0), stop=(r == 1))
                        last.then_inc(k_ready[u], 1)


NH, DH = 16, 32
NG = D // P
GH = NH // NG
SCALE = float(DH) ** -0.5


def layernorm_stats(nc, ctx, name):
    sb = lambda n, shape: ctx.enter_context(nc.sbuf_tensor(name + n, shape, F32))
    return sb("_stat", [P, NT, 6]), sb("_mv", [P, NT, 2]), sb("_rstd", [P, NT])


def attention(nc, res, h_dram, wqkvo, rope_tab, ident_in, identb_in, mask_in, headmask_in):
    with ExitStack() as ctx:
        sb = lambda name, shape, dt=F32: ctx.enter_context(nc.sbuf_tensor(name, shape, dt))
        sem, made = semaphores(nc, ctx)
        w = sb("w_qkvo", [P, 4, NG, D])
        rope = sb("rope", [P, 2, 2, DH])
        ident = sb("ident", [P, P])
        identb = sb("identb", [P, P], BF16)
        maskb = sb("maskb", [P, GH, P], BF16)
        headmask = sb("headmask", [P, GH])
        ones = sb("ones", [P, DH])
        stat, mv, rstd = layernorm_stats(nc, ctx, "ln1")
        eps = sb("eps", [P, 1])
        xn = sb("xn", [P, 2, D])
        xT = sb("xT", [P, 2, NG, P])
        qk = sb("qk", [P, 4, D])
        rot = sb("rot", [P, 4, D])
        r1 = sb("r1", [P, 2, D])
        r2 = sb("r2", [P, 2, D])
        vnext = sb("vnext", [P, 2, D])
        vcur = sb("vcur", [P, 2, D])
        qT = sb("qT", [P, NG, S])
        kz = sb("kz", [P, NG, GH, S])
        nmax = sb("nmax", [P, 2, GH])
        nbias = sb("nbias", [P, 2, GH])
        p0 = sb("p0", [P, GH, P])
        p1 = sb("p1", [P, GH, S])
        pt0 = sb("pt0", [P, GH, S])
        pt1 = sb("pt1", [P, GH, P])
        rden = sb("rden", [P, S])
        oT = sb("oT", [P, NG, S])
        bank = lambda name, shape: ctx.enter_context(nc.psum_tensor(name, shape, F32))
        pj = [bank("pj0", [P, D]), bank("pj1", [P, D])]
        s0 = bank("s0", [P, GH, P])
        s1 = [bank("s1a", [P, 2, S]), bank("s1b", [P, 2, S])]
        pta, ptb = bank("pta", [P, GH, P]), bank("ptb", [P, GH, P])
        od = bank("od", [P, 2, S])

        loaded, h_in, ln_dve, rstd_ready = sem("loaded"), sem("h_in"), sem("attn_dve"), sem("rstd_ready")
        setup, sqrt_done = sem("setup"), sem("sqrt_done")
        xn_ready = sem("xn_ready")
        pj_full = [sem(f"pj_full{i}") for i in range(2)]
        pj_free = [sem(f"pj_free{i}") for i in range(2)]
        rot_ready, vcur_ready = sem("rot_ready"), sem("vcur_ready")
        s_full, bias_ready, p_ready = sem("s_full"), sem("bias_ready"), sem("p_ready")
        pta_full, ptb_full, pta_free, ptb_free = sem("pta_full"), sem("ptb_full"), sem("pta_free"), sem("ptb_free")
        od_full, oT_ready, pool_pace = sem("od_full"), sem("oT_ready"), sem("attn_pool_pace")
        block = ctx.enter_context(nc.Block())

        USES = ["O0", "O1", "xT0", "xT1", "q0", "q1", "k0", "k1", "v0", "v1", "qTa", "qTb", "kTa", "kTb"]
        LOOP = NB - 1

        class Turn:

            def __init__(self, kind, b):
                self.kind, self.b = kind, b

            def attends(self):
                return self.kind != "first"

            def projects(self):
                return self.kind != "last"

            def pj(self, use):
                n = USES.index(use)
                if self.kind == "first":
                    return n % 2, n // 2 - 1
                return n % 2, self.b * 7 + (6 + n // 2)

        def turns(eng, body, enter=None, leave=None):
            body(Turn("first", -1))
            with eng.Fori(0, LOOP) as i:
                if enter:
                    enter(i)
                body(Turn("loop", i))
                if leave:
                    leave()
            body(Turn("last", NB - 1))

        @block.sync
        def _(sp):
            start(sp, made)
            for k in range(4):
                sp.dma_start(w[:, k], wqkvo[:, k]).then_inc(loaded, 16)
            sp.dma_start(rope[:], rope_tab[:]).then_inc(loaded, 16)
            sp.dma_start(ident[:], ident_in[:]).then_inc(loaded, 16)
            sp.dma_start(identb[:], identb_in[:]).then_inc(loaded, 16)
            sp.dma_start(maskb[:], mask_in[:]).then_inc(loaded, 16)
            sp.dma_start(headmask[:], headmask_in[:]).then_inc(loaded, 16)

        @block.gpsimd
        def _(pool):
            def body(t):
                if t.projects():
                    for name in ("v0", "v1"):
                        n, before = t.pj(name)
                        pool.wait_ge(pj_free[n], before + 1 + START)
                    if t.attends():
                        pool.wait_ge(od_full, t.b * NG + NG + START)
                    pool.sem_inc(pool_pace, 1)
                    nc.gpsimd.tensor_copy(vcur[:], vnext[:]).then_inc(vcur_ready, 1)

            turns(pool, body)

        @block.scalar
        def _(act):
            for q in range(8):
                act.dma_start(res[:, 2 + 4 * q:6 + 4 * q, :],
                              h_dram.rearrange("(t p) d -> p t d", p=P)[:, 4 * q:4 * q + 4, :]).then_inc(h_in, 16)
            act.wait_ge(rstd_ready, 1 + START)
            nc.scalar.activation(rstd[:, :], mv[:, :, 1], ACT.Sqrt, bias=eps[:, :]).then_inc(sqrt_done, 1)

            nc.scalar.preload_act_table(ACT.Exp)

            def body(t):
                A = nc.scalar.activation
                G = lambda g: t.b * NG + g

                for g in range(NG):
                    if g == 1 and t.projects():
                        for u in range(2):
                            n, before = t.pj(f"xT{u}")
                            act.wait_ge(pj_full[n], before + 1 + START)
                            A(xT[:, u].rearrange("p c t -> p (c t)"), pj[n][:, :], ACT.Copy).then_inc(pj_free[n], 1)
                    if t.attends():
                        act.wait_ge(bias_ready, G(g) + 1 + START)
                        for h in range(GH):
                            last = A(p0[:, h, :], s0[:, h, :], ACT.Exp, bias=nbias[:, 0, h:h + 1], scale=SCALE)
                        last.then_inc(p_ready, 1)
                        for h in range(GH):
                            last = A(p1[:, h, :], s1[h // 2][:, h % 2, :], ACT.Exp, bias=nbias[:, 1, h:h + 1], scale=SCALE)
                        last.then_inc(p_ready, 1)
                    if t.projects():
                        for name in {1: ["q0", "q1"], 2: ["k0", "k1"], 3: ["v0", "v1"]}.get(g, []):
                            n, before = t.pj(name)
                            act.wait_ge(pj_full[n], before + 1 + START)
                            u = int(name[1])
                            dst = vnext[:, u] if name[0] == "v" else qk[:, 2 * (name[0] == "k") + u]
                            if name == "v0" and t.attends():
                                act.wait_ge(vcur_ready, t.b + 1 + START)
                            A(dst, pj[n][:, :], ACT.Copy).then_inc(pj_free[n], 1)
                        if g == 3:
                            for k, name in enumerate(["qTa", "qTb"]):
                                n, before = t.pj(name)
                                act.wait_ge(pj_full[n], before + 1 + START)
                                A(qT[:, 2 * k:2 * k + 2, :], pj[n][:, :], ACT.Copy).then_inc(pj_free[n], 1)
                    if t.attends():
                        act.wait_ge(pta_full, G(g) * 2 + 1 + START)
                        A(pt0[:, :, 0:P], pta[:], ACT.Copy).then_inc(pta_free, 1)
                        act.wait_ge(pta_full, G(g) * 2 + 2 + START)
                        A(pt1[:], pta[:], ACT.Copy).then_inc(pta_free, 1)

            turns(act, body)

        @block.vector
        def _(dve):
            v = nc.vector
            ch = Chain(dve, ln_dve)
            ch.did(v.memset(eps[:], 1e-5))
            ch.did(v.memset(ones[:], 1.0))
            ch.did(v.memset(oT[:], 0.0))
            ch.did(v.memset(res[:, 0:2, :], 0.0))
            for k in range(NT):
                if k % 4 == 0:
                    dve.wait_ge(h_in, 16 * 8 + START)
                ch.did(v.bn_stats(stat[:, k, :], res[:, 2 + k, :]))
            ch.wait()
            for k in range(NT):
                ch.did(v.bn_aggr(mv[:, k, :], stat[:, k, :]))
            ch.wait()
            dve.sem_inc(rstd_ready, 1)
            dve.wait_ge(sqrt_done, 1 + START)
            ch.step(v.reciprocal(rstd[:, :], rstd[:, :]))
            dve.wait_ge(loaded, 16 * 9 + START)
            dve.sem_inc(setup, 1)

            def body(t):
                G = lambda g: t.b * NG + g
                B1 = t.b + 1
                for g in range(NG):
                    if t.attends():
                        dve.wait_ge(s_full, G(g) + 1 + START)
                        ch.did(v.tensor_reduce(nmax[:, 0, :], s0[:], AX.X, ALU.max, negate=True))
                        for k in range(2):
                            ch.did(v.tensor_reduce(nmax[:, 1, 2 * k:2 * k + 2], s1[k][:], AX.X, ALU.max, negate=True))
                        ch.wait()
                        v.tensor_scalar(nbias[:], nmax[:], SCALE, None, ALU.mult).then_inc(bias_ready, 1)
                        if g == 0:
                            for u in range(2):
                                n, before = t.pj(f"O{u}")
                                dve.wait_ge(pj_full[n], before + 1 + START)
                                slot = res[:, bass.ds(t.b * 2 + u, 1), :] if t.kind == "loop" else res[:, t.b * 2 + u:t.b * 2 + u + 1, :]
                                v.tensor_tensor(slot, pj[n][:, :].unsqueeze(1), slot, ALU.add).then_inc(pj_free[n], 1)
                    if g == 0 and t.projects():
                        for u in range(2):
                            k = B1 * 2 + u
                            at = (lambda a: a[:, bass.ds(k, 1)]) if t.kind == "loop" else (lambda a: a[:, k:k + 1])
                            src = res[:, bass.ds(k + 2, 1), :] if t.kind == "loop" else res[:, k + 2:k + 3, :]
                            if t.attends():
                                n, before = t.pj(f"xT{u}")
                                dve.wait_ge(pj_full[n], before - 6 + START)
                            v.tensor_scalar(xn[:, u:u + 1, :], src, at(mv[:, :, 0]), at(rstd[:, :]),
                                            ALU.subtract, ALU.mult).then_inc(xn_ready, 1)
                    if g in (1, 2) and t.projects():
                        for u in range(2):
                            name = "qk"[g - 1] + str(u)
                            n, before = t.pj(name)
                            dve.wait_ge(pj_free[n], before + 1 + START)
                            k = 2 * (g - 1) + u
                            src = qk[:, k].rearrange("p (h e f) -> p h e f", h=NH, e=2)
                            cos = rope[:, u, 0:1, :].to_broadcast([P, NH, DH])
                            sn = rope[:, u, 1, :].rearrange("p (e f) -> p e f", e=2)
                            r1v = r1[:, u].rearrange("p (h f) -> p h f", h=NH)
                            r2v = r2[:, u].rearrange("p (h e f) -> p h e f", h=NH, e=2)
                            ch.did(v.tensor_tensor(r1v, qk[:, k].rearrange("p (h f) -> p h f", h=NH), cos, ALU.mult))
                            for e in range(2):
                                ch.did(v.tensor_tensor(r2v[:, :, e], src[:, :, 1 - e],
                                                       sn[:, e:e + 1, :].to_broadcast([P, NH, DH // 2]), ALU.mult))
                            ch.wait()
                            v.tensor_tensor(rot[:, k], r1[:, u], r2[:, u], ALU.add).then_inc(rot_ready, 1)
                    if g == 3 and t.projects():
                        for k, name in enumerate(["kTa", "kTb"]):
                            n, before = t.pj(name)
                            dve.wait_ge(pj_full[n], before + 1 + START)
                            for e in range(2):
                                src = pj[n][:, e * S:(e + 1) * S].unsqueeze(1).to_broadcast([P, GH, S])
                                last = v.tensor_tensor(kz[:, 2 * k + e], src,
                                                       headmask[:, :].unsqueeze(2).to_broadcast([P, GH, S]), ALU.mult)
                            last.then_inc(pj_free[n], 1)
                    if t.attends():
                        dve.wait_ge(ptb_full, G(g) + 1 + START)
                        v.tensor_copy(pt0[:, :, P:S], ptb[:]).then_inc(ptb_free, 1)
                        dve.wait_ge(od_full, G(g) + 1 + START)
                        ch.step(v.reciprocal(rden[:], od[:, 1, :]))
                        v.tensor_tensor(oT[:, g, :], od[:, 0, :], rden[:], ALU.mult).then_inc(oT_ready, 1)

            body(Turn("first", -1))
            with dve.Fori(0, LOOP) as i:
                ch.enter(i, NG * (3 + 1) + 4 * 3)
                body(Turn("loop", i))
                ch.leave(LOOP)
            body(Turn("last", NB - 1))
            dve.wait_ge(oT_ready, NB * NG + START)
            n, before = Turn("last", NB - 1).pj("O0")
            for u in range(2):
                dve.wait_ge(pj_full[u], before + 2 + START)
                slot = res[:, 2 * NB + u, :]
                v.tensor_tensor(slot, pj[u][:, :], slot, ALU.add).then_inc(pj_free[u], 1)
            for u in range(2):
                dve.wait_ge(pj_free[u], before + 2 + START)

        @block.tensor
        def _(pe):
            mm = nc.tensor.matmul
            pe.wait_ge(setup, 1 + START)

            def use(t, name):
                n, before = t.pj(name)
                pe.wait_ge(pj_free[n], before + START)
                return n

            def out_proj(n, u):
                for c in range(NG):
                    last = mm(pj[n][:, :], oT[:, c, u * P:(u + 1) * P], w[:, 3, c, :], start=(c == 0), stop=(c == NG - 1))
                last.then_inc(pj_full[n], 1)

            def body(t):
                G = lambda g: t.b * NG + g
                for g in range(NG):
                    if t.attends():
                        if g == 0:
                            n, before = t.pj("O0")
                            for n in range(2):
                                pe.wait_ge(pj_free[n], before + START)
                        mm(s0[:], qT[:, g, 0:P], kz[:, g, :, 0:P], start=True, stop=False)
                        for k in range(2):
                            mm(s1[k][:], qT[:, g, P:S], kz[:, g, 2 * k:2 * k + 2, :], start=True, stop=False)
                        mm(s0[:], identb[:], maskb[:], start=False, stop=True)
                        for k in range(2):
                            last = mm(s1[k][:, :, P:S], identb[:], maskb[:, 0:2, :], start=False, stop=True)
                        last.then_inc(s_full, 1)
                    if g == 0 and t.attends():
                        pe.wait_ge(oT_ready, t.b * NG + START)
                        for u in range(2):
                            out_proj(use(t, f"O{u}"), u)
                    if g == 1 and t.projects():
                        for u in range(2):
                            n = use(t, f"xT{u}")
                            pe.wait_ge(xn_ready, (t.b + 1) * 2 + (u + 1) + START)
                            for c in range(NG):
                                last = nc.tensor.transpose(pj[n][:, c * P:(c + 1) * P], xn[:, u, c * P:(c + 1) * P], ident[:])
                            last.then_inc(pj_full[n], 1)
                        for u in range(2):
                            n, before = t.pj(f"xT{u}")
                            pe.wait_ge(pj_free[n], before + 1 + START)
                    if g >= 1 and t.projects():
                        for u in range(2):
                            n = use(t, "qkv"[g - 1] + str(u))
                            for c in range(NG):
                                last = mm(pj[n][:, :], xT[:, u, c], w[:, g - 1, c, :], start=(c == 0), stop=(c == NG - 1))
                            last.then_inc(pj_full[n], 1)
                    if g == 3 and t.projects():
                        for k, name in enumerate(["qTa", "qTb", "kTa", "kTb"]):
                            n = use(t, name)
                            pe.wait_ge(rot_ready, (t.b + 1) * 4 + 2 + 2 * (k // 2) + START)
                            for e in range(2):
                                for u in range(2):
                                    c = 2 * (k % 2) + e
                                    last = nc.tensor.transpose(pj[n][:, e * S + u * P:e * S + (u + 1) * P],
                                                               rot[:, 2 * (k // 2) + u, c * P:(c + 1) * P], ident[:])
                            last.then_inc(pj_full[n], 1)
                    if t.attends():
                        pe.wait_ge(p_ready, G(g) * 2 + 1 + START)
                        pe.wait_ge(pta_free, G(g) * 2 + START)
                        for h in range(GH):
                            last = nc.tensor.transpose(pta[:, h, :], p0[:, h, :], ident[:])
                        last.then_inc(pta_full, 1)
                        pe.wait_ge(p_ready, G(g) * 2 + 2 + START)
                        pe.wait_ge(ptb_free, G(g) + START)
                        for h in range(GH):
                            last = nc.tensor.transpose(ptb[:, h, :], p1[:, h, 0:P], ident[:])
                        last.then_inc(ptb_full, 1)
                        pe.wait_ge(pta_free, G(g) * 2 + 1 + START)
                        for h in range(GH):
                            last = nc.tensor.transpose(pta[:, h, :], p1[:, h, P:S], ident[:])
                        last.then_inc(pta_full, 1)
                        if g == 0:
                            pe.wait_ge(vcur_ready, t.b + 1 + START)
                        pe.wait_ge(ptb_free, G(g) + 1 + START)
                        pe.wait_ge(oT_ready, G(g) + START)
                        for k in range(2):
                            if k == 1:
                                pe.wait_ge(pta_free, G(g) * 2 + 2 + START)
                            for h in range(GH):
                                rows = slice(32 * h, 32 * h + 32)
                                head = slice((g * GH + h) * DH, (g * GH + h + 1) * DH)
                                src = pt1[:, h, :] if k else pt0[:, h, :]
                                cols = slice(P, S) if k else slice(0, S)
                                mm(od[rows, 0, cols], vcur[:, k, head], src, start=(k == 0), stop=(k == 1), skip_group_check=True)
                                last = mm(od[rows, 1, cols], ones[:], src, start=False, stop=(k == 1), skip_group_check=True)
                        last.then_inc(od_full, 1)

            turns(pe, body)
            pe.wait_ge(oT_ready, NB * NG + START)
            n, before = Turn("last", NB - 1).pj("O0")
            for u in range(2):
                pe.wait_ge(pj_free[u], before + 1 + START)
                out_proj(u, u)


NE, NGRP, GE = 32, 8, 4
TOPG, TOPK = 3, 4
CAP = -(-5 * T // (4 * NE))
HALF = CAP // 2
DI = 256
ROUTE_SCALE = 2.5
FAR = 1 << 20


def route(nc, res, xT2, wk, slots, rw_in, bias_in, ident_in, tri_in, ones_in, iota_in, xn_dram, table):
    with ExitStack() as ctx:
        sb = lambda name, shape, dt=F32: ctx.enter_context(nc.sbuf_tensor(name, shape, dt))
        sem, made = semaphores(nc, ctx)
        rw = sb("rw", [P, NG, NE])
        bias = sb("bias", [P, NE])
        ident = sb("ident2", [P, P])
        tri = sb("tri", [P, P], BF16)
        ones = sb("ones2", [P, P], BF16)
        iota = sb("iota", [P, 3, NE])
        stat, mv, rstd = layernorm_stats(nc, ctx, "ln2")
        eps = sb("eps2", [P, 1])
        xn = sb("xn2", [P, 2, D])
        lgT = sb("lgT", [P, 2, 4 * P])
        score = sb("score", [P, NT, NE])
        sc = sb("sc", [P, NT, NE])
        ga = sb("ga", [P, 4, NT * NGRP])
        gs = sb("gs", [P, NT, NGRP])
        gpick = sb("gpick", [P, NT, NGRP])
        gmask = sb("gmask", [P, NT, NGRP])
        gcand = sb("gcand", [P, NT, NGRP])
        best = sb("best", [P, NT])
        cand = sb("cand", [P, NT, NE])
        oh = sb("oh", [P, TOPK, NT, NE])
        chosen = sb("chosen", [P, NT, NE])
        chosenb = sb("chosenb", [P, NT, NE], BF16)
        before = sb("before", [P, NE, NT])
        scanned = sb("scanned", [P, NE, NT])
        gate = sb("gate", [P, NE, NT])
        slotf = sb("slotf", [P, TOPK, NT])
        wsel = sb("wsel", [P, TOPK, NT])
        wsum = sb("wsum", [P, NT])
        far = sb("far", [P, 2 * NE * CAP // P])
        tok = sb("tok", [P, NT], I32)
        bank = lambda name, shape: ctx.enter_context(nc.psum_tensor(name, shape, F32))
        tp = [bank(f"tp{u}", [P, NG, P]) for u in range(2)]
        lg = [bank(f"lg{u}", [P, 4 * P]) for u in range(2)]
        pre = [bank(f"pre{u}", [P, NT // 2, NE]) for u in range(2)]
        tot = [bank(f"tot{u}", [P, NT // 2, NE]) for u in range(2)]
        loaded, chain, mv_ready, sqrt_done = sem("loaded2"), sem("route_dve"), sem("mv_ready"), sem("sqrt_done2")
        xn_ready = [sem(f"xn2_ready{u}") for u in range(2)]
        stored = [sem(f"xn2_stored{u}") for u in range(2)]
        tp_full = [sem(f"tp_full{u}") for u in range(2)]
        tp_free = [sem(f"tp_free{u}") for u in range(2)]
        lg_full, lgT_ready, lt_full, score_ready = sem("lg_full"), sem("lgT_ready"), sem("lt_full"), sem("score_ready")
        chosen_ready, counted, far_set, far_out, act_pace = (
            sem("chosen_ready"), sem("counted"), sem("far_set"), sem("far_out"), sem("act_pace"))
        block = ctx.enter_context(nc.Block())
        TILES2 = NT // 2

        @block.sync
        def _(sp):
            start(sp, made)
            for dst, src in ((rw, rw_in), (bias, bias_in), (ident, ident_in), (tri, tri_in), (ones, ones_in), (iota, iota_in)):
                sp.dma_start(dst[:], src[:]).then_inc(loaded, 16)
            sp.wait_ge(far_set, 2 + START)
            sp.dma_start(table.rearrange("(p s) c -> p (s c)", p=P), far[:]).then_inc(far_out, 16)
            rows = xn_dram.rearrange("(t p) d -> p t d", p=P)
            with sp.Fori(0, TILES2) as i:
                for u in range(2):
                    sp.wait_ge(xn_ready[u], i + 1 + START)
                    sp.dma_start(rows[:, bass.ds(i * 2 + u, 1), :], xn[:, u:u + 1, :]).then_inc(stored[u], 16)
            for u in range(2):
                sp.wait_ge(stored[u], 16 * TILES2 + START)
            sp.wait_ge(far_out, 16 + START)

        @block.gpsimd
        def _(pool):
            g = nc.gpsimd
            fv = far[:].rearrange("p (s c) -> p s c", c=2)
            g.memset(fv[:, :, 0], float(FAR)).then_inc(far_set, 1)
            g.memset(fv[:, :, 1], 0.0).then_inc(far_set, 1)
            g.iota(tok[:], [[P, NT]], base=0, channel_multiplier=1).then_inc(far_set, 1)
            pool.wait_ge(far_set, 3 + START)
            for k in range(TOPK):
                g.tensor_copy(wk[:, k, :, 0], tok[:]).then_inc(far_set, 1)
            pool.wait_ge(far_set, 3 + TOPK + START)

        @block.scalar
        def _(act):
            act.wait_ge(mv_ready, 1 + START)
            nc.scalar.activation(rstd[:, :], mv[:, :, 1], ACT.Sqrt, bias=eps[:, :]).then_inc(sqrt_done, 1)
            nc.scalar.preload_act_table(ACT.Sigmoid)
            with act.Fori(0, TILES2) as i:
                for u in range(2):
                    act.wait_ge(tp_full[u], i + 1 + START)
                    act.sem_inc(act_pace, 1)
                    nc.scalar.activation(xT2[:, :, bass.ds(i * (2 * P) + u * P, P)], tp[u][:], ACT.Copy).then_inc(tp_free[u], 1)
            for k in range(2):
                act.wait_ge(lg_full, k + 1 + START)
                nc.scalar.activation(lgT[:, k], lg[k][:], ACT.Copy).then_inc(lgT_ready, 1)
            for k in range(2):
                act.wait_ge(lt_full, k + 1 + START)
                dst = score[:, 16 * k:16 * k + 16, :].rearrange("p (j q) e -> p q j e", q=4)
                for qb in range(4):
                    last = nc.scalar.activation(dst[:, qb], tp[k][:, qb].rearrange("p (j e) -> p j e", j=4), ACT.Sigmoid)
                last.then_inc(score_ready, 1)

        @block.tensor
        def _(pe):
            mm = nc.tensor.matmul
            pe.wait_ge(loaded, 16 * 6 + START)
            with pe.Fori(0, TILES2) as i:
                for u in range(2):
                    pe.wait_ge(tp_free[u], i + START)
                    pe.wait_ge(xn_ready[u], i + 1 + START)
                    for c in range(NG):
                        last = nc.tensor.transpose(tp[u][:, c, :], xn[:, u, c * P:(c + 1) * P], ident[:])
                    last.then_inc(tp_full[u], 1)
            for u in range(2):
                pe.wait_ge(tp_free[u], TILES2 + START)
            for k in range(2):
                for c in range(NG):
                    for j in range(4):
                        tok = (4 * k + j) * 4 * P
                        last = mm(lg[k][32 * j:32 * j + 32, :], rw[:, c, :], xT2[:, c, tok:tok + 4 * P],
                                  start=(c == 0), stop=(c == NG - 1), skip_group_check=True)
                last.then_inc(lg_full, 1)
            for k in range(2):
                pe.wait_ge(lgT_ready, k + 1 + START)
                for qb in range(4):
                    last = nc.tensor.transpose(tp[k][:, qb, :], lgT[:, k, qb * P:(qb + 1) * P], ident[:])
                last.then_inc(lt_full, 1)
            pe.wait_ge(chosen_ready, 1 + START)
            for k in range(2):
                mm(pre[k][:], tri[:], chosenb[:, 16 * k:16 * k + 16, :], start=True, stop=True)
                last = mm(tot[k][:], ones[:], chosenb[:, 16 * k:16 * k + 16, :], start=True, stop=True)
            last.then_inc(counted, 1)

        @block.vector
        def _(dve):
            v = nc.vector
            ch = Chain(dve, chain)
            ch.did(v.memset(eps[:], 1e-5))
            for k in range(NT):
                ch.did(v.bn_stats(stat[:, k, :], res[:, 2 + k, :]))
            ch.wait()
            for k in range(NT):
                ch.did(v.bn_aggr(mv[:, k, :], stat[:, k, :]))
            ch.wait()
            dve.sem_inc(mv_ready, 1)
            dve.wait_ge(sqrt_done, 1 + START)
            ch.step(v.reciprocal(rstd[:, :], rstd[:, :]))
            with dve.Fori(0, TILES2) as i:
                for u in range(2):
                    dve.wait_ge(tp_full[u], i + START)
                    dve.wait_ge(stored[u], i * 16 + START)
                    k = bass.ds(i * 2 + u, 1)
                    v.tensor_scalar(xn[:, u:u + 1, :], res[:, bass.ds(i * 2 + (u + 2), 1), :], mv[:, k, 0], rstd[:, k],
                                    ALU.subtract, ALU.mult).then_inc(xn_ready[u], 1)

            TT = lambda o, a, b, op: ch.did(v.tensor_tensor(o, a, b, op))
            along = lambda a, n: a.unsqueeze(2).to_broadcast([P, NT, n])
            row = lambda k, n: iota[:, k:k + 1, 0:n].to_broadcast([P, NT, n])

            def first_best(cand_, pick, values, k, n):
                ch.step(v.tensor_reduce(best[:], values, AX.X, ALU.max))
                TT(cand_, values, along(best[:], n), ALU.is_equal)
                ch.wait()
                TT(cand_, cand_, row(k, n), ALU.mult)
                ch.wait()
                ch.step(v.tensor_reduce(best[:], cand_, AX.X, ALU.min))
                TT(pick, row(k, n), along(best[:], n), ALU.is_equal)
                ch.wait()

            dve.wait_ge(score_ready, 2 + START)
            ch.step(v.tensor_tensor(sc[:], score[:], bias[:, :].unsqueeze(1).to_broadcast([P, NT, NE]), ALU.add))
            four = sc[:].rearrange("p t (g m) -> p (t g) m", m=GE)
            TT(ga[:, 0], four[:, :, 0], four[:, :, 1], ALU.max)
            TT(ga[:, 1], four[:, :, 2], four[:, :, 3], ALU.max)
            TT(ga[:, 2], four[:, :, 0], four[:, :, 1], ALU.add)
            TT(ga[:, 3], four[:, :, 2], four[:, :, 3], ALU.add)
            ch.wait()
            gsf = gs[:].rearrange("p t g -> p (t g)")
            TT(gsf, ga[:, 0], ga[:, 1], ALU.add)
            TT(ga[:, 2], ga[:, 2], ga[:, 3], ALU.max)
            ch.wait()
            TT(gsf, gsf, ga[:, 2], ALU.max)
            ch.wait()
            for k in range(TOPG):
                first_best(gcand[:], gpick[:] if k else gmask[:], gs[:], 1, NGRP)
                ch.did(v.scalar_tensor_tensor(gs[:], gpick[:] if k else gmask[:], -1e30, gs[:], ALU.mult, ALU.add))
                if k:
                    TT(gmask[:], gmask[:], gpick[:], ALU.add)
                ch.wait()
            TT(four, four, gmask[:].rearrange("p t g -> p (t g)").unsqueeze(2).to_broadcast([P, NT * NGRP, GE]), ALU.mult)
            ch.wait()
            for k in range(TOPK):
                first_best(cand[:], oh[:, k], sc[:], 0, NE)
                ch.did(v.scalar_tensor_tensor(sc[:], oh[:, k], -1e30, sc[:], ALU.mult, ALU.add))
                TT(cand[:], oh[:, k], score[:], ALU.mult)
                if k:
                    TT(chosen[:], chosen[:] if k > 1 else oh[:, 0], oh[:, k], ALU.add)
                ch.wait()
                ch.step(v.tensor_reduce(wsel[:, k], cand[:], AX.X, ALU.add))
            v.tensor_copy(chosenb[:], chosen[:]).then_inc(chosen_ready, 1)
            TT(wsum[:], wsel[:, 0], wsel[:, 1], ALU.add)
            ch.wait()
            for k in range(2, TOPK):
                ch.step(v.tensor_tensor(wsum[:], wsum[:], wsel[:, k], ALU.add))
            ch.step(v.tensor_scalar(wsum[:], wsum[:], 1e-20, None, ALU.add))
            ch.step(v.reciprocal(wsum[:], wsum[:]))
            for k in range(TOPK):
                ch.did(v.scalar_tensor_tensor(wk[:, k, :, 1], wsel[:, k], ROUTE_SCALE, wsum[:], ALU.mult, ALU.mult))
            ch.did(v.memset(before[:, :, 0:1], 0.0))
            ch.did(v.memset(gate[:], 1.0))
            ch.wait()
            ch.did(v.memset(gate[:, :, 0:1], 0.0))
            dve.wait_ge(counted, 1 + START)
            half = NT // 2
            ch.did(v.tensor_copy(before[:, :, 1:half + 1], tot[0][:].rearrange("p t e -> p e t")))
            ch.did(v.tensor_copy(before[:, :, half + 1:NT], tot[1][:, 0:half - 1, :].rearrange("p t e -> p e t")))
            ch.wait()
            ch.step(v.tensor_tensor_scan(scanned[:].rearrange("p e t -> p (e t)"), gate[:].rearrange("p e t -> p (e t)"),
                                         before[:].rearrange("p e t -> p (e t)"), 0.0, ALU.mult, ALU.add))
            for k in range(2):
                TT(chosen[:, 16 * k:16 * k + 16, :], pre[k][:], scanned[:].rearrange("p e t -> p t e")[:, 16 * k:16 * k + 16, :], ALU.add)
            ch.wait()
            ch.did(v.tensor_scalar(cand[:], chosen[:], float(CAP), float(FAR), ALU.is_ge, ALU.mult))
            TT(chosen[:], chosen[:], row(2, NE), ALU.add)
            ch.wait()
            TT(chosen[:], chosen[:], cand[:], ALU.add)
            ch.wait()
            for k in range(TOPK):
                TT(cand[:], oh[:, k], chosen[:], ALU.mult)
                ch.wait()
                ch.step(v.tensor_reduce(slotf[:, k], cand[:], AX.X, ALU.add))
            ch.step(v.tensor_copy(slots[:], slotf[:]))


def shared_and_table(nc, res, xT2, wk, slots, shared_w, table, out):
    TB = 4 * P
    NBLK = T // TB
    with ExitStack() as ctx:
        sb = lambda name, shape, dt=F32: ctx.enter_context(nc.sbuf_tensor(name, shape, dt))
        sem, made = semaphores(nc, ctx)
        w = sb("w_shared", [P, 3, NG, D])
        sg = sb("sg", [P, 2, TB])
        hT = sb("hT", [P, NG, TB])
        bank = lambda name, shape: ctx.enter_context(nc.psum_tensor(name, shape, F32))
        pg = [bank(f"pg{u}", [P, TB]) for u in range(2)]
        pu = [bank(f"pu{u}", [P, TB]) for u in range(2)]
        py = [bank(f"py{u}", [P, D]) for u in range(2)]
        loaded, stored = sem("loaded3"), sem("stored")
        slots_out = ctx.enter_context(nc.semaphore("slots_out"))
        gu_full = [sem(f"gu_full{u}") for u in range(2)]
        sg_ready = [sem(f"sg_ready{u}") for u in range(2)]
        hT_ready = [sem(f"hT_ready{u}") for u in range(2)]
        py_full = [sem(f"py_full{u}") for u in range(2)]
        py_free = [sem(f"py_free{u}") for u in range(2)]
        block = ctx.enter_context(nc.Block())

        @block.sync
        def _(sp):
            start(sp, made)
            for k in range(3):
                sp.dma_start(w[:, k], shared_w[:, k]).then_inc(loaded, 16)
            rows = out.rearrange("(t p) d -> p t d", p=P)
            with sp.Fori(0, NBLK) as i:
                for u in range(2):
                    sp.wait_ge(py_free[u], i * 2 + 2 + START)
                sp.dma_start(rows[:, bass.ds(i * 4, 4), :], res[:, bass.ds(i * 4 + 2, 4), :]).then_inc(stored, 16)
            sp.wait_ge(stored, 16 * NBLK + START)

        @block.gpsimd
        def _(pool):
            for k in range(TOPK):
                for t in range(NT):
                    nc.gpsimd.indirect_dma_start(
                        table[:, :], bass.IndirectOffsetOnAxis(slots[:, k, t:t + 1].bitcast(U32), 0),
                        wk[:, k, t, :], None, bounds_check=NE * CAP - 1, oob_is_err=False).then_inc(slots_out, 16)
            pool.wait_ge(slots_out, 16 * TOPK * NT)

        @block.tensor
        def _(pe):
            mm = nc.tensor.matmul
            pe.wait_ge(loaded, 48 + START)
            with pe.Fori(0, NBLK) as i:
                for f in range(NG):
                    u = f % 2
                    pe.wait_ge(hT_ready[u], i * 2 + f // 2 + START)
                    for dst, k in ((pg, 0), (pu, 1)):
                        for c in range(NG):
                            last = mm(dst[u][:], w[:, k, c, f * P:(f + 1) * P], xT2[:, c, bass.ds(i * TB, TB)],
                                      start=(c == 0), stop=(c == NG - 1))
                    last.then_inc(gu_full[u], 1)
                for u in range(2):
                    pe.wait_ge(hT_ready[u], i * 2 + 2 + START)
                for q in range(4):
                    u = q % 2
                    pe.wait_ge(py_free[u], i * 2 + q // 2 + START)
                    for f in range(NG):
                        last = mm(py[u][:], hT[:, f, q * P:(q + 1) * P], w[:, 2, f, :], start=(f == 0), stop=(f == NG - 1))
                    last.then_inc(py_full[u], 1)

        @block.scalar
        def _(act):
            with act.Fori(0, NBLK) as i:
                for f in range(NG):
                    u = f % 2
                    act.wait_ge(hT_ready[u], i * 2 + f // 2 + START)
                    act.wait_ge(gu_full[u], i * 2 + (f // 2 + 1) + START)
                    nc.scalar.activation(sg[:, u], pg[u][:], ACT.Silu).then_inc(sg_ready[u], 1)

        @block.vector
        def _(dve):
            v = nc.vector
            with dve.Fori(0, NBLK) as i:
                for f in range(NG):
                    u = f % 2
                    dve.wait_ge(sg_ready[u], i * 2 + (f // 2 + 1) + START)
                    if f < 2:
                        for b in range(2):
                            dve.wait_ge(py_full[b], i * 2 + START)
                    v.tensor_tensor(hT[:, f], pu[u][:], sg[:, u], ALU.mult).then_inc(hT_ready[u], 1)
                for q in range(4):
                    u = q % 2
                    dve.wait_ge(py_full[u], i * 2 + (q // 2 + 1) + START)
                    slot = res[:, bass.ds(i * 4 + (q + 2), 1), :]
                    v.tensor_tensor(slot, py[u][:].unsqueeze(1), slot, ALU.add).then_inc(py_free[u], 1)


def experts(nc, gate_in, up_in, down_in, ident_in, xn_dram, table, out):
    NI = DI // P
    with ExitStack() as ctx:
        sb = lambda name, shape, dt=F32: ctx.enter_context(nc.sbuf_tensor(name, shape, dt))
        sem, made = semaphores(nc, ctx)
        ident = sb("ident4", [P, P])
        wg = sb("wg", [P, 2, NG, DI])
        wu = sb("wu", [P, 2, NG, DI])
        wd = sb("wd", [P, 2, NI, D])
        tab = sb("tab", [2 * NE, HALF, 2])
        tokens = sb("tokens", [HALF, 2 * NE], I32)
        weight = sb("weight", [HALF, 2 * NE])
        xtok = sb("xtok", [HALF, 2, 2], I32)
        ytok = sb("ytok", [HALF, 2, 2], I32)
        xg = sb("xg", [HALF, 2, 2, D])
        xT = sb("xTe", [P, 2, NG, CAP])
        sg = sb("sge", [P, NI, CAP])
        hT = sb("hTe", [P, 2, NI, CAP])
        y = sb("y", [HALF, 2, 2, D])
        bank = lambda name, shape: ctx.enter_context(nc.psum_tensor(name, shape, F32))
        px = [bank(f"px{k}", [P, 2, CAP]) for k in range(2)]
        pg, pu = bank("peg", [P, NI, CAP]), bank("peu", [P, NI, CAP])
        py = [bank(f"pey{k}", [P, D]) for k in range(2)]
        two = lambda name: [sem(f"{name}{u}") for u in range(2)]
        ident_loaded, cleared = sem("ident_loaded"), sem("cleared")
        tab_loaded, tab_turned, tab_ready = sem("tab_loaded"), sem("tab_turned"), sem("tab_ready")
        gu_loaded, d_loaded = two("gu_loaded"), two("d_loaded")
        x_full, xT_ready = two("x_full"), two("xT_ready")
        gu_full, sg_ready, hT_ready, y_full, y_ready, y_done = (
            two("egu_full"), two("esg_ready"), two("ehT_ready"), two("ey_full"), two("ey_ready"), two("ey_done"))
        x_loaded, y_added = [[ctx.enter_context(nc.semaphore(f"{name}{u}")) for u in range(2)]
                             for name in ("x_loaded", "y_added")]
        picked = sem("picked")
        pace = sem("expert_pace")
        block = ctx.enter_context(nc.Block())
        HE = NE // 2

        @block.sync
        def _(sp):
            start(sp, made)
            sp.dma_start(tab[:], table.rearrange("(g s) c -> g s c", s=HALF)).then_inc(tab_loaded, 16)
            sp.dma_start(ident[:], ident_in[:]).then_inc(ident_loaded, 16)
            with sp.Fori(0, HE) as i:
                for u in range(2):
                    e = bass.ds(i * 2 + u, 1)
                    sp.wait_ge(gu_full[u], i + START)
                    sp.dma_start(wg[:, u:u + 1], gate_in[:, e]).then_inc(gu_loaded[u], 16)
                    sp.dma_start(wu[:, u:u + 1], up_in[:, e]).then_inc(gu_loaded[u], 16)
                    sp.wait_ge(y_full[u], i + START)
                    sp.dma_start(wd[:, u:u + 1], down_in[:, e]).then_inc(d_loaded[u], 16)

        @block.gpsimd
        def _(pool):
            g = nc.gpsimd
            pool.wait_ge(cleared, 1 + START)
            pool.wait_ge(tab_ready, 2 + START)

            def gather(i, u):
                pool.wait_ge(x_full[u], i + START)
                pool.sem_inc(pace, 1)
                g.tensor_copy(xtok[:, u], tokens[:, bass.ds(i * 4 + 2 * u, 2)]).then_inc(picked, 1)
                pool.wait_ge(picked, picks[0] + START)
                pool.sem_inc(pace, 1)
                for h in range(2):
                    g.indirect_dma_start(xg[:, u, h, :], None, xn_dram[:, :],
                                         bass.IndirectOffsetOnAxis(xtok[:, u, h:h + 1].bitcast(U32), 0),
                                         bounds_check=T - 1, oob_is_err=False).then_inc(x_loaded[u], 16)

            def add(i, u, last):
                if last is not None:
                    pool.wait_ge(y_added[1 - u], 32 * last)
                    pool.sem_inc(y_done[1 - u], 1)
                pool.wait_ge(y_ready[u], i + 1 + START)
                pool.sem_inc(pace, 1)
                g.tensor_copy(ytok[:, u], tokens[:, bass.ds(i * 4 + 2 * u, 2)]).then_inc(picked, 1)
                pool.wait_ge(picked, picks[0] + START)
                pool.sem_inc(pace, 1)
                for h in range(2):
                    g.indirect_dma_start(out[:, :], bass.IndirectOffsetOnAxis(ytok[:, u, h:h + 1].bitcast(U32), 0),
                                         y[:, u, h, :], None, bounds_check=T - 1, oob_is_err=False,
                                         compute_op=ALU.add).then_inc(y_added[u], 16)

            picks = [1]
            gather(0, 0)
            picks[0] = 2
            gather(0, 1)
            picks[0] = 3
            add(0, 0, None)
            with pool.Fori(0, HE - 1) as i:
                picks[0] = i * 4 + 4
                gather(i + 1, 0)
                picks[0] = i * 4 + 5
                add(i, 1, i + 1)
                picks[0] = i * 4 + 6
                gather(i + 1, 1)
                picks[0] = i * 4 + 7
                add(i + 1, 0, i + 1)
            picks[0] = 4 * HE
            add(HE - 1, 1, HE)
            pool.wait_ge(y_added[1], HE * 32)

        @block.tensor
        def _(pe):
            mm = nc.tensor.matmul
            pe.wait_ge(ident_loaded, 16 + START)
            pe.wait_ge(tab_loaded, 16 + START)
            for c in range(2):
                last = nc.tensor.transpose(px[c][0:HALF, 0, 0:2 * NE], tab[:, :, c], ident[0:2 * NE, 0:2 * NE])
            last.then_inc(tab_turned, 1)
            pe.wait_ge(tab_ready, 2 + START)

            def up(i, u):
                pe.wait_ge(xT_ready[1 - u], i + u + START)
                pe.wait_ge(x_loaded[u], i * 32 + 32)
                for c in range(NG):
                    for h in range(2):
                        last = nc.tensor.transpose(px[c // 2][:, c % 2, h * HALF:(h + 1) * HALF],
                                                   xg[:, u, h, c * P:(c + 1) * P], ident[0:HALF, 0:HALF])
                last.then_inc(x_full[u], 1)
                pe.wait_ge(xT_ready[u], i + 1 + START)
                pe.wait_ge(hT_ready[1 - u], i + u + START)
                pe.wait_ge(gu_loaded[u], i * 32 + 32 + START)
                for dst, w in ((pg, wg), (pu, wu)):
                    for k in range(NI):
                        for c in range(NG):
                            last = mm(dst[:, k, :], w[:, u, c, k * P:(k + 1) * P], xT[:, u, c, :],
                                      start=(c == 0), stop=(c == NG - 1))
                last.then_inc(gu_full[u], 1)

            def down(i, u):
                pe.wait_ge(y_ready[1 - u], i + u + START)
                pe.wait_ge(d_loaded[u], i * 16 + 16 + START)
                pe.wait_ge(hT_ready[u], i + 1 + START)
                for h in range(2):
                    for k in range(NI):
                        last = mm(py[h][0:HALF, :], hT[:, u, k, h * HALF:(h + 1) * HALF], wd[:, u, k, :],
                                  start=(k == 0), stop=(k == NI - 1))
                last.then_inc(y_full[u], 1)

            up(0, 0)
            with pe.Fori(0, HE - 1) as i:
                up(i, 1)
                down(i, 0)
                up(i + 1, 0)
                down(i, 1)
            up(HE - 1, 1)
            down(HE - 1, 0)
            down(HE - 1, 1)

        @block.scalar
        def _(act):
            A = nc.scalar.activation

            def silu(i, u):
                act.wait_ge(hT_ready[1 - u], i + u + START)
                act.wait_ge(gu_full[u], i + 1 + START)
                A(sg[:], pg[:], ACT.Silu).then_inc(sg_ready[u], 1)

            def scale(i, u):
                act.wait_ge(y_done[u], i + START)
                act.wait_ge(y_full[u], i + 1 + START)
                act.sem_inc(pace, 1)
                for h in range(2):
                    last = A(y[:, u, h, :], py[h][0:HALF, :], ACT.Copy, scale=weight[:, bass.ds(i * 4 + (2 * u + h), 1)])
                last.then_inc(y_ready[u], 1)

            act.wait_ge(tab_ready, 2 + START)
            silu(0, 0)
            with act.Fori(0, HE - 1) as i:
                silu(i, 1)
                scale(i, 0)
                silu(i + 1, 0)
                scale(i, 1)
            silu(HE - 1, 1)
            scale(HE - 1, 0)
            scale(HE - 1, 1)

        @block.vector
        def _(dve):
            v = nc.vector
            v.memset(xg[:], 0.0).then_inc(cleared, 1)
            dve.wait_ge(tab_turned, 1 + START)
            v.tensor_copy(tokens[:], px[0][0:HALF, 0, 0:2 * NE]).then_inc(tab_ready, 1)
            v.tensor_copy(weight[:], px[1][0:HALF, 0, 0:2 * NE]).then_inc(tab_ready, 1)

            def body(i, u):
                dve.wait_ge(gu_full[u], i + START)
                dve.wait_ge(x_full[u], i + 1 + START)
                for k in range(2):
                    last = v.tensor_copy(xT[:, u, 2 * k:2 * k + 2, :], px[k][:])
                last.then_inc(xT_ready[u], 1)
                dve.wait_ge(y_full[u], i + START)
                dve.wait_ge(sg_ready[u], i + 1 + START)
                v.tensor_tensor(hT[:, u], pu[:], sg[:], ALU.mult).then_inc(hT_ready[u], 1)

            with dve.Fori(0, HE) as i:
                for u in range(2):
                    body(i, u)


def build(nc, c_in, params, wqkvo, rope_tab, ident_in, identb_in, mask_in, headmask_in, rw_in, bias_in,
          tri_in, ones_in, iota_in, shared_w, gate_in, up_in, down_in, out):
    h_dram = nc.dram_tensor("h_dram", (T, D), F32, kind="Internal").ap()
    xn_dram = nc.dram_tensor("xn_dram", (T, D), F32, kind="Internal").ap()
    table = nc.dram_tensor("slot_table", (NE * CAP, 2), F32, kind="Internal").ap()
    state_space(nc, c_in, params, h_dram)
    with ExitStack() as ctx:
        sb = lambda name, shape, dt=F32: ctx.enter_context(nc.sbuf_tensor(name, shape, dt))
        res = sb("res", [P, 2 + NT, D])
        attention(nc, res, h_dram, wqkvo, rope_tab, ident_in, identb_in, mask_in, headmask_in)
        xT2 = sb("xT2", [P, NG, T])
        wk = sb("wk", [P, TOPK, NT, 2])
        slots = sb("slots", [P, TOPK, NT], I32)
        route(nc, res, xT2, wk, slots, rw_in, bias_in, ident_in, tri_in, ones_in, iota_in, xn_dram, table)
        shared_and_table(nc, res, xT2, wk, slots, shared_w, table, out)
    experts(nc, gate_in, up_in, down_in, ident_in, xn_dram, table, out)


def kernel(x, L0_tok_log_dt, L0_tok_B_ri, L0_tok_inv_A_real, L0_tok_A_imag, L0_attn_wq, L0_attn_wk, L0_attn_wv,
           L0_attn_wo, L0_ffn_router_w, L0_ffn_e_bias, L0_ffn_W_gate, L0_ffn_W_up, L0_ffn_W_down,
           L0_ffn_shared_gate, L0_ffn_shared_up, L0_ffn_shared_down):
    import ml_dtypes
    import concourse.bacc as bacc
    from concourse.bass_utils import run_bass_kernel_spmd

    bf = ml_dtypes.bfloat16
    x, log_dt, b_ri, a_re, a_im = (np.asarray(a) for a in (
        x, L0_tok_log_dt, L0_tok_B_ri, L0_tok_inv_A_real, L0_tok_A_imag))
    c_in = x.reshape(NB, NPAIR, 2, NSTATE, 2).transpose(2, 3, 1, 4, 0).reshape(P, NPAIR, 2, NB)
    pn = lambda a: a.reshape(NPAIR, 2, NSTATE).transpose(1, 2, 0).reshape(P, NPAIR)
    params = np.stack([pn(np.broadcast_to(log_dt[:, None], (S, NSTATE))), pn(a_re), pn(a_im),
                       pn(b_ri[..., 0]), pn(b_ri[..., 1])], 1)

    def lay(w):
        return w.reshape(w.shape[0] // P, P, w.shape[1]).transpose(1, 0, 2)

    pairs = (np.arange(NH)[:, None] * DH + np.concatenate([np.arange(0, DH, 2), np.arange(1, DH, 2)])).ravel()
    wqkvo = np.stack([lay(np.asarray(L0_attn_wq)[pairs].T), lay(np.asarray(L0_attn_wk)[pairs].T),
                      lay(np.asarray(L0_attn_wv).T), lay(np.asarray(L0_attn_wo).T)], 1)
    shared_w = np.stack([lay(np.asarray(a).T) for a in (L0_ffn_shared_gate, L0_ffn_shared_up, L0_ffn_shared_down)], 1)
    rw = lay(np.asarray(L0_ffn_router_w).T)
    ebias = np.broadcast_to(np.asarray(L0_ffn_e_bias), (P, NE))
    experts_lay = lambda w: np.asarray(w).reshape(NE, -1, P, w.shape[2]).transpose(2, 0, 1, 3)

    inv = (1.0 / 10000.0 ** (np.arange(0, DH, 2, dtype=np.float32) / np.float32(DH))).astype(np.float32)
    ang = np.outer(np.arange(S, dtype=np.float32), inv).astype(np.float32)
    cos, sin = np.cos(ang), np.sin(ang)
    rope = np.stack([np.concatenate([cos, cos], 1), np.concatenate([-sin, sin], 1)], 1)
    rope = rope.reshape(2, P, 2, DH).transpose(1, 0, 2, 3).astype(np.float32)
    ident = np.eye(P, dtype=np.float32)
    p = np.arange(P)
    mask = np.where(p[None, :] <= p[:, None], 0.0, -1e30).astype(bf)
    mask = np.broadcast_to(mask[:, None, :], (P, GH, P))
    headmask = (p[:, None] // DH == np.arange(GH)[None, :]).astype(np.float32)
    tri = (p[:, None] < p[None, :]).astype(bf)
    e = np.arange(NE, dtype=np.float32)
    iota = np.broadcast_to(np.stack([e - NE, e - NGRP, e * CAP]), (P, 3, NE))

    ins = {
        "c_in": c_in, "params": params, "wqkvo": wqkvo, "rope": rope, "ident": ident, "identb": ident.astype(bf),
        "mask": mask, "headmask": headmask, "rw": rw, "ebias": ebias, "tri": tri, "ones": np.ones((P, P), bf),
        "iota": iota, "shared_w": shared_w, "gate": experts_lay(L0_ffn_W_gate), "up": experts_lay(L0_ffn_W_up),
        "down": experts_lay(L0_ffn_W_down),
    }
    nc = bacc.Bacc("TRN2", target_bir_lowering=False, num_devices=1)
    arrays, args = {}, []
    for name, a in ins.items():
        a = np.ascontiguousarray(a)
        arrays[f"in_{name}"] = a
        args.append(nc.dram_tensor(f"in_{name}", a.shape, mybir.dt.from_np(a.dtype), kind="ExternalInput").ap())
    out = nc.dram_tensor("out_h", (T, D), F32, kind="ExternalOutput").ap()
    build(nc, *args, out)
    r = run_bass_kernel_spmd(nc, [arrays], core_ids=[0])
    return r.results[0]["out_h"].reshape(NB, S, D)
```

```python
import numpy as np
import concourse.bass as bass
from concourse import mybir
from contextlib import ExitStack

F32 = mybir.dt.float32
BF16 = mybir.dt.bfloat16
F32R = mybir.dt.float32r
I32 = mybir.dt.int32
U32 = mybir.dt.uint32
ALU = mybir.AluOpType
ACT = mybir.ActivationFunctionType
AX = mybir.AxisListType

P = 128
NB, S, D = 16, 256, 512
T = NB * S
NT = T // P
NSTATE = 64
NPAIR = S // 2
JG = 16
NCHUNK = NPAIR // JG
LO, NHI = 128, 4


START = 4


def semaphores(nc, ctx):
    made = []

    def sem(name):
        made.append(ctx.enter_context(nc.semaphore(name)))
        return made[-1]

    return sem, made


def start(eng, made):
    for s in made:
        eng.sem_inc(s, START)


class Chain:

    def __init__(self, eng, sem):
        self.eng, self.sem, self.base, self.n = eng, sem, 0, 0

    def did(self, ins):
        ins.then_inc(self.sem, 1)
        self.n += 1

    def wait(self):
        self.eng.wait_ge(self.sem, self.base + self.n + START)

    def step(self, ins):
        self.did(ins)
        self.wait()

    def enter(self, i, per):
        self.outer, self.per = self.base + self.n, per
        self.base, self.n = self.outer + i * per, 0

    def leave(self, trips):
        assert self.n == self.per, (self.n, self.per)
        self.base, self.n = self.outer + self.per * trips, 0


def state_space(nc, c_in, params, h_dram):
    with ExitStack() as ctx:
        sb = lambda name, shape, dt=F32: ctx.enter_context(nc.sbuf_tensor(name, shape, dt))
        sem, made = semaphores(nc, ctx)
        prm = sb("prm", [P, 5, NPAIR])
        dt_ = sb("dt_", [P, NPAIR])
        ear = sb("ear", [P, NPAIR])
        tmp = sb("tmp", [P, 8, NPAIR])
        scale = sb("scale", [P, 2, NPAIR])
        pw = sb("pw", [P, 8, 2, NPAIR])
        hop = sb("hop", [P, 2, 2, NPAIR])
        cin = sb("cin", [P, 2, JG, 2, NB])
        q = sb("q", [P, 2, 2, JG, LO])
        w = sb("w", [P, 2, 2, JG, NHI, NB])
        ta = sb("ta", [P, 2, JG, LO // 2])
        tb = sb("tb", [P, 2, JG, LO // 2])
        kout = sb("kout", [P, 2, JG, LO])
        ps = [ctx.enter_context(nc.psum_tensor(f"psk{i}", [P, 4, LO], F32)) for i in range(8)]
        prm_in, exps, dchain = sem("prm_in"), sem("exps"), sem("ssm_dve")
        c_loaded = [sem(f"c_loaded{u}") for u in range(2)]
        c_free = [sem(f"c_free{u}") for u in range(2)]
        qw_ready = [sem(f"qw_ready{u}") for u in range(2)]
        k_ready = [sem(f"k_ready{u}") for u in range(2)]
        kout_ready = [sem(f"kout_ready{u}") for u in range(2)]
        h_written = [sem(f"h_written{u}") for u in range(2)]
        pe_turns = sem("pe_turns")
        block = ctx.enter_context(nc.Block())

        @block.sync
        def _(sp):
            start(sp, made)
            sp.dma_start(prm[:, :, :], params[:, :, :]).then_inc(prm_in, 16)
            with sp.Fori(0, NCHUNK // 2) as i:
                for u in range(2):
                    sp.wait_ge(c_free[u], i + START)
                    sp.dma_start(cin[:, u], c_in[:, bass.ds(i * (2 * JG) + u * JG, JG), :, :]).then_inc(c_loaded[u], 16)

        @block.scalar
        def _(act):
            act.wait_ge(prm_in, 16 + START)
            nc.scalar.activation(dt_[:, :], prm[:, 0, :], ACT.Exp).then_inc(exps, 1)
            nc.scalar.activation(ear[:, :], prm[:, 1, :], ACT.Exp).then_inc(exps, 1)
            with act.Fori(0, NCHUNK // 2) as i:
                for u in range(2):
                    act.wait_ge(h_written[u], i * 128 + START)
                    for b in range(4):
                        act.wait_ge(k_ready[u], i * 4 + (b + 1) + START)
                        nc.scalar.activation(kout[:, u, 4 * b:4 * b + 4, :], ps[4 * u + b][:, :, :],
                                             ACT.Copy).then_inc(kout_ready[u], 1)
                    act.wait_ge(kout_ready[u], i * 4 + 4 + START)
                    for h2 in range(2):
                        for a in range(NHI):
                            p0 = h2 * 64 + a * NB
                            j0 = i * (2 * JG) + u * JG
                            dst = h_dram.rearrange("(c j e) d -> e c j d", c=NB, e=2)[
                                h2, :, bass.ds(j0, JG), a * LO:(a + 1) * LO]
                            act.dma_start(dst, kout[p0:p0 + NB, u, :, :]).then_inc(h_written[u], 16)
            for u in range(2):
                act.wait_ge(h_written[u], NCHUNK // 2 * 128 + START)

        @block.vector
        def _(dve):
            v = nc.vector
            ch = Chain(dve, dchain)
            TT = lambda o, a, b, op: ch.did(v.tensor_tensor(o, a, b, op))
            t = [tmp[:, k, :] for k in range(8)]
            dve.wait_ge(prm_in, 16 + START)
            dve.wait_ge(exps, 2 + START)
            ch.did(v.scalar_tensor_tensor(t[0], ear[:, :], -0.5, dt_[:, :], ALU.mult, ALU.mult))
            ch.did(v.scalar_tensor_tensor(t[1], prm[:, 2, :], 0.5, dt_[:, :], ALU.mult, ALU.mult))
            ch.wait()
            ch.did(v.tensor_scalar(t[2], t[0], -1.0, 1.0, ALU.mult, ALU.add))
            ch.did(v.tensor_scalar(t[3], t[0], 1.0, None, ALU.add))
            TT(t[4], t[1], t[1], ALU.mult)
            ch.wait()
            TT(t[5], t[2], t[2], ALU.mult)
            TT(t[3], t[3], t[2], ALU.mult)
            ch.wait()
            TT(t[5], t[5], t[4], ALU.add)
            TT(t[3], t[3], t[4], ALU.subtract)
            ch.wait()
            ch.step(v.reciprocal(t[5], t[5]))
            TT(pw[:, 0, 0, :], t[3], t[5], ALU.mult)
            ch.did(v.scalar_tensor_tensor(pw[:, 0, 1, :], t[1], -2.0, t[5], ALU.mult, ALU.mult))
            ch.did(v.scalar_tensor_tensor(t[5], t[5], 2.0, dt_[:, :], ALU.mult, ALU.mult))
            TT(t[6], prm[:, 3, :], t[2], ALU.mult)
            TT(t[7], prm[:, 4, :], t[1], ALU.mult)
            TT(t[0], prm[:, 3, :], t[1], ALU.mult)
            TT(t[2], prm[:, 4, :], t[2], ALU.mult)
            ch.wait()
            TT(t[6], t[6], t[7], ALU.subtract)
            TT(t[0], t[0], t[2], ALU.add)
            ch.wait()
            TT(scale[:, 0, :], t[6], t[5], ALU.mult)
            TT(scale[:, 1, :], t[0], t[5], ALU.mult)

            def square(dst, src):
                ch.wait()
                TT(t[0], src[:, 0, :], src[:, 0, :], ALU.mult)
                TT(t[1], src[:, 1, :], src[:, 1, :], ALU.mult)
                ch.did(v.scalar_tensor_tensor(dst[:, 1, :], src[:, 0, :], 2.0, src[:, 1, :], ALU.mult, ALU.mult))
                ch.wait()
                TT(dst[:, 0, :], t[0], t[1], ALU.subtract)

            for k in range(7):
                square(pw[:, k + 1], pw[:, k])
            square(hop[:, 0], pw[:, 6])
            ch.wait()
            ch.did(v.tensor_scalar(hop[:, 0, 1, :], hop[:, 0, 1, :], -1.0, None, ALU.mult))
            square(hop[:, 1], hop[:, 0])
            ch.wait()

            def times(dst, x, y, n):
                yr = y[:, 0:1, :].unsqueeze(3).to_broadcast([P, 2, JG, n])
                yi = y[:, 1:2, :].unsqueeze(3).to_broadcast([P, 2, JG, n])
                TT(ta[:, :, :, 0:n], x, yr, ALU.mult)
                TT(tb[:, :, :, 0:n], x, yi, ALU.mult)
                ch.wait()
                TT(dst[:, 0], ta[:, 0, :, 0:n], tb[:, 1, :, 0:n], ALU.subtract)
                TT(dst[:, 1], ta[:, 1, :, 0:n], tb[:, 0, :, 0:n], ALU.add)
                ch.wait()

            with dve.Fori(0, NCHUNK // 2) as i:
                ch.enter(i, 2 * 39)
                for u in range(2):
                    js = bass.ds(i * (2 * JG) + u * JG, JG)
                    dve.wait_ge(c_loaded[u], i * 16 + 16 + START)
                    dve.wait_ge(k_ready[u], i * 4 + START)
                    qu, wu = q[:, u], w[:, u].rearrange("p r j a c -> p r j (a c)")
                    ch.did(v.memset(qu[:, 0, :, 0:1], 1.0))
                    ch.did(v.memset(qu[:, 1, :, 0:1], 0.0))
                    ch.did(v.tensor_copy(qu[:, :, :, 1:2], pw[:, 0, :, js].unsqueeze(3)))
                    times(wu[:, :, :, 0:NB], cin[:, u].rearrange("p j r c -> p r j c"), scale[:, :, js], NB)
                    dve.sem_inc(c_free[u], 1)
                    times(wu[:, :, :, NB:2 * NB], wu[:, :, :, 0:NB], hop[:, 0, :, js], NB)
                    times(wu[:, :, :, 2 * NB:4 * NB], wu[:, :, :, 0:2 * NB], hop[:, 1, :, js], 2 * NB)
                    n = 2
                    for k in range(1, 7):
                        times(qu[:, :, :, n:2 * n], qu[:, :, :, 0:n], pw[:, k, :, js], n)
                        n *= 2
                    dve.sem_inc(qw_ready[u], 1)
                ch.leave(NCHUNK // 2)

        @block.tensor
        def _(pe):
            with pe.Fori(0, NCHUNK // 2) as i:
                for u in range(2):
                    pe.wait_ge(qw_ready[u], i + 1 + START)
                    pe.wait_ge(kout_ready[u], i * 4 + START)
                    pe.sem_inc(pe_turns, 1)
                    for b in range(4):
                        for j in range(4):
                            for h2 in range(2):
                                rows = slice(64 * h2, 64 * h2 + 64)
                                for r in range(2):
                                    last = nc.tensor.matmul(ps[4 * u + b][rows, j, :],
                                                            w[rows, u, r, 4 * b + j].rearrange("p a c -> p (a c)"),
                                                            q[rows, u, r, 4 * b + j], start=(r == 0), stop=(r == 1))
                        last.then_inc(k_ready[u], 1)


NH, DH = 16, 32
NG = D // P
GH = NH // NG
SCALE = float(DH) ** -0.5


def layernorm_stats(nc, ctx, name):
    sb = lambda n, shape: ctx.enter_context(nc.sbuf_tensor(name + n, shape, F32))
    return sb("_stat", [P, NT, 6]), sb("_mv", [P, NT, 2]), sb("_rstd", [P, NT])


def attention(nc, res, h_dram, wqkvo, rope_tab, ident_in, identb_in, mask_in, headmask_in):
    with ExitStack() as ctx:
        sb = lambda name, shape, dt=F32: ctx.enter_context(nc.sbuf_tensor(name, shape, dt))
        sem, made = semaphores(nc, ctx)
        w = sb("w_qkvo", [P, 4, NG, D])
        rope = sb("rope", [P, 2, 2, DH])
        ident = sb("ident", [P, P])
        identb = sb("identb", [P, P], BF16)
        maskb = sb("maskb", [P, GH, P], BF16)
        headmask = sb("headmask", [P, GH])
        ones = sb("ones", [P, DH])
        stat, mv, rstd = layernorm_stats(nc, ctx, "ln1")
        eps = sb("eps", [P, 1])
        xn = sb("xn", [P, 2, D])
        xT = sb("xT", [P, 2, NG, P])
        qk = sb("qk", [P, 4, D])
        rot = sb("rot", [P, 4, D])
        r1 = sb("r1", [P, 2, D])
        r2 = sb("r2", [P, 2, D])
        vnext = sb("vnext", [P, 2, D])
        vcur = sb("vcur", [P, 2, D])
        qT = sb("qT", [P, NG, S])
        kz = sb("kz", [P, NG, GH, S])
        nmax = sb("nmax", [P, 2, GH])
        nbias = sb("nbias", [P, 2, GH])
        p0 = sb("p0", [P, GH, P])
        p1 = sb("p1", [P, GH, S])
        pt0 = sb("pt0", [P, GH, S])
        pt1 = sb("pt1", [P, GH, P])
        rden = sb("rden", [P, S])
        oT = sb("oT", [P, NG, S])
        bank = lambda name, shape: ctx.enter_context(nc.psum_tensor(name, shape, F32))
        pj = [bank("pj0", [P, D]), bank("pj1", [P, D])]
        s0 = bank("s0", [P, GH, P])
        s1 = [bank("s1a", [P, 2, S]), bank("s1b", [P, 2, S])]
        pta, ptb = bank("pta", [P, GH, P]), bank("ptb", [P, GH, P])
        od = bank("od", [P, 2, S])

        loaded, h_in, ln_dve, rstd_ready = sem("loaded"), sem("h_in"), sem("attn_dve"), sem("rstd_ready")
        setup, sqrt_done = sem("setup"), sem("sqrt_done")
        xn_ready = sem("xn_ready")
        pj_full = [sem(f"pj_full{i}") for i in range(2)]
        pj_free = [sem(f"pj_free{i}") for i in range(2)]
        rot_ready, vcur_ready = sem("rot_ready"), sem("vcur_ready")
        s_full, bias_ready, p_ready = sem("s_full"), sem("bias_ready"), sem("p_ready")
        pta_full, ptb_full, pta_free, ptb_free = sem("pta_full"), sem("ptb_full"), sem("pta_free"), sem("ptb_free")
        od_full, oT_ready, pool_pace = sem("od_full"), sem("oT_ready"), sem("attn_pool_pace")
        block = ctx.enter_context(nc.Block())

        USES = ["O0", "O1", "xT0", "xT1", "q0", "q1", "k0", "k1", "v0", "v1", "qTa", "qTb", "kTa", "kTb"]
        LOOP = NB - 1

        class Turn:

            def __init__(self, kind, b):
                self.kind, self.b = kind, b

            def attends(self):
                return self.kind != "first"

            def projects(self):
                return self.kind != "last"

            def pj(self, use):
                n = USES.index(use)
                if self.kind == "first":
                    return n % 2, n // 2 - 1
                return n % 2, self.b * 7 + (6 + n // 2)

        def turns(eng, body, enter=None, leave=None):
            body(Turn("first", -1))
            with eng.Fori(0, LOOP) as i:
                if enter:
                    enter(i)
                body(Turn("loop", i))
                if leave:
                    leave()
            body(Turn("last", NB - 1))

        @block.sync
        def _(sp):
            start(sp, made)
            for k in range(4):
                sp.dma_start(w[:, k], wqkvo[:, k]).then_inc(loaded, 16)
            sp.dma_start(rope[:], rope_tab[:]).then_inc(loaded, 16)
            sp.dma_start(ident[:], ident_in[:]).then_inc(loaded, 16)
            sp.dma_start(identb[:], identb_in[:]).then_inc(loaded, 16)
            sp.dma_start(maskb[:], mask_in[:]).then_inc(loaded, 16)
            sp.dma_start(headmask[:], headmask_in[:]).then_inc(loaded, 16)

        @block.gpsimd
        def _(pool):
            def body(t):
                if t.projects():
                    for name in ("v0", "v1"):
                        n, before = t.pj(name)
                        pool.wait_ge(pj_free[n], before + 1 + START)
                    if t.attends():
                        pool.wait_ge(od_full, t.b * NG + NG + START)
                    pool.sem_inc(pool_pace, 1)
                    nc.gpsimd.tensor_copy(vcur[:], vnext[:]).then_inc(vcur_ready, 1)

            turns(pool, body)

        @block.scalar
        def _(act):
            for q in range(8):
                act.dma_start(res[:, 2 + 4 * q:6 + 4 * q, :],
                              h_dram.rearrange("(t p) d -> p t d", p=P)[:, 4 * q:4 * q + 4, :]).then_inc(h_in, 16)
            act.wait_ge(rstd_ready, 1 + START)
            nc.scalar.activation(rstd[:, :], mv[:, :, 1], ACT.Sqrt, bias=eps[:, :]).then_inc(sqrt_done, 1)

            nc.scalar.preload_act_table(ACT.Exp)

            def body(t):
                A = nc.scalar.activation
                G = lambda g: t.b * NG + g

                for g in range(NG):
                    if g == 1 and t.projects():
                        for u in range(2):
                            n, before = t.pj(f"xT{u}")
                            act.wait_ge(pj_full[n], before + 1 + START)
                            A(xT[:, u].rearrange("p c t -> p (c t)"), pj[n][:, :], ACT.Copy).then_inc(pj_free[n], 1)
                    if t.attends():
                        act.wait_ge(bias_ready, G(g) + 1 + START)
                        for h in range(GH):
                            last = A(p0[:, h, :], s0[:, h, :], ACT.Exp, bias=nbias[:, 0, h:h + 1], scale=SCALE)
                        last.then_inc(p_ready, 1)
                        for h in range(GH):
                            last = A(p1[:, h, :], s1[h // 2][:, h % 2, :], ACT.Exp, bias=nbias[:, 1, h:h + 1], scale=SCALE)
                        last.then_inc(p_ready, 1)
                    if t.projects():
                        for name in {1: ["q0", "q1"], 2: ["k0", "k1"], 3: ["v0", "v1"]}.get(g, []):
                            n, before = t.pj(name)
                            act.wait_ge(pj_full[n], before + 1 + START)
                            u = int(name[1])
                            dst = vnext[:, u] if name[0] == "v" else qk[:, 2 * (name[0] == "k") + u]
                            if name == "v0" and t.attends():
                                act.wait_ge(vcur_ready, t.b + 1 + START)
                            A(dst, pj[n][:, :], ACT.Copy).then_inc(pj_free[n], 1)
                        if g == 3:
                            for k, name in enumerate(["qTa", "qTb"]):
                                n, before = t.pj(name)
                                act.wait_ge(pj_full[n], before + 1 + START)
                                A(qT[:, 2 * k:2 * k + 2, :], pj[n][:, :], ACT.Copy).then_inc(pj_free[n], 1)
                    if t.attends():
                        act.wait_ge(pta_full, G(g) * 2 + 1 + START)
                        A(pt0[:, :, 0:P], pta[:], ACT.Copy).then_inc(pta_free, 1)
                        act.wait_ge(pta_full, G(g) * 2 + 2 + START)
                        A(pt1[:], pta[:], ACT.Copy).then_inc(pta_free, 1)

            turns(act, body)

        @block.vector
        def _(dve):
            v = nc.vector
            ch = Chain(dve, ln_dve)
            ch.did(v.memset(eps[:], 1e-5))
            ch.did(v.memset(ones[:], 1.0))
            ch.did(v.memset(oT[:], 0.0))
            ch.did(v.memset(res[:, 0:2, :], 0.0))
            for k in range(NT):
                if k % 4 == 0:
                    dve.wait_ge(h_in, 16 * 8 + START)
                ch.did(v.bn_stats(stat[:, k, :], res[:, 2 + k, :]))
            ch.wait()
            for k in range(NT):
                ch.did(v.bn_aggr(mv[:, k, :], stat[:, k, :]))
            ch.wait()
            dve.sem_inc(rstd_ready, 1)
            dve.wait_ge(sqrt_done, 1 + START)
            ch.step(v.reciprocal(rstd[:, :], rstd[:, :]))
            dve.wait_ge(loaded, 16 * 9 + START)
            dve.sem_inc(setup, 1)

            def body(t):
                G = lambda g: t.b * NG + g
                B1 = t.b + 1
                for g in range(NG):
                    if t.attends():
                        dve.wait_ge(s_full, G(g) + 1 + START)
                        ch.did(v.tensor_reduce(nmax[:, 0, :], s0[:], AX.X, ALU.max, negate=True))
                        for k in range(2):
                            ch.did(v.tensor_reduce(nmax[:, 1, 2 * k:2 * k + 2], s1[k][:], AX.X, ALU.max, negate=True))
                        ch.wait()
                        v.tensor_scalar(nbias[:], nmax[:], SCALE, None, ALU.mult).then_inc(bias_ready, 1)
                        if g == 0:
                            for u in range(2):
                                n, before = t.pj(f"O{u}")
                                dve.wait_ge(pj_full[n], before + 1 + START)
                                slot = res[:, bass.ds(t.b * 2 + u, 1), :] if t.kind == "loop" else res[:, t.b * 2 + u:t.b * 2 + u + 1, :]
                                v.tensor_tensor(slot, pj[n][:, :].unsqueeze(1), slot, ALU.add).then_inc(pj_free[n], 1)
                    if g == 0 and t.projects():
                        for u in range(2):
                            k = B1 * 2 + u
                            at = (lambda a: a[:, bass.ds(k, 1)]) if t.kind == "loop" else (lambda a: a[:, k:k + 1])
                            src = res[:, bass.ds(k + 2, 1), :] if t.kind == "loop" else res[:, k + 2:k + 3, :]
                            if t.attends():
                                n, before = t.pj(f"xT{u}")
                                dve.wait_ge(pj_full[n], before - 6 + START)
                            v.tensor_scalar(xn[:, u:u + 1, :], src, at(mv[:, :, 0]), at(rstd[:, :]),
                                            ALU.subtract, ALU.mult).then_inc(xn_ready, 1)
                    if g in (1, 2) and t.projects():
                        for u in range(2):
                            name = "qk"[g - 1] + str(u)
                            n, before = t.pj(name)
                            dve.wait_ge(pj_free[n], before + 1 + START)
                            k = 2 * (g - 1) + u
                            src = qk[:, k].rearrange("p (h e f) -> p h e f", h=NH, e=2)
                            cos = rope[:, u, 0:1, :].to_broadcast([P, NH, DH])
                            sn = rope[:, u, 1, :].rearrange("p (e f) -> p e f", e=2)
                            r1v = r1[:, u].rearrange("p (h f) -> p h f", h=NH)
                            r2v = r2[:, u].rearrange("p (h e f) -> p h e f", h=NH, e=2)
                            ch.did(v.tensor_tensor(r1v, qk[:, k].rearrange("p (h f) -> p h f", h=NH), cos, ALU.mult))
                            for e in range(2):
                                ch.did(v.tensor_tensor(r2v[:, :, e], src[:, :, 1 - e],
                                                       sn[:, e:e + 1, :].to_broadcast([P, NH, DH // 2]), ALU.mult))
                            ch.wait()
                            v.tensor_tensor(rot[:, k], r1[:, u], r2[:, u], ALU.add).then_inc(rot_ready, 1)
                    if g == 3 and t.projects():
                        for k, name in enumerate(["kTa", "kTb"]):
                            n, before = t.pj(name)
                            dve.wait_ge(pj_full[n], before + 1 + START)
                            for e in range(2):
                                src = pj[n][:, e * S:(e + 1) * S].unsqueeze(1).to_broadcast([P, GH, S])
                                last = v.tensor_tensor(kz[:, 2 * k + e], src,
                                                       headmask[:, :].unsqueeze(2).to_broadcast([P, GH, S]), ALU.mult)
                            last.then_inc(pj_free[n], 1)
                    if t.attends():
                        dve.wait_ge(ptb_full, G(g) + 1 + START)
                        v.tensor_copy(pt0[:, :, P:S], ptb[:]).then_inc(ptb_free, 1)
                        dve.wait_ge(od_full, G(g) + 1 + START)
                        ch.step(v.reciprocal(rden[:], od[:, 1, :]))
                        v.tensor_tensor(oT[:, g, :], od[:, 0, :], rden[:], ALU.mult).then_inc(oT_ready, 1)

            body(Turn("first", -1))
            with dve.Fori(0, LOOP) as i:
                ch.enter(i, NG * (3 + 1) + 4 * 3)
                body(Turn("loop", i))
                ch.leave(LOOP)
            body(Turn("last", NB - 1))
            dve.wait_ge(oT_ready, NB * NG + START)
            n, before = Turn("last", NB - 1).pj("O0")
            for u in range(2):
                dve.wait_ge(pj_full[u], before + 2 + START)
                slot = res[:, 2 * NB + u, :]
                v.tensor_tensor(slot, pj[u][:, :], slot, ALU.add).then_inc(pj_free[u], 1)
            for u in range(2):
                dve.wait_ge(pj_free[u], before + 2 + START)

        @block.tensor
        def _(pe):
            mm = nc.tensor.matmul
            pe.wait_ge(setup, 1 + START)

            def use(t, name):
                n, before = t.pj(name)
                pe.wait_ge(pj_free[n], before + START)
                return n

            def out_proj(n, u):
                for c in range(NG):
                    last = mm(pj[n][:, :], oT[:, c, u * P:(u + 1) * P], w[:, 3, c, :], start=(c == 0), stop=(c == NG - 1))
                last.then_inc(pj_full[n], 1)

            def body(t):
                G = lambda g: t.b * NG + g
                for g in range(NG):
                    if t.attends():
                        if g == 0:
                            n, before = t.pj("O0")
                            for n in range(2):
                                pe.wait_ge(pj_free[n], before + START)
                        mm(s0[:], qT[:, g, 0:P], kz[:, g, :, 0:P], start=True, stop=False)
                        for k in range(2):
                            mm(s1[k][:], qT[:, g, P:S], kz[:, g, 2 * k:2 * k + 2, :], start=True, stop=False)
                        mm(s0[:], identb[:], maskb[:], start=False, stop=True)
                        for k in range(2):
                            last = mm(s1[k][:, :, P:S], identb[:], maskb[:, 0:2, :], start=False, stop=True)
                        last.then_inc(s_full, 1)
                    if g == 0 and t.attends():
                        pe.wait_ge(oT_ready, t.b * NG + START)
                        for u in range(2):
                            out_proj(use(t, f"O{u}"), u)
                    if g == 1 and t.projects():
                        for u in range(2):
                            n = use(t, f"xT{u}")
                            pe.wait_ge(xn_ready, (t.b + 1) * 2 + (u + 1) + START)
                            for c in range(NG):
                                last = nc.tensor.transpose(pj[n][:, c * P:(c + 1) * P], xn[:, u, c * P:(c + 1) * P], ident[:])
                            last.then_inc(pj_full[n], 1)
                        for u in range(2):
                            n, before = t.pj(f"xT{u}")
                            pe.wait_ge(pj_free[n], before + 1 + START)
                    if g >= 1 and t.projects():
                        for u in range(2):
                            n = use(t, "qkv"[g - 1] + str(u))
                            for c in range(NG):
                                last = mm(pj[n][:, :], xT[:, u, c], w[:, g - 1, c, :], start=(c == 0), stop=(c == NG - 1))
                            last.then_inc(pj_full[n], 1)
                    if g == 3 and t.projects():
                        for k, name in enumerate(["qTa", "qTb", "kTa", "kTb"]):
                            n = use(t, name)
                            pe.wait_ge(rot_ready, (t.b + 1) * 4 + 2 + 2 * (k // 2) + START)
                            for e in range(2):
                                for u in range(2):
                                    c = 2 * (k % 2) + e
                                    last = nc.tensor.transpose(pj[n][:, e * S + u * P:e * S + (u + 1) * P],
                                                               rot[:, 2 * (k // 2) + u, c * P:(c + 1) * P], ident[:])
                            last.then_inc(pj_full[n], 1)
                    if t.attends():
                        pe.wait_ge(p_ready, G(g) * 2 + 1 + START)
                        pe.wait_ge(pta_free, G(g) * 2 + START)
                        for h in range(GH):
                            last = nc.tensor.transpose(pta[:, h, :], p0[:, h, :], ident[:])
                        last.then_inc(pta_full, 1)
                        pe.wait_ge(p_ready, G(g) * 2 + 2 + START)
                        pe.wait_ge(ptb_free, G(g) + START)
                        for h in range(GH):
                            last = nc.tensor.transpose(ptb[:, h, :], p1[:, h, 0:P], ident[:])
                        last.then_inc(ptb_full, 1)
                        pe.wait_ge(pta_free, G(g) * 2 + 1 + START)
                        for h in range(GH):
                            last = nc.tensor.transpose(pta[:, h, :], p1[:, h, P:S], ident[:])
                        last.then_inc(pta_full, 1)
                        if g == 0:
                            pe.wait_ge(vcur_ready, t.b + 1 + START)
                        pe.wait_ge(ptb_free, G(g) + 1 + START)
                        pe.wait_ge(oT_ready, G(g) + START)
                        for k in range(2):
                            if k == 1:
                                pe.wait_ge(pta_free, G(g) * 2 + 2 + START)
                            for h in range(GH):
                                rows = slice(32 * h, 32 * h + 32)
                                head = slice((g * GH + h) * DH, (g * GH + h + 1) * DH)
                                src = pt1[:, h, :] if k else pt0[:, h, :]
                                cols = slice(P, S) if k else slice(0, S)
                                mm(od[rows, 0, cols], vcur[:, k, head], src, start=(k == 0), stop=(k == 1), skip_group_check=True)
                                last = mm(od[rows, 1, cols], ones[:], src, start=False, stop=(k == 1), skip_group_check=True)
                        last.then_inc(od_full, 1)

            turns(pe, body)
            pe.wait_ge(oT_ready, NB * NG + START)
            n, before = Turn("last", NB - 1).pj("O0")
            for u in range(2):
                pe.wait_ge(pj_free[u], before + 1 + START)
                out_proj(u, u)


NE, NGRP, GE = 32, 8, 4
TOPG, TOPK = 3, 4
CAP = -(-5 * T // (4 * NE))
HALF = CAP // 2
DI = 256
ROUTE_SCALE = 2.5
PER_BLOCK = 82
FAR = 1 << 20


def feed_forward(nc, res, rw_in, bias_in, ident_in, tri_in, ones_in, iota_in, shared_w, xn_dram, table, out):
    TQ = 4
    TB = TQ * P
    NBLK = T // TB
    with ExitStack() as ctx:
        sb = lambda name, shape, dt=F32: ctx.enter_context(nc.sbuf_tensor(name, shape, dt))
        sem, made = semaphores(nc, ctx)
        rw = sb("rw", [P, NG, NE])
        rwh = sb("rwh", [P, NG, NE], F32R)
        rwl = sb("rwl", [P, NG, NE], F32R)
        bias = sb("bias", [P, NE])
        ident = sb("ident2", [P, P])
        tri = sb("tri", [P, P], BF16)
        ones = sb("ones2", [P, P], BF16)
        iota = sb("iota", [P, 3, NE])
        w = sb("w_shared", [P, 3, NG, D])
        wh = sb("wh_shared", [P, 3, NG, D], F32R)
        wl = sb("wl_shared", [P, 3, NG, D], F32R)
        stat, mv = sb("stat2", [P, TQ, 6]), sb("mv2", [P, TQ, 2])
        vare, half, rstd = sb("vare2", [P, TQ]), sb("half2", [P, TQ]), sb("rstd2", [P, TQ])
        xn = sb("xn2", [P, TQ, D])
        xh = sb("xh2", [P, NG, TB], F32R)
        xl = sb("xl2", [P, NG, TB], F32R)
        lgT = sb("lgT", [NE, TB])
        score = sb("score", [P, TQ, NE])
        sc = sb("sc", [P, TQ, NE])
        ga = sb("ga", [P, 4, TQ * NGRP])
        gs = sb("gs", [P, TQ, NGRP])
        gpick = sb("gpick", [P, 2, TQ, NGRP])
        gmask = sb("gmask", [P, TQ, NGRP])
        gcand = sb("gcand", [P, TQ, NGRP])
        best = sb("best", [P, 2, TQ])
        cand = sb("cand", [P, 2, TQ, NE])
        oh = sb("oh", [P, TOPK, TQ, NE])
        picked = sb("picked", [P, TQ, TOPK, NE])
        chosenb = sb("chosenb", [P, TQ, NE], BF16)
        place = sb("place", [P, TQ, NE])
        carry = sb("carry", [P, NE])
        wsel = sb("wsel", [P, TQ, TOPK])
        wsum = sb("wsum", [P, TQ])
        slotf = sb("slotf", [P, TQ, TOPK])
        slots = sb("slots", [P, TQ, TOPK], I32)
        tw = sb("tw", [P, TQ, TOPK, 2])
        tok = sb("tok", [P, NT + TQ], I32)
        empty = sb("empty", [P, 2 * NE * CAP // P])
        sg = sb("sg", [P, 2, TB])
        hf = sb("hf", [P, 2, TB])
        hh = sb("hh", [P, NG, TB], F32R)
        hl = sb("hl", [P, NG, TB], F32R)
        ys = sb("ys", [P, 2, D])
        bank = lambda name, shape: ctx.enter_context(nc.psum_tensor(name, shape, F32))
        tp = [bank("tp0", [P, TB]), bank("tp1", [P, TB])]
        pg = [bank(f"pg{u}", [P, TB]) for u in range(2)]
        pu = [bank(f"pu{u}", [P, TB]) for u in range(2)]
        py = [bank(f"py{u}", [P, D]) for u in range(2)]
        two = lambda name: [sem(f"{name}{u}") for u in range(2)]
        small_in, w_in, w_split, chain = sem("small_in"), [sem(f"w_in{k}") for k in range(3)], sem("w_split"), sem("ffn_dve")
        wh_done, pool_set, empty_out = sem("wh_done"), sem("pool_set"), sem("empty_out")
        mv_ready, rstd_ready, xn_ready, xn_stored = sem("mv_ready"), sem("rstd_ready"), sem("xn2_ready"), sem("xn2_stored")
        tp_full, tp_free, xh_ready = two("tp_full"), two("tp_free"), sem("xh_ready")
        lgT_ready, score_ready, chosen_ready = sem("lgT_ready"), sem("score_ready"), sem("chosen_ready")
        gu_full, sg_ready, h_ready, hf_ready, hh_ready = two("gu_full"), two("sg_ready"), sem("h_ready"), two("hf_ready"), sem("hh_ready")
        py_full, py_free, ys_free = two("py_full"), two("py_free"), two("ys_free")
        slots_ready, scattered, out_stored = sem("slots_ready"), sem("scattered"), sem("out_stored")
        pace_p, pace_d, pace_t = sem("ffn_pool_pace"), sem("ffn_dve_pace"), sem("ffn_pe_pace")
        slots_out = ctx.enter_context(nc.semaphore("slots_out"))
        block = ctx.enter_context(nc.Block())

        def turns(eng, body, enter=None, leave=None):
            body("first", -1)
            with eng.Fori(0, NBLK - 1) as i:
                if enter:
                    enter(i)
                body("loop", i)
                if leave:
                    leave()
            body("last", NBLK - 1)

        def tp_use(name, n):
            if name == "count":
                return 0, n * 4 + (3 if isinstance(n, int) else 6)
            k = ["x0", "x1", "x2", "x3", "lg", "lt"].index(name)
            if k % 2:
                return 1, n * 3 + k // 2
            return 0, k // 2 if isinstance(n, int) else n * 4 + (k // 2 - 1)

        @block.sync
        def _(sp):
            start(sp, made)
            for dst, src in ((ident, ident_in), (rw, rw_in), (bias, bias_in), (tri, tri_in), (ones, ones_in), (iota, iota_in)):
                sp.dma_start(dst[:], src[:]).then_inc(small_in, 16)
            for k in range(3):
                sp.dma_start(w[:, k], shared_w[:, k]).then_inc(w_in[k], 16)
            sp.wait_ge(pool_set, 2 + START)
            sp.dma_start(table.rearrange("(p s) c -> p (s c)", p=P), empty[:]).then_inc(empty_out, 16)
            xrows = xn_dram.rearrange("(t p) d -> p t d", p=P)
            rows = out.rearrange("(t p) d -> p t d", p=P)

            def body(kind, n):
                if kind != "last":
                    sp.wait_ge(xn_ready, (n + 1) * TQ + TQ + START)
                    dst = xrows[:, bass.ds(n * TQ + TQ, TQ), :] if kind == "loop" else xrows[:, 0:TQ, :]
                    sp.dma_start(dst, xn[:]).then_inc(xn_stored, 16)
                if kind != "first":
                    for u in range(2):
                        sp.wait_ge(ys_free[u], n * 2 + 2 + START)
                    at = bass.ds(n * TQ, TQ) if kind == "loop" else slice(n * TQ, n * TQ + TQ)
                    src = bass.ds(n * TQ + 2, TQ) if kind == "loop" else slice(n * TQ + 2, n * TQ + 2 + TQ)
                    sp.dma_start(rows[:, at, :], res[:, src, :]).then_inc(out_stored, 16)

            turns(sp, body)
            sp.wait_ge(xn_stored, 16 * NBLK + START)
            sp.wait_ge(out_stored, 16 * NBLK + START)
            sp.wait_ge(empty_out, 16 + START)

        @block.gpsimd
        def _(pool):
            g = nc.gpsimd
            ev = empty[:].rearrange("p (s c) -> p s c", c=2)
            g.memset(ev[:, :, 0], float(FAR)).then_inc(pool_set, 1)
            g.memset(ev[:, :, 1], 0.0).then_inc(pool_set, 1)
            g.memset(half[:], -0.5).then_inc(pool_set, 1)
            g.memset(slots[:], FAR).then_inc(pool_set, 1)
            g.memset(tw[:], 0.0).then_inc(pool_set, 1)
            g.iota(tok[:], [[P, NT + TQ]], base=-TB, channel_multiplier=1).then_inc(pool_set, 1)
            pool.wait_ge(pool_set, 6 + START)

            def scatter(kind, n, tks, before):
                pool.wait_ge(slots_ready, n + 1 + START)
                if kind == "loop":
                    pool.sem_inc(pace_p, 1)
                for k in range(TOPK):
                    g.tensor_copy(tw[:, :, k, 0], tks).then_inc(pool_set, 1)
                pool.wait_ge(pool_set, 6 + TOPK + before * TOPK + START)
                pool.sem_inc(pace_p, 1)
                pool.wait_ge(empty_out, 16 + START)
                for q in range(TQ):
                    for k in range(TOPK):
                        g.indirect_dma_start(
                            table[:, :], bass.IndirectOffsetOnAxis(slots[:, q, k:k + 1].bitcast(U32), 0),
                            tw[:, q, k, :], None, bounds_check=NE * CAP - 1, oob_is_err=False).then_inc(slots_out, 16)
                pool.wait_ge(slots_out, before * (16 * TQ * TOPK) + 16 * TQ * TOPK)
                pool.sem_inc(scattered, 1)

            def body(kind, n):
                if kind != "last":
                    pool.wait_ge(mv_ready, n + 2 + START)
                    pool.sem_inc(pace_p, 1)
                    g.tensor_tensor(rstd[:], vare[:], half[:], ALU.pow).then_inc(rstd_ready, 1)
                if kind != "first":
                    scatter(kind, n - 1, tok[:, bass.ds(n * TQ, TQ)] if kind == "loop" else tok[:, n * TQ:n * TQ + TQ], n)
                    for q in range(TQ):
                        u = q % 2
                        pool.wait_ge(py_free[u], n * 2 + (q // 2 + 1) + START)
                        pool.sem_inc(pace_p, 1)
                        at = bass.ds(n * TQ + (q + 2), 1) if kind == "loop" else slice(n * TQ + q + 2, n * TQ + q + 3)
                        g.tensor_tensor(res[:, at, :], ys[:, u:u + 1, :], res[:, at, :], ALU.add).then_inc(ys_free[u], 1)
                if kind == "last":
                    scatter(kind, n, tok[:, NT:NT + TQ], NBLK)

            turns(pool, body)

        @block.tensor
        def _(pe):
            mm = nc.tensor.matmul

            def exact(dst, terms):
                parts = [(a[x], b[y]) for a, b in terms for x, y in ((0, 0), (0, 1), (1, 0))]
                for m, (a, b) in enumerate(parts):
                    last = mm(dst, a, b, start=(m == 0), stop=(m == len(parts) - 1))
                return last

            def prepare(n, cs):
                pe.wait_ge(xn_ready, n * TQ + TQ + START)
                for c in cs:
                    b, before = tp_use(f"x{c}", n)
                    pe.wait_ge(tp_free[b], before + START)
                    for q in range(TQ):
                        last = nc.tensor.transpose(tp[b][:, q * P:(q + 1) * P], xn[:, q, c * P:(c + 1) * P], ident[:])
                    last.then_inc(tp_full[b], 1)

            def logits(n):
                b, before = tp_use("lg", n)
                pe.wait_ge(tp_free[b], before + START)
                pe.wait_ge(tp_free[1], tp_use("x3", n)[1] + 1 + START)
                exact(tp[b][0:NE, :], [((rwh[:, c, :], rwl[:, c, :]), (xh[:, c, :], xl[:, c, :])) for c in range(NG)]
                      ).then_inc(tp_full[b], 1)

            def scores(n):
                b, before = tp_use("lt", n)
                pe.wait_ge(tp_free[b], before + START)
                pe.wait_ge(lgT_ready, n + 1 + START)
                pe.sem_inc(pace_t, 1)
                for q in range(TQ):
                    last = nc.tensor.transpose(tp[b][:, q * NE:(q + 1) * NE], lgT[:, q * P:(q + 1) * P], ident[0:NE, 0:NE])
                last.then_inc(tp_full[b], 1)

            def count(n):
                b, before = tp_use("count", n)
                pe.wait_ge(chosen_ready, n + 1 + START)
                pe.wait_ge(tp_free[b], before + START)
                cnt = tp[b][:, 0:(TQ + 1) * NE].rearrange("p (q e) -> p q e", e=NE)
                for q in range(TQ):
                    mm(cnt[:, TQ, :], ones[:], chosenb[:, q, :], start=(q == 0), stop=(q == TQ - 1))
                mm(cnt[:, 0:TQ, :], tri[:], chosenb[:], start=True, stop=False, skip_group_check=True)
                for q in range(TQ - 1):
                    src = chosenb[:, q:q + 1, :].to_broadcast([P, TQ - 1 - q, NE])
                    last = mm(cnt[:, q + 1:TQ, :], ones[:], src, start=False, stop=(q == TQ - 2), skip_group_check=True)
                last.then_inc(tp_full[b], 1)

            def body(kind, n):
                if kind == "first":
                    prepare(0, range(NG))
                    pe.wait_ge(w_split, 1 + START)
                    logits(0)
                    scores(0)
                    return
                for f in range(NG):
                    u = f % 2
                    pe.wait_ge(hf_ready[u], n * 2 + f // 2 + START)
                    if kind == "loop" and f == 0 or kind == "last":
                        pe.wait_ge(w_split, 4 + START)
                    for dst, k in ((pg, 0), (pu, 1)):
                        cols = slice(f * P, (f + 1) * P)
                        last = exact(dst[u][:], [((wh[:, k, c, cols], wl[:, k, c, cols]), (xh[:, c, :], xl[:, c, :]))
                                                 for c in range(NG)])
                    last.then_inc(gu_full[u], 1)
                if kind == "loop":
                    prepare(n + 1, (0, 1))
                pe.wait_ge(h_ready, n * NG + NG + START)
                for q in range(TQ):
                    u = q % 2
                    if q == 1 and kind == "loop":
                        prepare(n + 1, (2, 3))
                    if q == 3:
                        if kind == "loop":
                            logits(n + 1)
                        count(n)
                    pe.wait_ge(py_free[u], n * 2 + q // 2 + START)
                    cols = slice(q * P, (q + 1) * P)
                    exact(py[u][:], [((hh[:, f, cols], hl[:, f, cols]), (wh[:, 2, f, :], wl[:, 2, f, :])) for f in range(NG)]
                          ).then_inc(py_full[u], 1)
                if kind == "loop":
                    scores(n + 1)

            pe.wait_ge(small_in, 96 + START)
            turns(pe, body)

        @block.scalar
        def _(act):
            A = nc.scalar.activation
            act.wait_ge(small_in, 96 + START)
            A(rwh[:], rw[:], ACT.Copy).then_inc(wh_done, 1)

            def split_high(k):
                act.wait_ge(w_in[k], 16 + START)
                A(wh[:, k], w[:, k], ACT.Copy).then_inc(wh_done, 1)

            def prepare(n, cs):
                for c in cs:
                    b, before = tp_use(f"x{c}", n)
                    act.wait_ge(tp_full[b], before + 1 + START)
                    A(xh[:, c, :], tp[b][:], ACT.Copy).then_inc(xh_ready, 1)

            def logits(n):
                b, before = tp_use("lg", n)
                act.wait_ge(tp_full[b], before + 1 + START)
                A(lgT[:], tp[b][0:NE, :], ACT.Copy).then_inc(lgT_ready, 1)
                act.wait_ge(lgT_ready, n + 1 + START)
                act.sem_inc(tp_free[b], 1)

            def scores(n):
                b, before = tp_use("lt", n)
                act.wait_ge(tp_full[b], before + 1 + START)
                A(score[:].rearrange("p q e -> p (q e)"), tp[b][:, 0:TQ * NE], ACT.Sigmoid).then_inc(score_ready, 1)
                act.wait_ge(score_ready, n + 1 + START)
                act.sem_inc(tp_free[b], 1)

            def body(kind, n):
                if kind == "first":
                    prepare(0, range(NG))
                    for k in range(3):
                        split_high(k)
                    logits(0)
                    scores(0)
                    return
                for f in range(NG):
                    u = f % 2
                    act.wait_ge(hf_ready[u], n * 2 + f // 2 + START)
                    act.wait_ge(gu_full[u], n * 2 + (f // 2 + 1) + START)
                    A(sg[:, u], pg[u][:], ACT.Silu).then_inc(sg_ready[u], 1)
                    act.wait_ge(hf_ready[u], n * 2 + (f // 2 + 1) + START)
                    A(hh[:, f], hf[:, u], ACT.Copy).then_inc(hh_ready, 1)
                for q in range(TQ):
                    u = q % 2
                    if q < 2 and kind == "loop":
                        prepare(n + 1, (2 * q, 2 * q + 1))
                    act.wait_ge(ys_free[u], n * 2 + q // 2 + START)
                    act.wait_ge(py_full[u], n * 2 + (q // 2 + 1) + START)
                    A(ys[:, u], py[u][:], ACT.Copy).then_inc(py_free[u], 1)
                    if q == 2 and kind == "loop":
                        logits(n + 1)
                if kind == "loop":
                    scores(n + 1)

            turns(act, body)

        @block.vector
        def _(dve):
            v = nc.vector
            ch = Chain(dve, chain)
            TT = lambda o, a, b, op: ch.did(v.tensor_tensor(o, a, b, op))
            along = lambda a, m: a.unsqueeze(2).to_broadcast([P, TQ, m])
            row = lambda k, m: iota[:, k:k + 1, 0:m].to_broadcast([P, TQ, m])

            def statistics(kind, n):
                for q in range(TQ):
                    at = bass.ds(n * TQ + (TQ + q + 2), 1) if kind == "loop" else slice(q + 2, q + 3)
                    ch.did(v.bn_stats(stat[:, q, :], res[:, at, :]))
                ch.wait()
                dve.sem_inc(pace_d, 1)
                for q in range(TQ):
                    ch.did(v.bn_aggr(mv[:, q, :], stat[:, q, :]))
                ch.wait()
                v.tensor_scalar(vare[:], mv[:, :, 1], 1e-5, None, ALU.add).then_inc(mv_ready, 1)

            def normalise(kind, n):
                dve.wait_ge(xn_stored, (n + 1) * 16 + START)
                dve.wait_ge(tp_full[1], tp_use("x3", n)[1] + 1 + START) if kind == "loop" else None
                dve.wait_ge(rstd_ready, n + 2 + START)
                for q in range(TQ):
                    at = bass.ds(n * TQ + (TQ + q + 2), 1) if kind == "loop" else slice(q + 2, q + 3)
                    v.tensor_scalar(xn[:, q:q + 1, :], res[:, at, :], mv[:, q, 0:1], rstd[:, q:q + 1],
                                    ALU.subtract, ALU.mult).then_inc(xn_ready, 1)

            def lower_x(n, cs):
                for c in cs:
                    b, before = tp_use(f"x{c}", n)
                    dve.wait_ge(xh_ready, n * NG + (c + 1) + START)
                    v.tensor_tensor(xl[:, c, :], tp[b][:], xh[:, c, :].bitcast(F32), ALU.subtract).then_inc(tp_free[b], 1)

            def first_best(cand_, best_, pick, values, k, m):
                ch.step(v.tensor_reduce(best_, values, AX.X, ALU.max))
                ch.step(v.tensor_tensor(cand_, values, along(best_, m), ALU.is_equal))
                ch.step(v.tensor_tensor(cand_, cand_, row(k, m), ALU.mult))
                ch.step(v.tensor_reduce(best_, cand_, AX.X, ALU.min))
                ch.step(v.tensor_tensor(pick, row(k, m), along(best_, m), ALU.is_equal))

            four = sc[:].rearrange("p t (g m) -> p (t g) m", m=GE)

            def score_groups(n):
                dve.wait_ge(score_ready, n + 1 + START)
                ch.step(v.tensor_tensor(sc[:], score[:], bias[:, :].unsqueeze(1).to_broadcast([P, TQ, NE]), ALU.add))
                TT(ga[:, 0], four[:, :, 0], four[:, :, 1], ALU.max)
                TT(ga[:, 1], four[:, :, 2], four[:, :, 3], ALU.max)
                TT(ga[:, 2], four[:, :, 0], four[:, :, 1], ALU.add)
                TT(ga[:, 3], four[:, :, 2], four[:, :, 3], ALU.add)
                ch.wait()
                gsf = gs[:].rearrange("p t g -> p (t g)")
                TT(gsf, ga[:, 0], ga[:, 1], ALU.add)
                TT(ga[:, 2], ga[:, 2], ga[:, 3], ALU.max)
                ch.wait()
                ch.step(v.tensor_tensor(gsf, gsf, ga[:, 2], ALU.max))

            def pick_groups(ks):
                for k in ks:
                    pick = gpick[:, k % 2] if k else gmask[:]
                    first_best(gcand[:], best[:, k % 2], pick, gs[:], 1, NGRP)
                    ch.did(v.scalar_tensor_tensor(gs[:], pick, -1e30, gs[:], ALU.mult, ALU.add))
                    if k:
                        TT(gmask[:], gmask[:], pick, ALU.add)
                    ch.wait()

            def keep_groups():
                ch.step(v.tensor_tensor(four, four, gmask[:].rearrange("p t g -> p (t g)").unsqueeze(2).to_broadcast(
                    [P, TQ * NGRP, GE]), ALU.mult))

            def pick_expert(k):
                ch.wait()
                first_best(cand[:, k % 2], best[:, k % 2], oh[:, k], sc[:], 0, NE)
                ch.did(v.scalar_tensor_tensor(sc[:], oh[:, k], -1e30, sc[:], ALU.mult, ALU.add))
                TT(picked[:, :, k, :], oh[:, k], score[:], ALU.mult)

            def weigh(n):
                ch.wait()
                TT(cand[:, 0], oh[:, 0], oh[:, 1], ALU.add)
                TT(cand[:, 1], oh[:, 2], oh[:, 3], ALU.add)
                ch.wait()
                ch.did(v.tensor_reduce(wsel[:], picked[:], AX.X, ALU.add))
                v.tensor_tensor(chosenb[:], cand[:, 0], cand[:, 1], ALU.add).then_inc(chosen_ready, 1)
                ch.wait()
                ch.step(v.tensor_reduce(wsum[:], wsel[:], AX.X, ALU.add))
                ch.step(v.tensor_scalar(wsum[:], wsum[:], 1e-20, None, ALU.add))
                ch.step(v.reciprocal(wsum[:], wsum[:]))
                dve.wait_ge(scattered, n + 1 + START)
                ch.step(v.tensor_tensor(wsel[:], wsel[:], wsum[:].unsqueeze(2).to_broadcast([P, TQ, TOPK]), ALU.mult))
                ch.did(v.tensor_scalar(tw[:, :, :, 1], wsel[:], ROUTE_SCALE, None, ALU.mult))

            def give_slots(n):
                b, before = tp_use("count", n)
                dve.wait_ge(tp_full[b], before + 1 + START)
                cnt = tp[b][:, 0:(TQ + 1) * NE].rearrange("p (q e) -> p q e", e=NE)
                ch.step(v.tensor_tensor(place[:], cnt[:, 0:TQ], carry[:].unsqueeze(1).to_broadcast([P, TQ, NE]), ALU.add))
                v.tensor_tensor(carry[:], cnt[:, TQ], carry[:], ALU.add).then_inc(tp_free[b], 1)
                ch.did(v.tensor_scalar(cand[:, 0], place[:], float(CAP), float(FAR), ALU.is_ge, ALU.mult))
                ch.step(v.tensor_tensor(place[:], place[:], row(2, NE), ALU.add))
                ch.step(v.tensor_tensor(place[:], place[:], cand[:, 0], ALU.add))
                for k in range(TOPK):
                    TT(picked[:, :, k, :], oh[:, k], place[:], ALU.mult)
                ch.wait()
                ch.step(v.tensor_reduce(slotf[:], picked[:], AX.X, ALU.add))
                v.tensor_copy(slots[:], slotf[:]).then_inc(slots_ready, 1)

            def hidden(n, f):
                u = f % 2
                dve.wait_ge(sg_ready[u], n * 2 + (f // 2 + 1) + START)
                v.tensor_tensor(hf[:, u], pu[u][:], sg[:, u], ALU.mult).then_inc(hf_ready[u], 1)

            def lower_h(n, f):
                dve.wait_ge(hh_ready, n * NG + (f + 1) + START)
                v.tensor_tensor(hl[:, f], hf[:, f % 2], hh[:, f].bitcast(F32), ALU.subtract).then_inc(h_ready, 1)

            def body(kind, n):
                if kind == "first":
                    statistics(kind, n)
                    normalise(kind, n)
                    dve.wait_ge(small_in, 96 + START)
                    dve.wait_ge(wh_done, 1 + START)
                    v.tensor_tensor(rwl[:], rw[:], rwh[:].bitcast(F32), ALU.subtract).then_inc(w_split, 1)
                    lower_x(0, range(NG))
                    for k in range(3):
                        dve.wait_ge(wh_done, k + 2 + START)
                        v.tensor_tensor(wl[:, k], w[:, k], wh[:, k].bitcast(F32), ALU.subtract).then_inc(w_split, 1)
                    return
                hidden(n, 0)
                if kind == "loop":
                    statistics(kind, n)
                score_groups(n)
                lower_h(n, 0)
                hidden(n, 1)
                pick_groups(range(0, 2))
                lower_h(n, 1)
                hidden(n, 2)
                if kind == "loop":
                    normalise(kind, n)
                pick_groups(range(2, TOPG))
                lower_h(n, 2)
                hidden(n, 3)
                keep_groups()
                lower_h(n, 3)
                if kind == "loop":
                    lower_x(n + 1, (0, 1))
                pick_expert(0)
                pick_expert(1)
                if kind == "loop":
                    lower_x(n + 1, (2, 3))
                pick_expert(2)
                pick_expert(3)
                weigh(n)
                give_slots(n)

            ch.did(v.memset(carry[:], 0.0))
            body("first", -1)
            with dve.Fori(0, NBLK - 1) as i:
                ch.enter(i, PER_BLOCK)
                body("loop", i)
                ch.leave(NBLK - 1)
            body("last", NBLK - 1)


def experts(nc, gate_in, up_in, down_in, ident_in, xn_dram, table, out):
    NI = DI // P
    R = 4
    with ExitStack() as ctx:
        sb = lambda name, shape, dt=F32: ctx.enter_context(nc.sbuf_tensor(name, shape, dt))
        sem, made = semaphores(nc, ctx)
        ident = sb("ident4", [P, P])
        wg = sb("wg", [P, R, NG, DI])
        wu = sb("wu", [P, R, NG, DI])
        wd = sb("wd", [P, R, NI, D])
        wdh = sb("wdh", [P, 2, NI, D], F32R)
        wdl = sb("wdl", [P, 2, NI, D], F32R)
        tab = sb("tab", [2 * NE, HALF, 2])
        tokens = sb("tokens", [HALF, 2 * NE], I32)
        weight = sb("weight", [HALF, 2 * NE])
        xtok = sb("xtok", [HALF, R, 2], I32)
        ytok = sb("ytok", [HALF, R, 2], I32)
        xg = sb("xg", [HALF, R, 2, D])
        xT = sb("xTe", [P, 2, NG, CAP])
        sg = sb("sge", [P, 2, NI, CAP])
        hf = sb("hfe", [P, 2, NI, CAP])
        hh = sb("hhe", [P, 2, NI, CAP], F32R)
        hl = sb("hle", [P, 2, NI, CAP], F32R)
        y = sb("y", [HALF, R, 2, D])
        bank = lambda name, shape: ctx.enter_context(nc.psum_tensor(name, shape, F32))
        px = [bank(f"px{k}", [P, 2, CAP]) for k in range(2)]
        pg = [bank(f"peg{k}", [P, NI, CAP]) for k in range(2)]
        pu = [bank(f"peu{k}", [P, NI, CAP]) for k in range(2)]
        py = [bank(f"pey{k}", [P, D]) for k in range(2)]
        ident_loaded, cleared = sem("ident_loaded"), sem("cleared")
        tab_loaded, tab_turned, tab_ready = sem("tab_loaded"), sem("tab_turned"), sem("tab_ready")
        gu_loaded, d_loaded = [[sem(f"{name}{k}") for k in range(R)] for name in ("gu_loaded", "d_loaded")]
        x_full, xT_ready, gu_full, sg_ready = sem("x_full"), sem("xT_ready"), sem("egu_full"), sem("esg_ready")
        hf_ready, hh_ready, h_ready = sem("ehf_ready"), sem("ehh_ready"), sem("eh_ready")
        wdh_ready, wd_ready = sem("wdh_ready"), sem("wd_ready")
        y_full, y_ready, y_done = sem("ey_full"), sem("ey_ready"), sem("ey_done")
        x_loaded, y_added = [[ctx.enter_context(nc.semaphore(f"{name}{k}")) for k in range(R)]
                             for name in ("x_loaded", "y_added")]
        xpicked, ypicked = sem("xpicked"), sem("ypicked")
        pace = sem("expert_pace")
        block = ctx.enter_context(nc.Block())

        class Expert:

            def __init__(self, i, c):
                self.i, self.c, self.n = i, c, i * R + c
                self.slot, self.turn = c % R, i + c // R
                self.half = c % 2

            def ahead(self, k):
                return Expert(self.i, self.c + k)

            def columns(self):
                return bass.ds(self.i * (2 * R) + 2 * self.c, 2)

        def each(eng, body, first, last):
            turns = (last - first) // R
            with eng.Fori(0, turns) as i:
                for k in range(R):
                    body(Expert(i, first + k))
            for c in range(first + turns * R, last):
                body(Expert(0, c))

        @block.sync
        def _(sp):
            start(sp, made)
            sp.dma_start(tab[:], table.rearrange("(g s) c -> g s c", s=HALF)).then_inc(tab_loaded, 16)
            sp.dma_start(ident[:], ident_in[:]).then_inc(ident_loaded, 16)

            def load(e):
                k, at = e.slot, bass.ds(e.n, 1)
                sp.wait_ge(gu_full, e.n - R + 1 + START)
                sp.dma_start(wg[:, k:k + 1], gate_in[:, at]).then_inc(gu_loaded[k], 16)
                sp.dma_start(wu[:, k:k + 1], up_in[:, at]).then_inc(gu_loaded[k], 16)
                sp.wait_ge(wd_ready, e.n - R + 1 + START)
                sp.dma_start(wd[:, k:k + 1], down_in[:, at]).then_inc(d_loaded[k], 16)

            each(sp, load, 0, NE)

        @block.gpsimd
        def _(pool):
            g = nc.gpsimd
            pool.wait_ge(cleared, 1 + START)
            pool.wait_ge(tab_ready, 2 + START)

            def gather(e):
                k = e.slot
                pool.wait_ge(x_full, e.n - R + 1 + START)
                pool.sem_inc(pace, 1)
                g.tensor_copy(xtok[:, k], tokens[:, e.columns()]).then_inc(xpicked, 1)
                pool.wait_ge(xpicked, e.n + 1 + START)
                pool.sem_inc(pace, 1)
                for h in range(2):
                    g.indirect_dma_start(xg[:, k, h, :], None, xn_dram[:, :],
                                         bass.IndirectOffsetOnAxis(xtok[:, k, h:h + 1].bitcast(U32), 0),
                                         bounds_check=T - 1, oob_is_err=False).then_inc(x_loaded[k], 16)

            def add(e, first=False):
                k = e.slot
                if not first:
                    last = e.ahead(-1)
                    pool.wait_ge(y_added[last.slot], last.turn * 32 + 32)
                    pool.sem_inc(y_done, 1)
                pool.wait_ge(y_ready, e.n + 1 + START)
                pool.sem_inc(pace, 1)
                g.tensor_copy(ytok[:, k], tokens[:, e.columns()]).then_inc(ypicked, 1)
                pool.wait_ge(ypicked, e.n + 1 + START)
                pool.sem_inc(pace, 1)
                for h in range(2):
                    g.indirect_dma_start(out[:, :], bass.IndirectOffsetOnAxis(ytok[:, k, h:h + 1].bitcast(U32), 0),
                                         y[:, k, h, :], None, bounds_check=T - 1, oob_is_err=False,
                                         compute_op=ALU.add).then_inc(y_added[k], 16)

            def both(e):
                gather(e.ahead(AHEAD))
                add(e)

            AHEAD = R - 1
            for c in range(AHEAD + 1):
                gather(Expert(0, c))
            add(Expert(0, 0), first=True)
            each(pool, both, 1, NE - AHEAD)
            for c in range(NE - AHEAD, NE):
                add(Expert(0, c))
            pool.wait_ge(y_added[R - 1], NE // R * 32)

        @block.tensor
        def _(pe):
            mm = nc.tensor.matmul
            pe.wait_ge(ident_loaded, 16 + START)
            pe.wait_ge(tab_loaded, 16 + START)
            for c in range(2):
                last = nc.tensor.transpose(px[c][0:HALF, 0, 0:2 * NE], tab[:, :, c], ident[0:2 * NE, 0:2 * NE])
            last.then_inc(tab_turned, 1)
            pe.wait_ge(tab_ready, 2 + START)

            def turn_x(e):
                pe.wait_ge(xT_ready, e.n + START)
                pe.wait_ge(x_loaded[e.slot], e.turn * 32 + 32)
                for c in range(NG):
                    for h in range(2):
                        last = nc.tensor.transpose(px[c // 2][:, c % 2, h * HALF:(h + 1) * HALF],
                                                   xg[:, e.slot, h, c * P:(c + 1) * P], ident[0:HALF, 0:HALF])
                last.then_inc(x_full, 1)

            def up(e):
                u = e.half
                pe.wait_ge(xT_ready, e.n + 1 + START)
                pe.wait_ge(hf_ready, e.n - 1 + START)
                pe.wait_ge(gu_loaded[e.slot], e.turn * 32 + 32 + START)
                for dst, w in ((pg[u], wg), (pu[u], wu)):
                    for k in range(NI):
                        for c in range(NG):
                            last = mm(dst[:, k, :], w[:, e.slot, c, k * P:(k + 1) * P], xT[:, u, c, :],
                                      start=(c == 0), stop=(c == NG - 1))
                last.then_inc(gu_full, 1)

            def down(e):
                u = e.half
                pe.wait_ge(y_ready, e.n + START)
                pe.wait_ge(wd_ready, e.n + 1 + START)
                pe.wait_ge(h_ready, e.n + 1 + START)
                for h in range(2):
                    cols = slice(h * HALF, (h + 1) * HALF)
                    parts = [(a[:, u, k, cols], b[:, u, k, :]) for k in range(NI)
                             for a, b in ((hh, wdh), (hh, wdl), (hl, wdh))]
                    for m, (a, b) in enumerate(parts):
                        last = mm(py[h][0:HALF, :], a, b, start=(m == 0), stop=(m == len(parts) - 1))
                last.then_inc(y_full, 1)

            def step(e):
                up(e)
                turn_x(e.ahead(1))
                down(e.ahead(-1))

            turn_x(Expert(0, 0))
            up(Expert(0, 0))
            turn_x(Expert(0, 1))
            each(pe, step, 1, NE - 1)
            up(Expert(0, NE - 1))
            down(Expert(0, NE - 2))
            down(Expert(0, NE - 1))

        @block.scalar
        def _(act):
            A = nc.scalar.activation

            def hidden(e):
                u = e.half
                act.wait_ge(y_full, e.n - 1 + START)
                act.wait_ge(d_loaded[e.slot], e.turn * 16 + 16 + START)
                A(wdh[:, u], wd[:, e.slot], ACT.Copy).then_inc(wdh_ready, 1)
                act.wait_ge(hf_ready, e.n - 1 + START)
                act.wait_ge(gu_full, e.n + 1 + START)
                A(sg[:, u], pg[u][:], ACT.Silu).then_inc(sg_ready, 1)
                act.wait_ge(hf_ready, e.n + 1 + START)
                A(hh[:, u], hf[:, u], ACT.Copy).then_inc(hh_ready, 1)

            def scale(e):
                act.wait_ge(y_done, e.n - R + 1 + START)
                act.wait_ge(y_full, e.n + 1 + START)
                act.sem_inc(pace, 1)
                for h in range(2):
                    last = A(y[:, e.slot, h, :], py[h][0:HALF, :], ACT.Copy,
                             scale=weight[:, bass.ds(e.i * (2 * R) + (2 * e.c + h), 1)])
                last.then_inc(y_ready, 1)

            def step(e):
                hidden(e)
                scale(e.ahead(-1))

            act.wait_ge(tab_ready, 2 + START)
            hidden(Expert(0, 0))
            each(act, step, 1, NE)
            scale(Expert(0, NE - 1))

        @block.vector
        def _(dve):
            v = nc.vector
            v.memset(xg[:], 0.0).then_inc(cleared, 1)
            dve.wait_ge(tab_turned, 1 + START)
            v.tensor_copy(tokens[:], px[0][0:HALF, 0, 0:2 * NE]).then_inc(tab_ready, 1)
            v.tensor_copy(weight[:], px[1][0:HALF, 0, 0:2 * NE]).then_inc(tab_ready, 1)

            def turn_x(e):
                dve.wait_ge(gu_full, e.n - 1 + START)
                dve.wait_ge(x_full, e.n + 1 + START)
                for k in range(2):
                    last = v.tensor_copy(xT[:, e.half, 2 * k:2 * k + 2, :], px[k][:])
                last.then_inc(xT_ready, 1)

            def body(e):
                u = e.half
                dve.wait_ge(wdh_ready, e.n + 1 + START)
                v.tensor_tensor(wdl[:, u], wd[:, e.slot], wdh[:, u].bitcast(F32), ALU.subtract).then_inc(wd_ready, 1)
                dve.wait_ge(sg_ready, e.n + 1 + START)
                v.tensor_tensor(hf[:, u], pu[u][:], sg[:, u], ALU.mult).then_inc(hf_ready, 1)
                dve.wait_ge(hh_ready, e.n + 1 + START)
                v.tensor_tensor(hl[:, u], hf[:, u], hh[:, u].bitcast(F32), ALU.subtract).then_inc(h_ready, 1)

            def step(e):
                body(e)
                turn_x(e.ahead(2))

            turn_x(Expert(0, 0))
            turn_x(Expert(0, 1))
            each(dve, step, 0, NE - 2)
            for c in (NE - 2, NE - 1):
                body(Expert(0, c))


def build(nc, c_in, params, wqkvo, rope_tab, ident_in, identb_in, mask_in, headmask_in, rw_in, bias_in,
          tri_in, ones_in, iota_in, shared_w, gate_in, up_in, down_in, out):
    h_dram = nc.dram_tensor("h_dram", (T, D), F32, kind="Internal").ap()
    xn_dram = nc.dram_tensor("xn_dram", (T, D), F32, kind="Internal").ap()
    table = nc.dram_tensor("slot_table", (NE * CAP, 2), F32, kind="Internal").ap()
    state_space(nc, c_in, params, h_dram)
    with ExitStack() as ctx:
        sb = lambda name, shape, dt=F32: ctx.enter_context(nc.sbuf_tensor(name, shape, dt))
        res = sb("res", [P, 2 + NT, D])
        attention(nc, res, h_dram, wqkvo, rope_tab, ident_in, identb_in, mask_in, headmask_in)
        feed_forward(nc, res, rw_in, bias_in, ident_in, tri_in, ones_in, iota_in, shared_w, xn_dram, table, out)
    experts(nc, gate_in, up_in, down_in, ident_in, xn_dram, table, out)


def kernel(x, L0_tok_log_dt, L0_tok_B_ri, L0_tok_inv_A_real, L0_tok_A_imag, L0_attn_wq, L0_attn_wk, L0_attn_wv,
           L0_attn_wo, L0_ffn_router_w, L0_ffn_e_bias, L0_ffn_W_gate, L0_ffn_W_up, L0_ffn_W_down,
           L0_ffn_shared_gate, L0_ffn_shared_up, L0_ffn_shared_down):
    import ml_dtypes
    import concourse.bacc as bacc
    from concourse.bass_utils import run_bass_kernel_spmd

    bf = ml_dtypes.bfloat16
    x, log_dt, b_ri, a_re, a_im = (np.asarray(a) for a in (
        x, L0_tok_log_dt, L0_tok_B_ri, L0_tok_inv_A_real, L0_tok_A_imag))
    c_in = x.reshape(NB, NPAIR, 2, NSTATE, 2).transpose(2, 3, 1, 4, 0).reshape(P, NPAIR, 2, NB)
    pn = lambda a: a.reshape(NPAIR, 2, NSTATE).transpose(1, 2, 0).reshape(P, NPAIR)
    params = np.stack([pn(np.broadcast_to(log_dt[:, None], (S, NSTATE))), pn(a_re), pn(a_im),
                       pn(b_ri[..., 0]), pn(b_ri[..., 1])], 1)

    def lay(w):
        return w.reshape(w.shape[0] // P, P, w.shape[1]).transpose(1, 0, 2)

    pairs = (np.arange(NH)[:, None] * DH + np.concatenate([np.arange(0, DH, 2), np.arange(1, DH, 2)])).ravel()
    wqkvo = np.stack([lay(np.asarray(L0_attn_wq)[pairs].T), lay(np.asarray(L0_attn_wk)[pairs].T),
                      lay(np.asarray(L0_attn_wv).T), lay(np.asarray(L0_attn_wo).T)], 1)
    shared_w = np.stack([lay(np.asarray(a).T) for a in (L0_ffn_shared_gate, L0_ffn_shared_up, L0_ffn_shared_down)], 1)
    rw = lay(np.asarray(L0_ffn_router_w).T)
    ebias = np.broadcast_to(np.asarray(L0_ffn_e_bias), (P, NE))
    experts_lay = lambda w: np.asarray(w).reshape(NE, -1, P, w.shape[2]).transpose(2, 0, 1, 3)

    inv = (1.0 / 10000.0 ** (np.arange(0, DH, 2, dtype=np.float32) / np.float32(DH))).astype(np.float32)
    ang = np.outer(np.arange(S, dtype=np.float32), inv).astype(np.float32)
    cos, sin = np.cos(ang), np.sin(ang)
    rope = np.stack([np.concatenate([cos, cos], 1), np.concatenate([-sin, sin], 1)], 1)
    rope = rope.reshape(2, P, 2, DH).transpose(1, 0, 2, 3).astype(np.float32)
    ident = np.eye(P, dtype=np.float32)
    p = np.arange(P)
    mask = np.where(p[None, :] <= p[:, None], 0.0, -1e30).astype(bf)
    mask = np.broadcast_to(mask[:, None, :], (P, GH, P))
    headmask = (p[:, None] // DH == np.arange(GH)[None, :]).astype(np.float32)
    tri = (p[:, None] < p[None, :]).astype(bf)
    e = np.arange(NE, dtype=np.float32)
    iota = np.broadcast_to(np.stack([e - NE, e - NGRP, e * CAP]), (P, 3, NE))

    ins = {
        "c_in": c_in, "params": params, "wqkvo": wqkvo, "rope": rope, "ident": ident, "identb": ident.astype(bf),
        "mask": mask, "headmask": headmask, "rw": rw, "ebias": ebias, "tri": tri, "ones": np.ones((P, P), bf),
        "iota": iota, "shared_w": shared_w, "gate": experts_lay(L0_ffn_W_gate), "up": experts_lay(L0_ffn_W_up),
        "down": experts_lay(L0_ffn_W_down),
    }
    nc = bacc.Bacc("TRN2", target_bir_lowering=False, num_devices=1)
    arrays, args = {}, []
    for name, a in ins.items():
        a = np.ascontiguousarray(a)
        arrays[f"in_{name}"] = a
        args.append(nc.dram_tensor(f"in_{name}", a.shape, mybir.dt.from_np(a.dtype), kind="ExternalInput").ap())
    out = nc.dram_tensor("out_h", (T, D), F32, kind="ExternalOutput").ap()
    build(nc, *args, out)
    r = run_bass_kernel_spmd(nc, [arrays], core_ids=[0])
    return r.results[0]["out_h"].reshape(NB, S, D)
```

```python
import numpy as np
import concourse.bass as bass
from concourse import mybir
from contextlib import ExitStack

F32 = mybir.dt.float32
BF16 = mybir.dt.bfloat16
F32R = mybir.dt.float32r
I32 = mybir.dt.int32
U32 = mybir.dt.uint32
ALU = mybir.AluOpType
ACT = mybir.ActivationFunctionType
AX = mybir.AxisListType

P = 128
NB, S, D = 16, 256, 512
T = NB * S
NT = T // P
NSTATE = 64
NPAIR = S // 2
JG = 16
NCHUNK = NPAIR // JG
LO, NHI = 128, 4


START = 4


def semaphores(nc, ctx):
    made = []

    def sem(name):
        made.append(ctx.enter_context(nc.semaphore(name)))
        return made[-1]

    return sem, made


def start(eng, made):
    for s in made:
        eng.sem_inc(s, START)


class Chain:

    def __init__(self, eng, sem):
        self.eng, self.sem, self.base, self.n = eng, sem, 0, 0

    def did(self, ins):
        ins.then_inc(self.sem, 1)
        self.n += 1

    def wait(self):
        self.eng.wait_ge(self.sem, self.base + self.n + START)

    def step(self, ins):
        self.did(ins)
        self.wait()

    def enter(self, i, per):
        self.outer, self.per = self.base + self.n, per
        self.base, self.n = self.outer + i * per, 0

    def leave(self, trips):
        assert self.n == self.per, (self.n, self.per)
        self.base, self.n = self.outer + self.per * trips, 0


def state_space(nc, c_in, params, h_dram):
    with ExitStack() as ctx:
        sb = lambda name, shape, dt=F32: ctx.enter_context(nc.sbuf_tensor(name, shape, dt))
        sem, made = semaphores(nc, ctx)
        prm = sb("prm", [P, 5, NPAIR])
        dt_ = sb("dt_", [P, NPAIR])
        ear = sb("ear", [P, NPAIR])
        tmp = sb("tmp", [P, 8, NPAIR])
        scale = sb("scale", [P, 2, NPAIR])
        pw = sb("pw", [P, 8, 2, NPAIR])
        hop = sb("hop", [P, 2, 2, NPAIR])
        cin = sb("cin", [P, 2, JG, 2, NB])
        q = sb("q", [P, 2, 2, JG, LO])
        w = sb("w", [P, 2, 2, JG, NHI, NB])
        ta = [sb(f"ta{e}", [P, 2, JG, n]) for e, n in enumerate((LO // 2, 2 * NB))]
        tb = [sb(f"tb{e}", [P, 2, JG, n]) for e, n in enumerate((LO // 2, 2 * NB))]
        kout = sb("kout", [P, 2, JG, LO])
        ps = [ctx.enter_context(nc.psum_tensor(f"psk{i}", [P, 4, LO], F32)) for i in range(8)]
        prm_in, exps, dchain = sem("prm_in"), sem("exps"), sem("ssm_dve")
        c_loaded = [sem(f"c_loaded{u}") for u in range(2)]
        c_free = [sem(f"c_free{u}") for u in range(2)]
        q_ready = [sem(f"q_ready{u}") for u in range(2)]
        w_ready = [sem(f"w_ready{u}") for u in range(2)]
        powers_ready, pchain = sem("powers_ready"), sem("ssm_pool")
        k_ready = [sem(f"k_ready{u}") for u in range(2)]
        kout_ready = [sem(f"kout_ready{u}") for u in range(2)]
        h_written = [sem(f"h_written{u}") for u in range(2)]
        pe_turns, pool_turns = sem("pe_turns"), sem("pool_turns")
        block = ctx.enter_context(nc.Block())

        def times(eng, ch, e, dst, x, y, n):
            yr = y[:, 0:1, :].unsqueeze(3).to_broadcast([P, 2, JG, n])
            yi = y[:, 1:2, :].unsqueeze(3).to_broadcast([P, 2, JG, n])
            a, b = ta[e][:, :, :, 0:n], tb[e][:, :, :, 0:n]
            ch.did(eng.tensor_tensor(a, x, yr, ALU.mult))
            ch.did(eng.tensor_tensor(b, x, yi, ALU.mult))
            ch.wait()
            if e:
                ch.eng.sem_inc(pool_turns, 1)
            ch.did(eng.tensor_tensor(dst[:, 0], a[:, 0], b[:, 1], ALU.subtract))
            ch.did(eng.tensor_tensor(dst[:, 1], a[:, 1], b[:, 0], ALU.add))
            ch.wait()
            if e:
                ch.eng.sem_inc(pool_turns, 1)

        @block.sync
        def _(sp):
            start(sp, made)
            sp.dma_start(prm[:, :, :], params[:, :, :]).then_inc(prm_in, 16)
            with sp.Fori(0, NCHUNK // 2) as i:
                for u in range(2):
                    sp.wait_ge(c_free[u], i + START)
                    sp.dma_start(cin[:, u], c_in[:, bass.ds(i * (2 * JG) + u * JG, JG), :, :]).then_inc(c_loaded[u], 16)

        @block.scalar
        def _(act):
            act.wait_ge(prm_in, 16 + START)
            nc.scalar.activation(dt_[:, :], prm[:, 0, :], ACT.Exp).then_inc(exps, 1)
            nc.scalar.activation(ear[:, :], prm[:, 1, :], ACT.Exp).then_inc(exps, 1)
            with act.Fori(0, NCHUNK // 2) as i:
                for u in range(2):
                    act.wait_ge(h_written[u], i * 128 + START)
                    for b in range(4):
                        act.wait_ge(k_ready[u], i * 4 + (b + 1) + START)
                        nc.scalar.activation(kout[:, u, 4 * b:4 * b + 4, :], ps[4 * u + b][:, :, :],
                                             ACT.Copy).then_inc(kout_ready[u], 1)
                    act.wait_ge(kout_ready[u], i * 4 + 4 + START)
                    for h2 in range(2):
                        for a in range(NHI):
                            p0 = h2 * 64 + a * NB
                            j0 = i * (2 * JG) + u * JG
                            dst = h_dram[0:T].rearrange("(c j e) d -> e c j d", c=NB, e=2)[
                                h2, :, bass.ds(j0, JG), a * LO:(a + 1) * LO]
                            act.dma_start(dst, kout[p0:p0 + NB, u, :, :]).then_inc(h_written[u], 16)
            for u in range(2):
                act.wait_ge(h_written[u], NCHUNK // 2 * 128 + START)

        @block.vector
        def _(dve):
            v = nc.vector
            ch = Chain(dve, dchain)
            TT = lambda o, a, b, op: ch.did(v.tensor_tensor(o, a, b, op))
            t = [tmp[:, k, :] for k in range(8)]
            dve.wait_ge(prm_in, 16 + START)
            dve.wait_ge(exps, 2 + START)
            ch.did(v.scalar_tensor_tensor(t[0], ear[:, :], -0.5, dt_[:, :], ALU.mult, ALU.mult))
            ch.did(v.scalar_tensor_tensor(t[1], prm[:, 2, :], 0.5, dt_[:, :], ALU.mult, ALU.mult))
            ch.wait()
            ch.did(v.tensor_scalar(t[2], t[0], -1.0, 1.0, ALU.mult, ALU.add))
            ch.did(v.tensor_scalar(t[3], t[0], 1.0, None, ALU.add))
            TT(t[4], t[1], t[1], ALU.mult)
            ch.wait()
            TT(t[5], t[2], t[2], ALU.mult)
            TT(t[3], t[3], t[2], ALU.mult)
            ch.wait()
            TT(t[5], t[5], t[4], ALU.add)
            TT(t[3], t[3], t[4], ALU.subtract)
            ch.wait()
            ch.step(v.reciprocal(t[5], t[5]))
            TT(pw[:, 0, 0, :], t[3], t[5], ALU.mult)
            ch.did(v.scalar_tensor_tensor(pw[:, 0, 1, :], t[1], -2.0, t[5], ALU.mult, ALU.mult))
            ch.did(v.scalar_tensor_tensor(t[5], t[5], 2.0, dt_[:, :], ALU.mult, ALU.mult))
            TT(t[6], prm[:, 3, :], t[2], ALU.mult)
            TT(t[7], prm[:, 4, :], t[1], ALU.mult)
            TT(t[0], prm[:, 3, :], t[1], ALU.mult)
            TT(t[2], prm[:, 4, :], t[2], ALU.mult)
            ch.wait()
            TT(t[6], t[6], t[7], ALU.subtract)
            TT(t[0], t[0], t[2], ALU.add)
            ch.wait()
            TT(scale[:, 0, :], t[6], t[5], ALU.mult)
            TT(scale[:, 1, :], t[0], t[5], ALU.mult)

            def square(dst, src):
                ch.wait()
                TT(t[0], src[:, 0, :], src[:, 0, :], ALU.mult)
                TT(t[1], src[:, 1, :], src[:, 1, :], ALU.mult)
                ch.did(v.scalar_tensor_tensor(dst[:, 1, :], src[:, 0, :], 2.0, src[:, 1, :], ALU.mult, ALU.mult))
                ch.wait()
                TT(dst[:, 0, :], t[0], t[1], ALU.subtract)

            for k in range(7):
                square(pw[:, k + 1], pw[:, k])
            square(hop[:, 0], pw[:, 6])
            ch.wait()
            ch.did(v.tensor_scalar(hop[:, 0, 1, :], hop[:, 0, 1, :], -1.0, None, ALU.mult))
            square(hop[:, 1], hop[:, 0])
            ch.wait()

            dve.sem_inc(powers_ready, 1)

            with dve.Fori(0, NCHUNK // 2) as i:
                ch.enter(i, 2 * (3 + 6 * 4))
                for u in range(2):
                    js = bass.ds(i * (2 * JG) + u * JG, JG)
                    dve.wait_ge(k_ready[u], i * 4 + START)
                    qu = q[:, u]
                    ch.did(v.memset(qu[:, 0, :, 0:1], 1.0))
                    ch.did(v.memset(qu[:, 1, :, 0:1], 0.0))
                    ch.did(v.tensor_copy(qu[:, :, :, 1:2], pw[:, 0, :, js].unsqueeze(3)))
                    ch.wait()
                    n = 2
                    for k in range(1, 7):
                        times(v, ch, 0, qu[:, :, :, n:2 * n], qu[:, :, :, 0:n], pw[:, k, :, js], n)
                        n *= 2
                    dve.sem_inc(q_ready[u], 1)
                ch.leave(NCHUNK // 2)

        @block.gpsimd
        def _(pool):
            g = nc.gpsimd
            ch = Chain(pool, pchain)
            pool.wait_ge(powers_ready, 1 + START)
            with pool.Fori(0, NCHUNK // 2) as i:
                ch.enter(i, 2 * 3 * 4)
                for u in range(2):
                    js = bass.ds(i * (2 * JG) + u * JG, JG)
                    pool.wait_ge(c_loaded[u], i * 16 + 16 + START)
                    pool.wait_ge(k_ready[u], i * 4 + START)
                    pool.sem_inc(pool_turns, 1)
                    wu = w[:, u].rearrange("p r j a c -> p r j (a c)")
                    times(g, ch, 1, wu[:, :, :, 0:NB], cin[:, u].rearrange("p j r c -> p r j c"), scale[:, :, js], NB)
                    pool.sem_inc(c_free[u], 1)
                    times(g, ch, 1, wu[:, :, :, NB:2 * NB], wu[:, :, :, 0:NB], hop[:, 0, :, js], NB)
                    times(g, ch, 1, wu[:, :, :, 2 * NB:4 * NB], wu[:, :, :, 0:2 * NB], hop[:, 1, :, js], 2 * NB)
                    pool.sem_inc(w_ready[u], 1)
                ch.leave(NCHUNK // 2)

        @block.tensor
        def _(pe):
            with pe.Fori(0, NCHUNK // 2) as i:
                for u in range(2):
                    pe.wait_ge(q_ready[u], i + 1 + START)
                    pe.wait_ge(w_ready[u], i + 1 + START)
                    pe.wait_ge(kout_ready[u], i * 4 + START)
                    pe.sem_inc(pe_turns, 1)
                    for b in range(4):
                        for j in range(4):
                            for h2 in range(2):
                                rows = slice(64 * h2, 64 * h2 + 64)
                                for r in range(2):
                                    last = nc.tensor.matmul(ps[4 * u + b][rows, j, :],
                                                            w[rows, u, r, 4 * b + j].rearrange("p a c -> p (a c)"),
                                                            q[rows, u, r, 4 * b + j], start=(r == 0), stop=(r == 1))
                        last.then_inc(k_ready[u], 1)


NH, DH = 16, 32
NG = D // P
GH = NH // NG
SCALE = float(DH) ** -0.5


PER_TWO = 48


def attention(nc, h_dram, wqkvo, rope_tab, ident_in, identb_in, mask_in, h2_dram):
    with ExitStack() as ctx:
        sb = lambda name, shape, dt=F32: ctx.enter_context(nc.sbuf_tensor(name, shape, dt))
        sem, made = semaphores(nc, ctx)
        wh = sb("wh_qkvo", [P, 4, NG, D], F32R)
        wl = sb("wl_qkvo", [P, 4, NG, D], F32R)
        raw = sb("raw", [P, 2, GH, NG, S])
        stack = sb("stack", [P, 2, NG, GH, S], F32R)
        rope = sb("rope", [P, 2, 2, 2, DH])
        ident = sb("ident", [P, P])
        identb = sb("identb", [P, P], BF16)
        maskb = sb("maskb", [P, GH, P], BF16)
        half = sb("half1", [P, 2])
        stat, mv = sb("stat1", [P, 2, 6]), sb("mv1", [P, 2, 2])
        vare, rstd = sb("vare1", [P, 2]), sb("rstd1", [P, 2])
        x = sb("x", [P, 2, D])
        hres = sb("hres", [P, 2, D])
        xh = sb("xh", [P, 2, NG, P], F32R)
        xl = sb("xl", [P, 2, NG, P], F32R)
        r1, r2 = sb("r1", [P, D]), sb("r2", [P, D])
        rot = sb("rot", [P, 4, D])
        th = sb("th", [P, 2, NG, S], F32R)
        tl = sb("tl", [P, 2, NG, S])
        vv = sb("vv", [P, 2, 2, D])
        nbias = sb("nbias", [P, 2, GH])
        den, rden = sb("den", [P, 2, GH]), sb("rden", [P, 2, GH])
        p0 = sb("p0", [P, GH, P])
        p1 = sb("p1", [P, GH, S])
        pt0 = sb("pt0", [P, GH, S])
        pt1 = sb("pt1", [P, GH, P])
        oh = sb("oh_attn", [P, NG, S], F32R)
        ol = sb("ol_attn", [P, NG, S], F32R)
        bank = lambda name, shape: ctx.enter_context(nc.psum_tensor(name, shape, F32))
        pj = [bank("pj0", [P, D]), bank("pj1", [P, D])]
        s0 = bank("s0", [P, GH, P])
        s1 = [bank("s1a", [P, 2, S]), bank("s1b", [P, 2, S])]
        pta, ptb = bank("pta", [P, GH, P]), bank("ptb", [P, GH, P])
        od = bank("od", [P, S])

        w_loaded, loaded, chain = [sem(f"w_loaded{k}") for k in range(4)], sem("loaded"), sem("attn_dve")
        wh_ready, w_ready, half_set = sem("wh_ready"), sem("w_ready"), sem("half_set")
        mv_ready, rstd_ready, xn_ready, xh_ready = sem("mv1_ready"), sem("rstd1_ready"), sem("xn_ready"), sem("xh1_ready")
        pj_full = [sem(f"pj_full{i}") for i in range(2)]
        pj_free = [sem(f"pj_free{i}") for i in range(2)]
        rot_ready, th_ready, stacked = sem("rot_ready"), sem("th_ready"), sem("stacked")
        act_copied, dve_copied, pool_copied = sem("act_copied"), sem("dve_copied"), sem("pool_copied")
        s_full, bias_ready = sem("s_full"), sem("bias_ready")
        exp_done, p_ready = sem("exp_done"), sem("p_ready")
        pta_full, ptb_full, pta_free, ptb_free = sem("pta_full"), sem("ptb_full"), sem("pta_free"), sem("ptb_free")
        od_full, oh_ready, ol_ready = sem("od_full"), sem("oh_ready"), sem("ol_ready")
        hres_loaded, h2_stored = sem("hres_loaded"), sem("h2_stored")
        pace_d, pace_p, pace_s, pace_a = [sem(f"attn_{name}_pace") for name in ("dve", "pool", "sp", "act")]
        x_loaded, zeros_stored, low_stacked = [ctx.enter_context(nc.semaphore(name)) for name in (
            "x1_loaded", "zeros_stored", "low_stacked")]
        block = ctx.enter_context(nc.Block())

        HEADS = (range(GH), range(0, 2), range(2, GH))
        USES = ["xT0", "xT1", "O0", "O1", "q0", "q1", "k0", "qTa", "qTb", "k1", "kTa", "kTb", "v0", "v1"]

        class Turn:

            def __init__(self, b, parity):
                self.b, self.mine, self.other = b, parity, 1 - parity
                fixed = isinstance(b, int)
                self.first, self.last = fixed and b < 0, fixed and b == NB - 1
                self.attends = not (fixed and b < 0)
                self.projects = not (fixed and b == NB - 1)
                self.outputs = not (fixed and b < 1)

            def pj(self, use):
                n = USES.index(use)
                if self.last:
                    return n % 2, NB * 7 - 2
                if self.first:
                    return n % 2, max(n // 2 - 1, 0)
                if not self.outputs:
                    return n % 2, 5 + max(n // 2, 1)
                return n % 2, self.b * 7 + (5 + n // 2)

        LAST = NB * 7 - 1

        def turns(eng, body, ch=None):
            body(Turn(-1, 1))
            body(Turn(0, 0))
            with eng.Fori(0, NB // 2 - 1) as i:
                if ch:
                    ch.enter(i, PER_TWO)
                body(Turn(i * 2 + 1, 1))
                body(Turn(i * 2 + 2, 0))
                if ch:
                    ch.leave(NB // 2 - 1)
            body(Turn(NB - 1, 1))

        batch = lambda dram, b: dram.rearrange("(t p) d -> p t d", p=P)[
            :, slice(2 * b, 2 * b + 2) if isinstance(b, int) else bass.ds(b * 2, 2), :]

        staged = lambda k: raw[:, k // 2, 2 * (k % 2):2 * (k % 2) + 2].rearrange("p a c s -> p (a c s)")

        @block.sync
        def _(sp):
            start(sp, made)
            for dst, src in ((ident, ident_in), (rope, rope_tab), (identb, identb_in), (maskb, mask_in)):
                sp.dma_start(dst[:], src[:]).then_inc(loaded, 16)
            for k in range(4):
                if k == 1:
                    sp.wait_ge(x_loaded, 16)
                sp.dma_start(staged(k), wqkvo[:, k].rearrange("p c d -> p (c d)")).then_inc(w_loaded[k], 16)

            def fill(t, k):
                if k == 0:
                    sp.wait_ge(pool_copied, (t.b + 1) * 4 + START)
                    sp.sem_inc(pace_s, 1)
                    if t.first:
                        sp.wait_ge(w_ready, 4 + START)

                sp.wait_ge(th_ready, (t.b + 1) * 4 + 2 * k + 2 + START)
                sp.sem_inc(pace_s, 1)
                for part in (0, 2) if k else (0, 1):
                    for h in range(GH):
                        sp.dma_start(raw[part * DH:(part + 1) * DH, k, h], th[h * DH:(h + 1) * DH, k].bitcast(F32)
                                     ).then_inc(stacked, 16)

            def store(b, added):
                for n in range(2):
                    sp.wait_ge(pj_free[n], added + START)
                    sp.sem_inc(pace_s, 1)
                sp.dma_start(batch(h2_dram, b), hres[:]).then_inc(h2_stored, 16)

            def body(t):
                if t.outputs:
                    store(t.b - 1, t.pj("O0")[1] + 1)
                if t.projects:
                    fill(t, 0)
                if t.first:
                    sp.wait_ge(zeros_stored, 16)
                if t.attends:
                    sp.wait_ge(h2_stored, t.b * 16 + START)
                    sp.sem_inc(pace_s, 1)
                    sp.dma_start(hres[:], batch(h_dram, t.b)).then_inc(hres_loaded, 16)
                if t.projects:
                    fill(t, 1)

            turns(sp, body)
            store(NB - 1, LAST + 1)
            sp.wait_ge(h2_stored, NB * 16 + START)

        def rounded(copy, eng, t, k, g, done, pace):
            if g in (0, 2):
                eng.wait_ge(low_stacked, (t.b + 1) * (2 * GH * 16))
                eng.sem_inc(pace, 1)
                eng.wait_ge(stacked, (t.b + 1) * (4 * GH * 16) + START)
                eng.sem_inc(pace, 1)
            copy(stack[0:3 * DH, k, g], raw[0:3 * DH, k, :, g]).then_inc(done, 1)

        @block.gpsimd
        def _(pool):
            g = nc.gpsimd
            g.memset(half[:], -0.5).then_inc(half_set, 1)
            pool.wait_ge(half_set, 1 + START)

            def load(b):
                g.dma_start(x[:], batch(h_dram, b)).then_inc(x_loaded, 16)

            def deviate(b):
                pool.wait_ge(mv_ready, b + 1 + START)
                g.tensor_tensor(rstd[:], vare[:], half[:], ALU.pow).then_inc(rstd_ready, 1)

            def copies(t):
                pool.wait_ge(s_full, t.b * (NG * 3) + START)
                pool.sem_inc(pace_p, 1)
                for n in (2, 3):
                    for k in range(2):
                        rounded(g.tensor_copy, pool, t, k, n, pool_copied, pace_p)

            def body(t):
                if t.projects:
                    n, before = t.pj("xT1")
                    pool.wait_ge(pj_full[n], before + 1 + START)
                    pool.sem_inc(pace_p, 1)
                    load(t.b + 2)
                if t.attends:
                    copies(t)
                if t.projects:
                    deviate(t.b + 2)
                    pool.wait_ge(pool_copied, (t.b + 1) * 4 + START)
                    pool.sem_inc(pace_p, 1)
                    if t.first:
                        pool.wait_ge(w_ready, 4 + START)
                    for k, part in enumerate((2, 1)):
                        for name in ("kTa", "kTb") if k else ("qTa", "qTb"):
                            n, before = t.pj(name)
                            pool.wait_ge(pj_free[n], before + 1 + START)
                            pool.sem_inc(pace_p, 1)
                        for h in range(GH):
                            g.dma_start(raw[part * DH:(part + 1) * DH, k, h], tl[h * DH:(h + 1) * DH, k]
                                        ).then_inc(low_stacked, 16)

            load(0)
            g.memset(hres[:], 0.0).then_inc(half_set, 1)
            pool.wait_ge(half_set, 2 + START)
            g.dma_start(batch(h_dram, NB), hres[:]).then_inc(zeros_stored, 16)
            deviate(0)
            pool.wait_ge(zeros_stored, 16)

            turns(pool, body)

        @block.scalar
        def _(act):
            A = nc.scalar.activation
            nc.scalar.preload_act_table(ACT.Exp)

            def copy(t, name, dst, done):
                n, before = t.pj(name)
                act.wait_ge(pj_full[n], before + 1 + START)
                A(dst, pj[n][:], ACT.Copy).then_inc(pj_free[n] if done is None else done, 1)

            def exps(G, part):
                act.wait_ge(bias_ready, G * 3 + part + 1 + START)
                u = min(part, 1)
                for h in HEADS[part]:
                    src, dst = (s1[h // 2][:, h % 2, :], p1[:, h, :]) if u else (s0[:, h, :], p0[:, h, :])
                    last = A(dst, src, ACT.Exp, bias=nbias[:, u, h:h + 1], accum_out=den[:, u, h:h + 1])
                last.then_inc(exp_done, 1)

            def split_out(G, g):
                act.wait_ge(od_full, G + 1 + START)
                A(oh[:, g], od[:], ACT.Copy).then_inc(oh_ready, 1)

            def body(t):
                G = lambda g: t.b * NG + g
                for g in range(NG):
                    if g == 0:
                        if t.projects:
                            copy(t, "xT0", xh[:, 0], xh_ready)
                        if t.outputs:
                            split_out(G(-1), NG - 1)
                        if t.projects:
                            copy(t, "xT1", xh[:, 1], xh_ready)
                        if t.attends:
                            rounded(lambda dst, src: A(dst, src, ACT.Copy), act, t, 0, 0, act_copied, pace_a)
                        if t.first:
                            for k in range(4):
                                act.wait_ge(w_loaded[k], 16 + START)
                                A(wh[:, k].rearrange("p c d -> p (c d)"), staged(k), ACT.Copy).then_inc(wh_ready, 1)
                    for part in range(3):
                        if g >= 2 and part < 2 and t.projects:
                            copy(t, "qk"[g - 2] + "T" + "ab"[part], th[:, g - 2, 2 * part:2 * part + 2], th_ready)
                        if t.attends:
                            exps(G(g), part)
                    if g == 0 and t.attends:
                        rounded(lambda dst, src: A(dst, src, ACT.Copy), act, t, 0, 1, act_copied, pace_a)
                    if t.attends and g:
                        split_out(G(g - 1), g - 1)
                    for k, dst in enumerate((pt0[:, :, 0:P], pt1[:])):
                        if g == 3 and t.projects:
                            copy(t, f"v{k}", vv[:, t.other, k], None)
                        if t.attends and k:
                            act.wait_ge(ptb_full, G(g) + 1 + START)
                            A(pt0[:, :, P:S], ptb[:], ACT.Copy).then_inc(ptb_free, 1)
                        if t.attends:
                            act.wait_ge(pta_full, G(g) * 2 + k + 1 + START)
                            A(dst, pta[:], ACT.Copy).then_inc(pta_free, 1)

            turns(act, body)
            split_out(NB * NG - 1, NG - 1)

        @block.vector
        def _(dve):
            v = nc.vector
            ch = Chain(dve, chain)

            def statistics(b):
                dve.wait_ge(x_loaded, (b + 1) * 16)
                for u in range(2):
                    ch.did(v.bn_stats(stat[:, u, :], x[:, u, :]))
                ch.wait()
                dve.sem_inc(pace_d, 1)
                for u in range(2):
                    ch.did(v.bn_aggr(mv[:, u, :], stat[:, u, :]))
                ch.wait()
                v.tensor_scalar(vare[:], mv[:, :, 1], 1e-5, None, ALU.add).then_inc(mv_ready, 1)

            def normalise(b):
                dve.wait_ge(rstd_ready, b + 1 + START)
                for u in range(2):
                    v.tensor_scalar(x[:, u, :], x[:, u, :], mv[:, u, 0:1], rstd[:, u:u + 1],
                                    ALU.subtract, ALU.mult).then_inc(xn_ready, 1)

            def add(b, u, before):
                dve.wait_ge(hres_loaded, b * 16 + 16 + START)
                dve.wait_ge(pj_full[u], before + 1 + START)
                v.tensor_tensor(hres[:, u], pj[u][:], hres[:, u], ALU.add).then_inc(pj_free[u], 1)

            def lower(t, name, dst, high, ready, count):
                n, _ = t.pj(name)
                dve.wait_ge(ready, count + START)
                last = v.tensor_tensor(dst, pj[n][:].rearrange("p (a b) -> p a b", a=dst.shape[1]), high.bitcast(F32), ALU.subtract)
                last.then_inc(pj_free[n], 1)

            def rotate(t, name):
                n, before = t.pj(name)
                u, k = int(name[1]), 2 * (name[0] == "k") + int(name[1])
                dve.wait_ge(pj_full[n], before + 1 + START)
                dve.wait_ge(rot_ready, (t.b + 1) * 4 + k + START)
                src = pj[n][:].rearrange("p (h e f) -> p h e f", h=NH, e=2)
                cos = rope[:, k // 2, u, 0:1, :].to_broadcast([P, NH, DH])
                sn = rope[:, k // 2, u, 1, :].rearrange("p (e f) -> p e f", e=2)
                r2v = r2[:].rearrange("p (h e f) -> p h e f", h=NH, e=2)
                ch.did(v.tensor_tensor(r1[:].rearrange("p (h f) -> p h f", h=NH),
                                       pj[n][:].rearrange("p (h f) -> p h f", h=NH), cos, ALU.mult))
                for e in range(2):
                    last = v.tensor_tensor(r2v[:, :, e], src[:, :, 1 - e],
                                           sn[:, e:e + 1, :].to_broadcast([P, NH, DH // 2]), ALU.mult)
                    last.then_inc(pj_free[n], 1) if e else ch.did(last)
                dve.wait_ge(pj_free[n], before + 1 + START)
                v.tensor_tensor(rot[:, k], r1[:], r2[:], ALU.add).then_inc(rot_ready, 1)

            def greatest(G, part):
                dst, src = ((nbias[:, 0], s0), (nbias[:, 1, 0:2], s1[0]), (nbias[:, 1, 2:4], s1[1]))[part]
                dve.wait_ge(s_full, G * 3 + part + 1 + START)
                v.tensor_reduce(dst, src[:], AX.X, ALU.max, negate=True).then_inc(bias_ready, 1)

            def divide(G, parts):
                for part in parts:
                    hs = HEADS[part]
                    u, p = (1, p1) if part else (0, p0)
                    dve.wait_ge(exp_done, G * 3 + part + 1 + START)
                    ch.step(v.reciprocal(rden[:, u, hs[0]:hs[-1] + 1], den[:, u, hs[0]:hs[-1] + 1]))
                    for h in hs:
                        last = v.tensor_scalar(p[:, h], p[:, h], rden[:, u, h:h + 1], None, ALU.mult)
                    last.then_inc(p_ready, 1)

            def split_out(G, g):
                dve.wait_ge(oh_ready, G + 1 + START)
                v.tensor_tensor(ol[:, g], od[:], oh[:, g].bitcast(F32), ALU.subtract).then_inc(ol_ready, 1)

            def body(t):
                G = lambda g: t.b * NG + g
                lower_x = lambda u: lower(t, f"xT{u}", xl[:, u], xh[:, u], xh_ready, (t.b + 1) * 2 + u + 1)

                def lower_qk(name):
                    k, b = "qk".index(name[0]), "ab".index(name[2])
                    lower(t, name, tl[:, k, 2 * b:2 * b + 2], th[:, k, 2 * b:2 * b + 2], th_ready,
                          (t.b + 1) * 4 + 2 * k + b + 1)

                for g in range(NG):
                    if g == 0:
                        if t.projects:
                            lower_x(0)
                        if t.outputs:
                            split_out(G(-1), NG - 1)
                        if t.projects:
                            lower_x(1)
                        if t.attends:
                            rounded(v.tensor_copy, dve, t, 1, 0, dve_copied, pace_d)
                        if t.outputs:
                            add(t.b - 1, 0, t.pj("O0")[1])
                        if t.first:
                            for k in range(4):
                                dve.wait_ge(wh_ready, k + 1 + START)
                                v.tensor_tensor(wl[:, k].rearrange("p c d -> p (c d)"), staged(k),
                                                wh[:, k].rearrange("p c d -> p (c d)").bitcast(F32),
                                                ALU.subtract).then_inc(w_ready, 1)
                            dve.wait_ge(loaded, 64 + START)
                    if t.attends:
                        greatest(G(g), 0)
                    if g >= 2 and t.projects:
                        lower_qk("qk"[g - 2] + "Ta")
                    if t.attends:
                        greatest(G(g), 1)
                        greatest(G(g), 2)
                    if t.attends:
                        divide(G(g), [0])
                    if g >= 2 and t.projects:
                        lower_qk("qk"[g - 2] + "Tb")
                    if t.attends:
                        divide(G(g), [1, 2])
                    if g == 0 and t.outputs:
                        add(t.b - 1, 1, t.pj("O1")[1])
                    if g == 0 and t.attends:
                        rounded(v.tensor_copy, dve, t, 1, 1, dve_copied, pace_d)
                    if g and t.attends:
                        split_out(G(g - 1), g - 1)
                    if g == 1 and t.projects:
                        rotate(t, "q1")
                    if g == 0 and t.projects:
                        statistics(t.b + 2)
                    if g == 3 and t.projects:
                        normalise(t.b + 2)
                    if g < 3 and t.projects:
                        rotate(t, ["q0", "k0", "k1"][g])

            statistics(0)
            normalise(0)
            turns(dve, body, ch)
            split_out(NB * NG - 1, NG - 1)
            for u in range(2):
                add(NB - 1, u, LAST)

        @block.tensor
        def _(pe):
            mm = nc.tensor.matmul

            def use(t, name):
                n, before = t.pj(name)
                pe.wait_ge(pj_free[n], before + START)
                return n

            def exact(dst, terms):
                parts = [(a[m], b[n]) for a, b in terms for m, n in ((0, 0), (0, 1), (1, 0))]
                for m, (a, b) in enumerate(parts):
                    last = mm(dst, a, b, start=(m == 0), stop=(m == len(parts) - 1))
                return last

            def out_proj(b, u):
                rows = slice(u * P, (u + 1) * P)
                parts = [(c, x_[:, c, rows], y[:, 3, c]) for c in range(NG) for x_, y in ((oh, wh), (oh, wl), (ol, wh))]
                for m, (c, x_, y) in enumerate(parts):
                    if u == 0 and m % 3 == 0 and c >= NG - 2:
                        pe.wait_ge(ol_ready, (b + 1) * NG - (NG - 1 - c) + START)
                    last = mm(pj[u][:], x_, y, start=(m == 0), stop=(m == len(parts) - 1))
                last.then_inc(pj_full[u], 1)

            def turn_x(t, u):
                n = use(t, f"xT{u}")
                pe.wait_ge(xn_ready, (t.b + 1) * 2 + (u + 1) + START)
                for c in range(NG):
                    last = nc.tensor.transpose(pj[n][:, c * P:(c + 1) * P], x[:, u, c * P:(c + 1) * P], ident[:])
                last.then_inc(pj_full[n], 1)

            def project(t, name):
                k, u = "qkv".index(name[0]), int(name[1])
                n, before = t.pj(f"xT{u}")
                pe.wait_ge(pj_free[n], before + 1 + START)
                if t.first:
                    pe.wait_ge(w_ready, k + 1 + START)
                    if name == "v1":
                        pe.wait_ge(w_ready, 4 + START)
                n = use(t, name)
                exact(pj[n][:], [((xh[:, u, c], xl[:, u, c]), (wh[:, k, c], wl[:, k, c])) for c in range(NG)]
                      ).then_inc(pj_full[n], 1)

            def turn_qk(t, name):
                k, pair = "qk".index(name[0]), "ab".index(name[2])
                n = use(t, name)
                pe.wait_ge(rot_ready, (t.b + 1) * 4 + 2 + 2 * k + START)
                for e in range(2):
                    for u in range(2):
                        c = 2 * pair + e
                        last = nc.tensor.transpose(pj[n][:, e * S + u * P:e * S + (u + 1) * P],
                                                   rot[:, 2 * k + u, c * P:(c + 1) * P], ident[:])
                last.then_inc(pj_full[n], 1)

            def scores(t, g):
                G = t.b * NG + g
                if g < 2:
                    pe.wait_ge(act_copied, t.b * 2 + g + 1 + START)
                    pe.wait_ge(dve_copied, t.b * 2 + g + 1 + START)
                else:
                    pe.wait_ge(pool_copied, t.b * 4 + 2 * (g - 1) + START)
                for part, hs in enumerate(HEADS):
                    u, dst = (1, s1[part - 1]) if part else (0, s0)
                    pe.wait_ge(exp_done, G * 3 - 2 + part + START)
                    mm(dst[:, :, P:S] if u else dst[:], identb[:], maskb[:, 0:len(hs), :], start=True, stop=False,
                       skip_group_check=True)
                    for n, h in enumerate(hs):
                        last = mm(dst[:, n, :], stack[0:3 * DH, 0, g, h, u * P:(u + 1) * P],
                                  stack[0:3 * DH, 1, g, h, 0:(u + 1) * P], start=False, stop=True,
                                  skip_group_check=True)
                    last.then_inc(s_full, 1)

            def turn_p(t, g, parts):
                G = t.b * NG + g
                for part in parts:
                    src, dst, full, free, after = (
                        (p0[:], pta, pta_full, pta_free, G * 2), (p1[:, :, 0:P], ptb, ptb_full, ptb_free, G),
                        (p1[:, :, P:S], pta, pta_full, pta_free, G * 2 + 1))[part]
                    if part < 2:
                        pe.wait_ge(p_ready, G * 3 + 2 * part + 1 + START)
                    pe.wait_ge(free, after + START)
                    for h in range(GH):
                        last = nc.tensor.transpose(dst[:, h, :], src[:, h, :], ident[:])
                    last.then_inc(full, 1)

            def weigh(G, g, parity):
                pe.wait_ge(pta_free, G * 2 + 1 + START)
                pe.wait_ge(ptb_free, G + 1 + START)
                pe.wait_ge(ol_ready, G + START)
                for k, (src, cols) in enumerate(((pt0, slice(0, S)), (pt1, slice(P, S)))):
                    if k:
                        pe.wait_ge(pta_free, G * 2 + 2 + START)
                    for h in range(GH):
                        head = slice((g * GH + h) * DH, (g * GH + h + 1) * DH)
                        last = mm(od[h * DH:(h + 1) * DH, cols], vv[:, parity, k, head], src[:, h, :],
                                  start=(k == 0), stop=(k == 1), skip_group_check=True)
                last.then_inc(od_full, 1)

            def body(t):
                G = lambda g: t.b * NG + g
                if t.first:
                    pe.wait_ge(loaded, 64 + START)
                if t.projects:
                    turn_x(t, 0)
                if t.outputs:
                    weigh(G(-1), NG - 1, t.other)
                if t.projects:
                    turn_x(t, 1)
                if t.outputs:
                    use(t, "O0")
                    out_proj(t.b - 1, 0)
                for g in range(NG):
                    if t.attends:
                        scores(t, g)
                    if g >= 2 and t.projects:
                        turn_qk(t, "qk"[g - 2] + "Ta")
                        turn_qk(t, "qk"[g - 2] + "Tb")
                    if g and t.attends:
                        weigh(G(g - 1), g - 1, t.mine)
                    if g == 0 and t.outputs:
                        use(t, "O1")
                        out_proj(t.b - 1, 1)
                    early, late = (([], ["q0"]), (["q1"], ["k0"]), (["k1"], []), (["v0"], ["v1"]))[g]
                    for names, parts in ((early, [0]), (late, [1, 2])):
                        if t.projects:
                            for name in names:
                                project(t, name)
                        if t.attends:
                            turn_p(t, g, parts)

            turns(pe, body)
            weigh(NB * NG - 1, NG - 1, 1)
            for u in range(2):
                pe.wait_ge(pj_free[u], LAST + START)
                out_proj(NB - 1, u)


NE, NGRP, GE = 32, 8, 4
TOPG, TOPK = 3, 4
CAP = -(-5 * T // (4 * NE))
HALF = CAP // 2
DI = 256
ROUTE_SCALE = 2.5
PER_BLOCK = 82
FAR = 1 << 20


def feed_forward(nc, h2_dram, rw_in, bias_in, ident_in, tri_in, ones_in, iota_in, shared_w, xn_dram, table, out):
    TQ = 4
    TB = TQ * P
    NBLK = T // TB
    with ExitStack() as ctx:
        sb = lambda name, shape, dt=F32: ctx.enter_context(nc.sbuf_tensor(name, shape, dt))
        sem, made = semaphores(nc, ctx)
        rw = sb("rw", [P, NG, NE])
        rwh = sb("rwh", [P, NG, NE], F32R)
        rwl = sb("rwl", [P, NG, NE], F32R)
        bias = sb("bias", [P, NE])
        ident = sb("ident2", [P, P])
        tri = sb("tri", [P, P], BF16)
        ones = sb("ones2", [P, P], BF16)
        iota = sb("iota", [P, 3, NE])
        w = sb("w_shared", [P, 3, NG, D])
        wh = sb("wh_shared", [P, 3, NG, D], F32R)
        wl = sb("wl_shared", [P, 3, NG, D], F32R)
        stat, mv = sb("stat2", [P, TQ, 6]), sb("mv2", [P, TQ, 2])
        vare, half, rstd = sb("vare2", [P, TQ]), sb("half2", [P, TQ]), sb("rstd2", [P, TQ])
        xn = sb("xn2", [P, TQ, D])
        hres = sb("hres2", [P, TQ, D])
        xh = sb("xh2", [P, NG, TB], F32R)
        xl = sb("xl2", [P, NG, TB], F32R)
        lgT = sb("lgT", [NE, TB])
        score = sb("score", [P, TQ, NE])
        sc = sb("sc", [P, TQ, NE])
        ga = sb("ga", [P, 4, TQ * NGRP])
        gs = sb("gs", [P, TQ, NGRP])
        gpick = sb("gpick", [P, 2, TQ, NGRP])
        gmask = sb("gmask", [P, TQ, NGRP])
        gcand = sb("gcand", [P, TQ, NGRP])
        best = sb("best", [P, 2, TQ])
        cand = sb("cand", [P, 2, TQ, NE])
        oh = sb("oh", [P, TOPK, TQ, NE])
        picked = sb("picked", [P, TQ, TOPK, NE])
        chosenb = sb("chosenb", [P, TQ, NE], BF16)
        place = sb("place", [P, TQ, NE])
        carry = sb("carry", [P, NE])
        wsel = sb("wsel", [P, TQ, TOPK])
        wsum = sb("wsum", [P, TQ])
        slotf = sb("slotf", [P, TQ, TOPK])
        slots = sb("slots", [P, TQ, TOPK], I32)
        tw = sb("tw", [P, TQ, TOPK, 2])
        tok = sb("tok", [P, NT + TQ], I32)
        empty = sb("empty", [P, 2 * NE * CAP // P])
        sg = sb("sg", [P, 2, TB])
        hf = sb("hf", [P, 2, TB])
        hh = sb("hh", [P, NG, TB], F32R)
        hl = sb("hl", [P, NG, TB], F32R)
        ys = sb("ys", [P, 2, D])
        bank = lambda name, shape: ctx.enter_context(nc.psum_tensor(name, shape, F32))
        tp = [bank("tp0", [P, TB]), bank("tp1", [P, TB])]
        pg = [bank(f"pg{u}", [P, TB]) for u in range(2)]
        pu = [bank(f"pu{u}", [P, TB]) for u in range(2)]
        py = [bank(f"py{u}", [P, D]) for u in range(2)]
        x_in, hres_in = sem("x2_in"), sem("hres2_in")
        two = lambda name: [sem(f"{name}{u}") for u in range(2)]
        small_in, w_in, w_split, chain = sem("small_in"), [sem(f"w_in{k}") for k in range(3)], sem("w_split"), sem("ffn_dve")
        wh_done, pool_set, empty_out = sem("wh_done"), sem("pool_set"), sem("empty_out")
        mv_ready, rstd_ready, xn_ready, xn_stored = sem("mv_ready"), sem("rstd_ready"), sem("xn2_ready"), sem("xn2_stored")
        tp_full, tp_free, xh_ready = two("tp_full"), two("tp_free"), sem("xh_ready")
        lgT_ready, score_ready, chosen_ready = sem("lgT_ready"), sem("score_ready"), sem("chosen_ready")
        gu_full, sg_ready, h_ready, hf_ready, hh_ready = two("gu_full"), two("sg_ready"), sem("h_ready"), two("hf_ready"), sem("hh_ready")
        py_full, py_free, ys_free = two("py_full"), two("py_free"), two("ys_free")
        slots_ready, scattered, out_stored = sem("slots_ready"), sem("scattered"), sem("out_stored")
        pace_p, pace_d, pace_t, pace_s, pace_a = [sem(f"ffn_{name}_pace") for name in ("pool", "dve", "pe", "sp", "act")]
        slots_out = ctx.enter_context(nc.semaphore("slots_out"))
        block = ctx.enter_context(nc.Block())

        def turns(eng, body):
            body("first", -1)
            with eng.Fori(0, NBLK - 1) as i:
                body("loop", i)
            body("last", NBLK - 1)

        def tp_use(name, n):
            if name == "count":
                return 0, n * 4 + (3 if isinstance(n, int) else 6)
            k = ["x0", "x1", "x2", "x3", "lg", "lt"].index(name)
            if k % 2:
                return 1, n * 3 + k // 2
            return 0, k // 2 if isinstance(n, int) else n * 4 + (k // 2 - 1)

        hrows = h2_dram.rearrange("(t p) d -> p t d", p=P)
        block_of = lambda a, n: a[:, slice(n * TQ, n * TQ + TQ) if isinstance(n, int) else bass.ds(n * TQ, TQ), :]

        @block.sync
        def _(sp):
            start(sp, made)
            xrows = xn_dram.rearrange("(t p) d -> p t d", p=P)
            rows = out.rearrange("(t p) d -> p t d", p=P)
            sp.dma_start(xn[:], block_of(hrows, 0)).then_inc(x_in, 16)
            for dst, src in ((ident, ident_in), (rw, rw_in), (bias, bias_in), (tri, tri_in), (ones, ones_in), (iota, iota_in)):
                sp.dma_start(dst[:], src[:]).then_inc(small_in, 16)
            sp.wait_ge(pool_set, 2 + START)
            sp.dma_start(table.rearrange("(p s) c -> p (s c)", p=P), empty[:]).then_inc(empty_out, 16)
            def body(kind, n):
                if kind != "first":
                    sp.wait_ge(out_stored, n * 16 + START)
                    sp.sem_inc(pace_s, 1)
                    sp.dma_start(hres[:], block_of(hrows, n)).then_inc(hres_in, 16)
                if kind != "last":
                    sp.wait_ge(xn_ready, (n + 1) * TQ + TQ + START)
                    sp.sem_inc(pace_s, 1)
                    sp.dma_start(block_of(xrows, n + 1), xn[:]).then_inc(xn_stored, 16)
                if kind != "first":
                    for u in range(2):
                        sp.wait_ge(ys_free[u], n * 2 + 2 + START)
                        sp.sem_inc(pace_s, 1)
                    sp.dma_start(block_of(rows, n), hres[:]).then_inc(out_stored, 16)

            turns(sp, body)
            sp.wait_ge(xn_stored, 16 * NBLK + START)
            sp.wait_ge(out_stored, 16 * NBLK + START)
            sp.wait_ge(empty_out, 16 + START)

        @block.gpsimd
        def _(pool):
            g = nc.gpsimd
            ev = empty[:].rearrange("p (s c) -> p s c", c=2)
            g.memset(ev[:, :, 0], float(FAR)).then_inc(pool_set, 1)
            g.memset(ev[:, :, 1], 0.0).then_inc(pool_set, 1)
            g.memset(half[:], -0.5).then_inc(pool_set, 1)
            g.memset(slots[:], FAR).then_inc(pool_set, 1)
            g.memset(tw[:], 0.0).then_inc(pool_set, 1)
            g.iota(tok[:], [[P, NT + TQ]], base=-TB, channel_multiplier=1).then_inc(pool_set, 1)
            pool.wait_ge(pool_set, 6 + START)

            def scatter(kind, n, tks, before):
                pool.wait_ge(slots_ready, n + 1 + START)
                if kind == "loop":
                    pool.sem_inc(pace_p, 1)
                for k in range(TOPK):
                    g.tensor_copy(tw[:, :, k, 0], tks).then_inc(pool_set, 1)
                pool.wait_ge(pool_set, 6 + TOPK + before * TOPK + START)
                pool.sem_inc(pace_p, 1)
                pool.wait_ge(empty_out, 16 + START)
                for q in range(TQ):
                    for k in range(TOPK):
                        g.indirect_dma_start(
                            table[:, :], bass.IndirectOffsetOnAxis(slots[:, q, k:k + 1].bitcast(U32), 0),
                            tw[:, q, k, :], None, bounds_check=NE * CAP - 1, oob_is_err=False).then_inc(slots_out, 16)
                pool.wait_ge(slots_out, before * (16 * TQ * TOPK) + 16 * TQ * TOPK)
                pool.sem_inc(scattered, 1)

            def body(kind, n):
                if kind != "last":
                    pool.wait_ge(mv_ready, n + 2 + START)
                    pool.sem_inc(pace_p, 1)
                    g.tensor_tensor(rstd[:], vare[:], half[:], ALU.pow).then_inc(rstd_ready, 1)
                if kind != "first":
                    scatter(kind, n - 1, tok[:, bass.ds(n * TQ, TQ)] if kind == "loop" else tok[:, n * TQ:n * TQ + TQ], n)
                    if kind == "last":
                        scatter(kind, n, tok[:, NT:NT + TQ], NBLK)
                        return
                    pool.wait_ge(hres_in, n * 16 + 16 + START)
                    for q in range(TQ):
                        u = q % 2
                        pool.wait_ge(py_free[u], n * 2 + (q // 2 + 1) + START)
                        pool.sem_inc(pace_p, 1)
                        g.tensor_tensor(hres[:, q], ys[:, u], hres[:, q], ALU.add).then_inc(ys_free[u], 1)

            turns(pool, body)

        @block.tensor
        def _(pe):
            mm = nc.tensor.matmul

            def exact(dst, terms):
                parts = [(a[x], b[y]) for a, b in terms for x, y in ((0, 0), (0, 1), (1, 0))]
                for m, (a, b) in enumerate(parts):
                    last = mm(dst, a, b, start=(m == 0), stop=(m == len(parts) - 1))
                return last

            def prepare(n, cs):
                pe.wait_ge(xn_ready, n * TQ + TQ + START)
                for c in cs:
                    b, before = tp_use(f"x{c}", n)
                    pe.wait_ge(tp_free[b], before + START)
                    for q in range(TQ):
                        last = nc.tensor.transpose(tp[b][:, q * P:(q + 1) * P], xn[:, q, c * P:(c + 1) * P], ident[:])
                    last.then_inc(tp_full[b], 1)

            def logits(n):
                b, before = tp_use("lg", n)
                pe.wait_ge(tp_free[b], before + START)
                pe.wait_ge(tp_free[1], tp_use("x3", n)[1] + 1 + START)
                exact(tp[b][0:NE, :], [((rwh[:, c, :], rwl[:, c, :]), (xh[:, c, :], xl[:, c, :])) for c in range(NG)]
                      ).then_inc(tp_full[b], 1)

            def scores(n):
                b, before = tp_use("lt", n)
                pe.wait_ge(tp_free[b], before + START)
                pe.wait_ge(lgT_ready, n + 1 + START)
                pe.sem_inc(pace_t, 1)
                for q in range(TQ):
                    last = nc.tensor.transpose(tp[b][:, q * NE:(q + 1) * NE], lgT[:, q * P:(q + 1) * P], ident[0:NE, 0:NE])
                last.then_inc(tp_full[b], 1)

            def count(n):
                b, before = tp_use("count", n)
                pe.wait_ge(chosen_ready, n + 1 + START)
                pe.wait_ge(tp_free[b], before + START)
                cnt = tp[b][:, 0:(TQ + 1) * NE].rearrange("p (q e) -> p q e", e=NE)
                for q in range(TQ):
                    mm(cnt[:, TQ, :], ones[:], chosenb[:, q, :], start=(q == 0), stop=(q == TQ - 1))
                mm(cnt[:, 0:TQ, :], tri[:], chosenb[:], start=True, stop=False, skip_group_check=True)
                for q in range(TQ - 1):
                    src = chosenb[:, q:q + 1, :].to_broadcast([P, TQ - 1 - q, NE])
                    last = mm(cnt[:, q + 1:TQ, :], ones[:], src, start=False, stop=(q == TQ - 2), skip_group_check=True)
                last.then_inc(tp_full[b], 1)

            def body(kind, n):
                if kind == "first":
                    prepare(0, range(NG))
                    pe.wait_ge(w_split, 1 + START)
                    logits(0)
                    scores(0)
                    return
                for f in range(NG):
                    u = f % 2
                    pe.wait_ge(hf_ready[u], n * 2 + f // 2 + START)
                    if f == 0:
                        pe.wait_ge(w_split, 3 + START)
                    for dst, k in ((pg, 0), (pu, 1)):
                        cols = slice(f * P, (f + 1) * P)
                        last = exact(dst[u][:], [((wh[:, k, c, cols], wl[:, k, c, cols]), (xh[:, c, :], xl[:, c, :]))
                                                 for c in range(NG)])
                    last.then_inc(gu_full[u], 1)
                if kind == "loop":
                    prepare(n + 1, (0, 1))
                pe.wait_ge(w_split, 4 + START)
                for q in range(TQ):
                    u = q % 2
                    if q == 1 and kind == "loop":
                        prepare(n + 1, (2, 3))
                    if kind == "loop" and q == 3:
                        logits(n + 1)
                    if kind == "last" and q == 1:
                        count(n)
                    pe.wait_ge(py_free[u], n * 2 + q // 2 + START)
                    cols = slice(q * P, (q + 1) * P)
                    parts = [(f, a[:, f, cols], b[:, 2, f, :]) for f in range(NG)
                             for a, b in ((hh, wh), (hh, wl), (hl, wh))]
                    for m, (f, a, b) in enumerate(parts):
                        if q == 0 and m % 3 == 0:
                            pe.wait_ge(h_ready, n * NG + (f + 1) + START)
                        last = mm(py[u][:], a, b, start=(m == 0), stop=(m == len(parts) - 1))
                    last.then_inc(py_full[u], 1)
                if kind == "loop":
                    count(n)
                    scores(n + 1)

            pe.wait_ge(small_in, 96 + START)
            turns(pe, body)

        @block.scalar
        def _(act):
            A = nc.scalar.activation
            act.wait_ge(x_in, 16 + START)
            for k in range(3):
                act.dma_start(w[:, k], shared_w[:, k]).then_inc(w_in[k], 16)
            act.wait_ge(small_in, 96 + START)
            A(rwh[:], rw[:], ACT.Copy).then_inc(wh_done, 1)

            def split_high(k):
                act.wait_ge(w_in[k], 16 + START)
                A(wh[:, k], w[:, k], ACT.Copy).then_inc(wh_done, 1)

            def prepare(n, cs):
                for c in cs:
                    b, before = tp_use(f"x{c}", n)
                    act.wait_ge(tp_full[b], before + 1 + START)
                    A(xh[:, c, :], tp[b][:], ACT.Copy).then_inc(xh_ready, 1)

            def logits(n):
                b, before = tp_use("lg", n)
                act.wait_ge(tp_full[b], before + 1 + START)
                A(lgT[:], tp[b][0:NE, :], ACT.Copy).then_inc(lgT_ready, 1)
                act.wait_ge(lgT_ready, n + 1 + START)
                act.sem_inc(tp_free[b], 1)

            def scores(n):
                b, before = tp_use("lt", n)
                act.wait_ge(tp_full[b], before + 1 + START)
                A(score[:].rearrange("p q e -> p (q e)"), tp[b][:, 0:TQ * NE], ACT.Sigmoid).then_inc(score_ready, 1)
                act.wait_ge(score_ready, n + 1 + START)
                act.sem_inc(tp_free[b], 1)

            def body(kind, n):
                if kind == "first":
                    prepare(0, range(NG))
                    for k in range(3):
                        split_high(k)
                    logits(0)
                    scores(0)
                    return
                if kind == "loop":
                    act.wait_ge(xn_stored, (n + 1) * 16 + START)
                    act.sem_inc(pace_a, 1)
                    act.wait_ge(tp_full[1], tp_use("x3", n)[1] + 1 + START)
                    act.sem_inc(pace_a, 1)
                    act.dma_start(xn[:], block_of(hrows, n + 1)).then_inc(x_in, 16)
                for f in range(NG):
                    u = f % 2
                    act.wait_ge(hf_ready[u], n * 2 + f // 2 + START)
                    act.wait_ge(gu_full[u], n * 2 + (f // 2 + 1) + START)
                    A(sg[:, u], pg[u][:], ACT.Silu).then_inc(sg_ready[u], 1)
                    act.wait_ge(hf_ready[u], n * 2 + (f // 2 + 1) + START)
                    A(hh[:, f], hf[:, u], ACT.Copy).then_inc(hh_ready, 1)
                for q in range(TQ):
                    u = q % 2
                    if q < 2 and kind == "loop":
                        prepare(n + 1, (2 * q, 2 * q + 1))
                    act.wait_ge(ys_free[u], n * 2 + q // 2 + START)
                    act.wait_ge(py_full[u], n * 2 + (q // 2 + 1) + START)
                    A(ys[:, u], py[u][:], ACT.Copy).then_inc(py_free[u], 1)
                    if q == 2 and kind == "loop":
                        logits(n + 1)
                if kind == "loop":
                    scores(n + 1)

            turns(act, body)

        @block.vector
        def _(dve):
            v = nc.vector
            ch = Chain(dve, chain)
            TT = lambda o, a, b, op: ch.did(v.tensor_tensor(o, a, b, op))
            along = lambda a, m: a.unsqueeze(2).to_broadcast([P, TQ, m])
            row = lambda k, m: iota[:, k:k + 1, 0:m].to_broadcast([P, TQ, m])

            def statistics(kind, n):
                dve.wait_ge(x_in, n * 16 + 32 + START)
                dve.sem_inc(pace_d, 1)
                for q in range(TQ):
                    ch.did(v.bn_stats(stat[:, q, :], xn[:, q, :]))
                ch.wait()
                dve.sem_inc(pace_d, 1)
                for q in range(TQ):
                    ch.did(v.bn_aggr(mv[:, q, :], stat[:, q, :]))
                ch.wait()
                v.tensor_scalar(vare[:], mv[:, :, 1], 1e-5, None, ALU.add).then_inc(mv_ready, 1)

            def normalise(kind, n):
                dve.wait_ge(rstd_ready, n + 2 + START)
                for q in range(TQ):
                    v.tensor_scalar(xn[:, q, :], xn[:, q, :], mv[:, q, 0:1], rstd[:, q:q + 1],
                                    ALU.subtract, ALU.mult).then_inc(xn_ready, 1)

            def lower_x(n, cs):
                for c in cs:
                    b, before = tp_use(f"x{c}", n)
                    dve.wait_ge(xh_ready, n * NG + (c + 1) + START)
                    v.tensor_tensor(xl[:, c, :], tp[b][:], xh[:, c, :].bitcast(F32), ALU.subtract).then_inc(tp_free[b], 1)

            def first_best(cand_, best_, pick, values, k, m):
                ch.step(v.tensor_reduce(best_, values, AX.X, ALU.max))
                ch.step(v.tensor_tensor(cand_, values, along(best_, m), ALU.is_equal))
                ch.step(v.tensor_tensor(cand_, cand_, row(k, m), ALU.mult))
                ch.step(v.tensor_reduce(best_, cand_, AX.X, ALU.min))
                ch.step(v.tensor_tensor(pick, row(k, m), along(best_, m), ALU.is_equal))

            four = sc[:].rearrange("p t (g m) -> p (t g) m", m=GE)

            def score_groups(n):
                dve.wait_ge(score_ready, n + 1 + START)
                ch.step(v.tensor_tensor(sc[:], score[:], bias[:, :].unsqueeze(1).to_broadcast([P, TQ, NE]), ALU.add))
                TT(ga[:, 0], four[:, :, 0], four[:, :, 1], ALU.max)
                TT(ga[:, 1], four[:, :, 2], four[:, :, 3], ALU.max)
                TT(ga[:, 2], four[:, :, 0], four[:, :, 1], ALU.add)
                TT(ga[:, 3], four[:, :, 2], four[:, :, 3], ALU.add)
                ch.wait()
                gsf = gs[:].rearrange("p t g -> p (t g)")
                TT(gsf, ga[:, 0], ga[:, 1], ALU.add)
                TT(ga[:, 2], ga[:, 2], ga[:, 3], ALU.max)
                ch.wait()
                ch.step(v.tensor_tensor(gsf, gsf, ga[:, 2], ALU.max))

            def pick_groups(ks):
                for k in ks:
                    pick = gpick[:, k % 2] if k else gmask[:]
                    first_best(gcand[:], best[:, k % 2], pick, gs[:], 1, NGRP)
                    ch.did(v.scalar_tensor_tensor(gs[:], pick, -1e30, gs[:], ALU.mult, ALU.add))
                    if k:
                        TT(gmask[:], gmask[:], pick, ALU.add)
                    ch.wait()

            def keep_groups():
                ch.step(v.tensor_tensor(four, four, gmask[:].rearrange("p t g -> p (t g)").unsqueeze(2).to_broadcast(
                    [P, TQ * NGRP, GE]), ALU.mult))

            def pick_expert(k):
                ch.wait()
                first_best(cand[:, k % 2], best[:, k % 2], oh[:, k], sc[:], 0, NE)
                ch.did(v.scalar_tensor_tensor(sc[:], oh[:, k], -1e30, sc[:], ALU.mult, ALU.add))
                TT(picked[:, :, k, :], oh[:, k], score[:], ALU.mult)

            def weigh(n):
                ch.wait()
                TT(cand[:, 0], oh[:, 0], oh[:, 1], ALU.add)
                TT(cand[:, 1], oh[:, 2], oh[:, 3], ALU.add)
                ch.wait()
                ch.did(v.tensor_reduce(wsel[:], picked[:], AX.X, ALU.add))
                v.tensor_tensor(chosenb[:], cand[:, 0], cand[:, 1], ALU.add).then_inc(chosen_ready, 1)
                ch.wait()
                ch.step(v.tensor_reduce(wsum[:], wsel[:], AX.X, ALU.add))
                ch.step(v.tensor_scalar(wsum[:], wsum[:], 1e-20, None, ALU.add))
                ch.step(v.reciprocal(wsum[:], wsum[:]))
                dve.wait_ge(scattered, n + 1 + START)
                ch.step(v.tensor_tensor(wsel[:], wsel[:], wsum[:].unsqueeze(2).to_broadcast([P, TQ, TOPK]), ALU.mult))
                ch.did(v.tensor_scalar(tw[:, :, :, 1], wsel[:], ROUTE_SCALE, None, ALU.mult))

            def give_slots(n):
                b, before = tp_use("count", n)
                dve.wait_ge(tp_full[b], before + 1 + START)
                cnt = tp[b][:, 0:(TQ + 1) * NE].rearrange("p (q e) -> p q e", e=NE)
                ch.step(v.tensor_tensor(place[:], cnt[:, 0:TQ], carry[:].unsqueeze(1).to_broadcast([P, TQ, NE]), ALU.add))
                v.tensor_tensor(carry[:], cnt[:, TQ], carry[:], ALU.add).then_inc(tp_free[b], 1)
                ch.did(v.tensor_scalar(cand[:, 0], place[:], float(CAP), float(FAR), ALU.is_ge, ALU.mult))
                ch.step(v.tensor_tensor(place[:], place[:], row(2, NE), ALU.add))
                ch.step(v.tensor_tensor(place[:], place[:], cand[:, 0], ALU.add))
                for k in range(TOPK):
                    TT(picked[:, :, k, :], oh[:, k], place[:], ALU.mult)
                ch.wait()
                ch.step(v.tensor_reduce(slotf[:], picked[:], AX.X, ALU.add))
                v.tensor_copy(slots[:], slotf[:]).then_inc(slots_ready, 1)

            def hidden(n, f):
                u = f % 2
                dve.wait_ge(sg_ready[u], n * 2 + (f // 2 + 1) + START)
                v.tensor_tensor(hf[:, u], pu[u][:], sg[:, u], ALU.mult).then_inc(hf_ready[u], 1)

            def lower_h(n, f):
                dve.wait_ge(hh_ready, n * NG + (f + 1) + START)
                v.tensor_tensor(hl[:, f], hf[:, f % 2], hh[:, f].bitcast(F32), ALU.subtract).then_inc(h_ready, 1)

            def body(kind, n):
                if kind == "first":
                    statistics(kind, n)
                    normalise(kind, n)
                    dve.wait_ge(small_in, 96 + START)
                    dve.wait_ge(wh_done, 1 + START)
                    v.tensor_tensor(rwl[:], rw[:], rwh[:].bitcast(F32), ALU.subtract).then_inc(w_split, 1)
                    lower_x(0, range(NG))
                    for k in range(3):
                        dve.wait_ge(wh_done, k + 2 + START)
                        v.tensor_tensor(wl[:, k], w[:, k], wh[:, k].bitcast(F32), ALU.subtract).then_inc(w_split, 1)
                    return
                score_groups(n)
                pick_groups([0])
                hidden(n, 0)
                pick_groups([1])
                lower_h(n, 0)
                if kind == "loop":
                    statistics(kind, n)
                hidden(n, 1)
                pick_groups([2])
                lower_h(n, 1)
                if kind == "last":
                    keep_groups()
                    pick_expert(0)
                hidden(n, 2)
                if kind == "loop":
                    normalise(kind, n)
                    keep_groups()
                    pick_expert(0)
                else:
                    pick_expert(1)
                lower_h(n, 2)
                hidden(n, 3)
                if kind == "last":
                    pick_expert(2)
                lower_h(n, 3)
                if kind == "loop":
                    lower_x(n + 1, (0, 1))
                    pick_expert(1)
                    pick_expert(2)
                    lower_x(n + 1, (2, 3))
                pick_expert(3)
                weigh(n)
                give_slots(n)
                if kind == "last":
                    dve.wait_ge(hres_in, n * 16 + 16 + START)
                    for q in range(TQ):
                        u = q % 2
                        dve.wait_ge(py_free[u], n * 2 + (q // 2 + 1) + START)
                        v.tensor_tensor(hres[:, q], ys[:, u], hres[:, q], ALU.add).then_inc(ys_free[u], 1)

            ch.did(v.memset(carry[:], 0.0))
            body("first", -1)
            with dve.Fori(0, NBLK - 1) as i:
                ch.enter(i, PER_BLOCK)
                body("loop", i)
                ch.leave(NBLK - 1)
            body("last", NBLK - 1)


def experts(nc, gate_in, up_in, down_in, ident_in, xn_dram, table, out):
    NI = DI // P
    R = 4
    with ExitStack() as ctx:
        sb = lambda name, shape, dt=F32: ctx.enter_context(nc.sbuf_tensor(name, shape, dt))
        sem, made = semaphores(nc, ctx)
        ident = sb("ident4", [P, P])
        wg = sb("wg", [P, R, NG, DI])
        wu = sb("wu", [P, R, NG, DI])
        wd = sb("wd", [P, R, NI, D])
        wdh = sb("wdh", [P, 2, NI, D], F32R)
        wdl = sb("wdl", [P, 2, NI, D], F32R)
        tab = sb("tab", [2 * NE, HALF, 2])
        tokens = sb("tokens", [HALF, 2 * NE], I32)
        weight = sb("weight", [HALF, 2 * NE])
        xtok = sb("xtok", [HALF, R, 2], I32)
        ytok = sb("ytok", [HALF, R, 2], I32)
        xg = sb("xg", [HALF, R, 2, D])
        xT = sb("xTe", [P, 2, NG, CAP])
        sg = sb("sge", [P, 2, NI, CAP])
        hf = sb("hfe", [P, 2, NI, CAP])
        hh = sb("hhe", [P, 2, NI, CAP], F32R)
        hl = sb("hle", [P, 2, NI, CAP], F32R)
        y = sb("y", [HALF, R, 2, D])
        bank = lambda name, shape: ctx.enter_context(nc.psum_tensor(name, shape, F32))
        px = [bank(f"px{k}", [P, 2, CAP]) for k in range(2)]
        pg = [bank(f"peg{k}", [P, NI, CAP]) for k in range(2)]
        pu = [bank(f"peu{k}", [P, NI, CAP]) for k in range(2)]
        py = [bank(f"pey{k}", [P, D]) for k in range(2)]
        ident_loaded, cleared = sem("ident_loaded"), sem("cleared")
        tab_loaded, tab_turned, tab_ready = sem("tab_loaded"), sem("tab_turned"), sem("tab_ready")
        gu_loaded, d_loaded = [[sem(f"{name}{k}") for k in range(R)] for name in ("gu_loaded", "d_loaded")]
        x_full, xT_ready, gu_full, sg_ready = sem("x_full"), sem("xT_ready"), sem("egu_full"), sem("esg_ready")
        hf_ready, hh_ready, h_ready = sem("ehf_ready"), sem("ehh_ready"), sem("eh_ready")
        wdh_ready, wd_ready = sem("wdh_ready"), sem("wd_ready")
        y_full, y_ready, y_done = sem("ey_full"), sem("ey_ready"), sem("ey_done")
        x_loaded, y_added = [[ctx.enter_context(nc.semaphore(f"{name}{k}")) for k in range(R)]
                             for name in ("x_loaded", "y_added")]
        xpicked, ypicked = sem("xpicked"), sem("ypicked")
        pace = sem("expert_pace")
        block = ctx.enter_context(nc.Block())

        class Expert:

            def __init__(self, i, c):
                self.i, self.c, self.n = i, c, i * R + c
                self.slot, self.turn = c % R, i + c // R
                self.half = c % 2

            def ahead(self, k):
                return Expert(self.i, self.c + k)

            def columns(self):
                return bass.ds(self.i * (2 * R) + 2 * self.c, 2)

        def each(eng, body, first, last):
            turns = (last - first) // R
            with eng.Fori(0, turns) as i:
                for k in range(R):
                    body(Expert(i, first + k))
            for c in range(first + turns * R, last):
                body(Expert(0, c))

        @block.sync
        def _(sp):
            start(sp, made)
            sp.dma_start(tab[:], table.rearrange("(g s) c -> g s c", s=HALF)).then_inc(tab_loaded, 16)
            sp.dma_start(ident[:], ident_in[:]).then_inc(ident_loaded, 16)

            def load(e):
                k, at = e.slot, bass.ds(e.n, 1)
                sp.wait_ge(gu_full, e.n - R + 1 + START)
                sp.dma_start(wg[:, k:k + 1], gate_in[:, at]).then_inc(gu_loaded[k], 16)
                sp.dma_start(wu[:, k:k + 1], up_in[:, at]).then_inc(gu_loaded[k], 16)
                sp.wait_ge(wd_ready, e.n - R + 1 + START)
                sp.dma_start(wd[:, k:k + 1], down_in[:, at]).then_inc(d_loaded[k], 16)

            each(sp, load, 0, NE)

        @block.gpsimd
        def _(pool):
            g = nc.gpsimd
            pool.wait_ge(cleared, 1 + START)
            pool.wait_ge(tab_ready, 2 + START)

            def gather(e):
                k = e.slot
                pool.wait_ge(x_full, e.n - R + 1 + START)
                pool.sem_inc(pace, 1)
                g.tensor_copy(xtok[:, k], tokens[:, e.columns()]).then_inc(xpicked, 1)
                pool.wait_ge(xpicked, e.n + 1 + START)
                pool.sem_inc(pace, 1)
                for h in range(2):
                    g.indirect_dma_start(xg[:, k, h, :], None, xn_dram[:, :],
                                         bass.IndirectOffsetOnAxis(xtok[:, k, h:h + 1].bitcast(U32), 0),
                                         bounds_check=T - 1, oob_is_err=False).then_inc(x_loaded[k], 16)

            def add(e, first=False):
                k = e.slot
                if not first:
                    last = e.ahead(-1)
                    pool.wait_ge(y_added[last.slot], last.turn * 32 + 32)
                    pool.sem_inc(y_done, 1)
                pool.wait_ge(y_ready, e.n + 1 + START)
                pool.sem_inc(pace, 1)
                g.tensor_copy(ytok[:, k], tokens[:, e.columns()]).then_inc(ypicked, 1)
                pool.wait_ge(ypicked, e.n + 1 + START)
                pool.sem_inc(pace, 1)
                for h in range(2):
                    g.indirect_dma_start(out[:, :], bass.IndirectOffsetOnAxis(ytok[:, k, h:h + 1].bitcast(U32), 0),
                                         y[:, k, h, :], None, bounds_check=T - 1, oob_is_err=False,
                                         compute_op=ALU.add).then_inc(y_added[k], 16)

            def both(e):
                gather(e.ahead(AHEAD))
                add(e)

            AHEAD = R - 1
            for c in range(AHEAD + 1):
                gather(Expert(0, c))
            add(Expert(0, 0), first=True)
            each(pool, both, 1, NE - AHEAD)
            for c in range(NE - AHEAD, NE):
                add(Expert(0, c))
            pool.wait_ge(y_added[R - 1], NE // R * 32)

        @block.tensor
        def _(pe):
            mm = nc.tensor.matmul
            pe.wait_ge(ident_loaded, 16 + START)
            pe.wait_ge(tab_loaded, 16 + START)
            for c in range(2):
                last = nc.tensor.transpose(px[c][0:HALF, 0, 0:2 * NE], tab[:, :, c], ident[0:2 * NE, 0:2 * NE])
            last.then_inc(tab_turned, 1)
            pe.wait_ge(tab_ready, 2 + START)

            def turn_x(e):
                pe.wait_ge(xT_ready, e.n + START)
                pe.wait_ge(x_loaded[e.slot], e.turn * 32 + 32)
                for c in range(NG):
                    for h in range(2):
                        last = nc.tensor.transpose(px[c // 2][:, c % 2, h * HALF:(h + 1) * HALF],
                                                   xg[:, e.slot, h, c * P:(c + 1) * P], ident[0:HALF, 0:HALF])
                last.then_inc(x_full, 1)

            def up(e):
                u = e.half
                pe.wait_ge(xT_ready, e.n + 1 + START)
                pe.wait_ge(hf_ready, e.n - 1 + START)
                pe.wait_ge(gu_loaded[e.slot], e.turn * 32 + 32 + START)
                for dst, w in ((pg[u], wg), (pu[u], wu)):
                    for k in range(NI):
                        for c in range(NG):
                            last = mm(dst[:, k, :], w[:, e.slot, c, k * P:(k + 1) * P], xT[:, u, c, :],
                                      start=(c == 0), stop=(c == NG - 1))
                last.then_inc(gu_full, 1)

            def down(e):
                u = e.half
                pe.wait_ge(y_ready, e.n + START)
                pe.wait_ge(wd_ready, e.n + 1 + START)
                pe.wait_ge(h_ready, e.n + 1 + START)
                for h in range(2):
                    cols = slice(h * HALF, (h + 1) * HALF)
                    parts = [(a[:, u, k, cols], b[:, u, k, :]) for k in range(NI)
                             for a, b in ((hh, wdh), (hh, wdl), (hl, wdh))]
                    for m, (a, b) in enumerate(parts):
                        last = mm(py[h][0:HALF, :], a, b, start=(m == 0), stop=(m == len(parts) - 1))
                last.then_inc(y_full, 1)

            def step(e):
                up(e)
                turn_x(e.ahead(1))
                down(e.ahead(-1))

            turn_x(Expert(0, 0))
            up(Expert(0, 0))
            turn_x(Expert(0, 1))
            each(pe, step, 1, NE - 1)
            up(Expert(0, NE - 1))
            down(Expert(0, NE - 2))
            down(Expert(0, NE - 1))

        @block.scalar
        def _(act):
            A = nc.scalar.activation

            def hidden(e):
                u = e.half
                act.wait_ge(y_full, e.n - 1 + START)
                act.wait_ge(d_loaded[e.slot], e.turn * 16 + 16 + START)
                A(wdh[:, u], wd[:, e.slot], ACT.Copy).then_inc(wdh_ready, 1)
                act.wait_ge(hf_ready, e.n - 1 + START)
                act.wait_ge(gu_full, e.n + 1 + START)
                A(sg[:, u], pg[u][:], ACT.Silu).then_inc(sg_ready, 1)
                act.wait_ge(hf_ready, e.n + 1 + START)
                A(hh[:, u], hf[:, u], ACT.Copy).then_inc(hh_ready, 1)

            def scale(e):
                act.wait_ge(y_done, e.n - R + 1 + START)
                act.wait_ge(y_full, e.n + 1 + START)
                act.sem_inc(pace, 1)
                for h in range(2):
                    last = A(y[:, e.slot, h, :], py[h][0:HALF, :], ACT.Copy,
                             scale=weight[:, bass.ds(e.i * (2 * R) + (2 * e.c + h), 1)])
                last.then_inc(y_ready, 1)

            def step(e):
                hidden(e)
                scale(e.ahead(-1))

            act.wait_ge(tab_ready, 2 + START)
            hidden(Expert(0, 0))
            each(act, step, 1, NE)
            scale(Expert(0, NE - 1))

        @block.vector
        def _(dve):
            v = nc.vector
            v.memset(xg[:], 0.0).then_inc(cleared, 1)
            dve.wait_ge(tab_turned, 1 + START)
            v.tensor_copy(tokens[:], px[0][0:HALF, 0, 0:2 * NE]).then_inc(tab_ready, 1)
            v.tensor_copy(weight[:], px[1][0:HALF, 0, 0:2 * NE]).then_inc(tab_ready, 1)

            def turn_x(e):
                dve.wait_ge(gu_full, e.n - 1 + START)
                dve.wait_ge(x_full, e.n + 1 + START)
                for k in range(2):
                    last = v.tensor_copy(xT[:, e.half, 2 * k:2 * k + 2, :], px[k][:])
                last.then_inc(xT_ready, 1)

            def body(e):
                u = e.half
                dve.wait_ge(wdh_ready, e.n + 1 + START)
                v.tensor_tensor(wdl[:, u], wd[:, e.slot], wdh[:, u].bitcast(F32), ALU.subtract).then_inc(wd_ready, 1)
                dve.wait_ge(sg_ready, e.n + 1 + START)
                v.tensor_tensor(hf[:, u], pu[u][:], sg[:, u], ALU.mult).then_inc(hf_ready, 1)
                dve.wait_ge(hh_ready, e.n + 1 + START)
                v.tensor_tensor(hl[:, u], hf[:, u], hh[:, u].bitcast(F32), ALU.subtract).then_inc(h_ready, 1)

            def step(e):
                body(e)
                turn_x(e.ahead(2))

            turn_x(Expert(0, 0))
            turn_x(Expert(0, 1))
            each(dve, step, 0, NE - 2)
            for c in (NE - 2, NE - 1):
                body(Expert(0, c))


def build(nc, c_in, params, wqkvo, rope_tab, ident_in, identb_in, mask_in, rw_in, bias_in,
          tri_in, ones_in, iota_in, shared_w, gate_in, up_in, down_in, out):
    h_dram = nc.dram_tensor("h_dram", (T + S, D), F32, kind="Internal").ap()
    h2_dram = nc.dram_tensor("h2_dram", (T, D), F32, kind="Internal").ap()
    xn_dram = nc.dram_tensor("xn_dram", (T, D), F32, kind="Internal").ap()
    table = nc.dram_tensor("slot_table", (NE * CAP, 2), F32, kind="Internal").ap()
    state_space(nc, c_in, params, h_dram)
    attention(nc, h_dram, wqkvo, rope_tab, ident_in, identb_in, mask_in, h2_dram)
    feed_forward(nc, h2_dram, rw_in, bias_in, ident_in, tri_in, ones_in, iota_in, shared_w, xn_dram, table, out)
    experts(nc, gate_in, up_in, down_in, ident_in, xn_dram, table, out)


def kernel(x, L0_tok_log_dt, L0_tok_B_ri, L0_tok_inv_A_real, L0_tok_A_imag, L0_attn_wq, L0_attn_wk, L0_attn_wv,
           L0_attn_wo, L0_ffn_router_w, L0_ffn_e_bias, L0_ffn_W_gate, L0_ffn_W_up, L0_ffn_W_down,
           L0_ffn_shared_gate, L0_ffn_shared_up, L0_ffn_shared_down):
    import ml_dtypes
    import concourse.bacc as bacc
    from concourse.bass_utils import run_bass_kernel_spmd

    bf = ml_dtypes.bfloat16
    x, log_dt, b_ri, a_re, a_im = (np.asarray(a) for a in (
        x, L0_tok_log_dt, L0_tok_B_ri, L0_tok_inv_A_real, L0_tok_A_imag))
    c_in = x.reshape(NB, NPAIR, 2, NSTATE, 2).transpose(2, 3, 1, 4, 0).reshape(P, NPAIR, 2, NB)
    pn = lambda a: a.reshape(NPAIR, 2, NSTATE).transpose(1, 2, 0).reshape(P, NPAIR)
    params = np.stack([pn(np.broadcast_to(log_dt[:, None], (S, NSTATE))), pn(a_re), pn(a_im),
                       pn(b_ri[..., 0]), pn(b_ri[..., 1])], 1)

    def lay(w):
        return w.reshape(w.shape[0] // P, P, w.shape[1]).transpose(1, 0, 2)

    pairs = (np.arange(NH)[:, None] * DH + np.concatenate([np.arange(0, DH, 2), np.arange(1, DH, 2)])).ravel()
    wqkvo = np.stack([lay(np.asarray(L0_attn_wq)[pairs].T), lay(np.asarray(L0_attn_wk)[pairs].T),
                      lay(np.asarray(L0_attn_wv).T), lay(np.asarray(L0_attn_wo).T)], 1)
    shared_w = np.stack([lay(np.asarray(a).T) for a in (L0_ffn_shared_gate, L0_ffn_shared_up, L0_ffn_shared_down)], 1)
    rw = lay(np.asarray(L0_ffn_router_w).T)
    ebias = np.broadcast_to(np.asarray(L0_ffn_e_bias), (P, NE))
    experts_lay = lambda w: np.asarray(w).reshape(NE, -1, P, w.shape[2]).transpose(2, 0, 1, 3)

    inv = (1.0 / 10000.0 ** (np.arange(0, DH, 2, dtype=np.float32) / np.float32(DH))).astype(np.float32)
    ang = np.outer(np.arange(S, dtype=np.float32), inv).astype(np.float32)
    cos, sin = np.cos(ang), np.sin(ang)
    rope = np.stack([np.concatenate([cos, cos], 1), np.concatenate([-sin, sin], 1)], 1)
    rope = rope.reshape(2, P, 2, DH).transpose(1, 0, 2, 3).astype(np.float32)
    rope = np.stack([rope * np.float32(SCALE), rope], 1)
    ident = np.eye(P, dtype=np.float32)
    p = np.arange(P)
    mask = np.where(p[None, :] <= p[:, None], 0.0, -1e30).astype(bf)
    mask = np.broadcast_to(mask[:, None, :], (P, GH, P))
    tri = (p[:, None] < p[None, :]).astype(bf)
    e = np.arange(NE, dtype=np.float32)
    iota = np.broadcast_to(np.stack([e - NE, e - NGRP, e * CAP]), (P, 3, NE))

    ins = {
        "c_in": c_in, "params": params, "wqkvo": wqkvo, "rope": rope, "ident": ident, "identb": ident.astype(bf),
        "mask": mask, "rw": rw, "ebias": ebias, "tri": tri, "ones": np.ones((P, P), bf),
        "iota": iota, "shared_w": shared_w, "gate": experts_lay(L0_ffn_W_gate), "up": experts_lay(L0_ffn_W_up),
        "down": experts_lay(L0_ffn_W_down),
    }
    nc = bacc.Bacc("TRN2", target_bir_lowering=False, num_devices=1)
    arrays, args = {}, []
    for name, a in ins.items():
        a = np.ascontiguousarray(a)
        arrays[f"in_{name}"] = a
        args.append(nc.dram_tensor(f"in_{name}", a.shape, mybir.dt.from_np(a.dtype), kind="ExternalInput").ap())
    out = nc.dram_tensor("out_h", (T, D), F32, kind="ExternalOutput").ap()
    build(nc, *args, out)
    r = run_bass_kernel_spmd(nc, [arrays], core_ids=[0])
    return r.results[0]["out_h"].reshape(NB, S, D)
```
